# Optimizing a Trainium2 kernel written in Bass

```python
import numpy as np
import jax
import jax.numpy as jnp

def _softmax(x, axis=-1):
    return jax.nn.softmax(x, axis=axis)

def _gelu(x):
    return jax.nn.gelu(x, approximate=True)

def _silu(x):
    return jax.nn.silu(x)

def _sigmoid(x):
    return jax.nn.sigmoid(x)

def _layernorm(x, axis=-1, eps=1e-05):
    m = jnp.mean(x, axis=axis, keepdims=True)
    v = jnp.var(x, axis=axis, keepdims=True)
    return (x - m) / jnp.sqrt(v + eps)

def _scatter_add(tgt, idx, src, axis=0):
    return tgt.at[idx].add(src)

def _segment_sum(src, seg, n):
    return jax.ops.segment_sum(src, seg, n)
kernel_name = 'mk_seq_preln_d4_jaxref_r8_2dfd1f'

def setup_inputs(seed: int=0):
    np.random.seed(seed)
    _w = jnp.asarray

    def _L0_attn_setup():
        import jax, jax.numpy as jnp
        import numpy as np
        B, L, D, H = (2, 128, 128, 8)
        HD = D // H

        def _deltanet(x, Wq, Wk, Wv, Wb, ln_w, ln_b):
            Bb, Ll, Dd = x.shape
            q = (x @ Wq).reshape(Bb, Ll, H, HD)
            k = (x @ Wk).reshape(Bb, Ll, H, HD)
            k = k / jnp.maximum(jnp.linalg.norm(k, axis=-1, keepdims=True), 1e-12)
            v = jax.nn.silu(x @ Wv).reshape(Bb, Ll, H, HD)
            beta = jax.nn.sigmoid(x @ Wb)
            qs = jnp.moveaxis(q, 1, 0)
            ks_ = jnp.moveaxis(k, 1, 0)
            vs = jnp.moveaxis(v, 1, 0)
            bs = jnp.moveaxis(beta, 1, 0)

            def step(S, inp):
                qt, kt, vt, bt = inp
                Sk = jnp.einsum('bhk,bhkv->bhv', kt, S)
                S = S + jnp.einsum('bh,bhk,bhv->bhkv', bt, kt, vt - Sk)
                ot = jnp.einsum('bhk,bhkv->bhv', qt, S)
                return (S, ot)
            S0 = jnp.zeros((Bb, H, HD, HD), x.dtype)
            _, os_ = jax.lax.scan(step, S0, (qs, ks_, vs, bs))
            o = jnp.moveaxis(os_, 0, 1).reshape(Bb, Ll, Dd)
            mu = jnp.mean(o, axis=-1, keepdims=True)
            var = jnp.var(o, axis=-1, keepdims=True)
            return (o - mu) / jnp.sqrt(var + 1e-05) * ln_w + ln_b
        key = jax.random.key(seed)
        ks = jax.random.split(key, 5)
        s = 1.0 / np.sqrt(D)
        x = jax.random.normal(ks[0], (B, L, D), jnp.float32)
        Wq = jax.random.uniform(ks[1], (D, D), jnp.float32, -s, s)
        Wk = jax.random.uniform(ks[2], (D, D), jnp.float32, -s, s)
        Wv = jax.random.uniform(ks[3], (D, D), jnp.float32, -s, s)
        Wb = jax.random.uniform(ks[4], (D, H), jnp.float32, -s, s)
        ln_w = jnp.ones((D,), jnp.float32)
        ln_b = jnp.zeros((D,), jnp.float32)
        return {'x': x, 'Wq': Wq, 'Wk': Wk, 'Wv': Wv, 'Wb': Wb, 'ln_w': ln_w, 'ln_b': ln_b}
    _L0_attn_in = _L0_attn_setup()

    def _L0_ffn_setup():
        import jax, jax.numpy as jnp
        import numpy as np
        B, S, D_MODEL, D_FF = (4, 256, 128, 512)

        def _quantum_transform(hidden, theta, w_real, w_imag):
            imag = w_imag * jnp.sin(theta + hidden * 0.1)
            quantum_phase = jnp.cos(theta) * w_real + jnp.sin(theta) * w_imag
            return hidden + quantum_phase * imag * 0.1
        key = jax.random.key(seed)
        ks = jax.random.split(key, 8)
        return {'x': jax.random.normal(ks[0], (B, S, D_MODEL), dtype=jnp.float32), 'W1': jax.random.normal(ks[1], (D_MODEL, D_FF), dtype=jnp.float32) * (1.0 / np.sqrt(D_MODEL)), 'b1': jnp.zeros((D_FF,), dtype=jnp.float32), 'quantum_phases': jax.random.normal(ks[2], (D_FF,), dtype=jnp.float32) * (2.0 * np.pi), 'quantum_weights_real': jax.random.normal(ks[3], (D_FF,), dtype=jnp.float32) * 0.1, 'quantum_weights_imag': jax.random.normal(ks[4], (D_FF,), dtype=jnp.float32) * 0.1, 'W2': jax.random.normal(ks[5], (D_FF, D_MODEL), dtype=jnp.float32) * (1.0 / np.sqrt(D_FF)), 'b2': jnp.zeros((D_MODEL,), dtype=jnp.float32)}
    _L0_ffn_in = _L0_ffn_setup()

    def _L1_attn_setup():
        import jax, jax.numpy as jnp
        import numpy as np
        LR = 0.001

        def _mlp(params, h):
            W1, b1, W2, b2 = params
            return jax.nn.silu(h @ W1 + b1) @ W2 + b2
        key = jax.random.key(seed)
        ks = jax.random.split(key, 6)
        B, S, D = (8, 256, 128)
        sc = 1.0 / np.sqrt(D)
        x = jax.random.normal(ks[0], (B, S, D), dtype=jnp.float32)
        W_Q = jax.random.normal(ks[1], (D, D), dtype=jnp.float32) * sc
        W_KV = jax.random.normal(ks[2], (D, 2 * D), dtype=jnp.float32) * sc
        W1 = jax.random.normal(ks[3], (D, D), dtype=jnp.float32) * sc
        b1 = jnp.zeros((D,), dtype=jnp.float32)
        W2 = jax.random.normal(ks[4], (D, D), dtype=jnp.float32) * sc
        b2 = jnp.zeros((D,), dtype=jnp.float32)
        return {'x': x, 'W_Q': W_Q, 'W_KV': W_KV, 'W1': W1, 'b1': b1, 'W2': W2, 'b2': b2}
    _L1_attn_in = _L1_attn_setup()

    def _L1_ffn_setup():
        import jax, jax.numpy as jnp
        import numpy as np
        THRESHOLD = 0.1
        key = jax.random.key(seed)
        k1, k2, k3 = jax.random.split(key, 3)
        B, S, D, E = (4, 512, 128, 8)
        inputs = jax.random.normal(k1, (B, S, D), dtype=jnp.float32)
        gate_w = jax.random.normal(k2, (D, E), dtype=jnp.float32) * 0.02
        gate_b = jnp.zeros((E,), dtype=jnp.float32)
        expert_w = jax.random.normal(k3, (E, D, D), dtype=jnp.float32) * 0.02
        expert_b = jnp.zeros((E, D), dtype=jnp.float32)
        return {'inputs': inputs, 'gate_w': gate_w, 'gate_b': gate_b, 'expert_w': expert_w, 'expert_b': expert_b}
    _L1_ffn_in = _L1_ffn_setup()

    def _L2_attn_setup():
        import jax, jax.numpy as jnp
        import numpy as np
        H = 8
        LN_EPS = 1e-05
        key = jax.random.key(seed)
        ks = jax.random.split(key, 4)
        B, S, D = (4, 256, 128)
        x = jax.random.normal(ks[0], (B, S, D), dtype=jnp.float32)
        sc = 1.0 / np.sqrt(D)
        Wq = jax.random.normal(ks[1], (D, D), dtype=jnp.float32) * sc
        Wk = jax.random.normal(ks[2], (D, D), dtype=jnp.float32) * sc
        Wv = jax.random.normal(ks[3], (D, D * H), dtype=jnp.float32) * sc
        return {'x': x, 'Wq': Wq, 'bq': jnp.zeros((D,), jnp.float32), 'Wk': Wk, 'bk': jnp.zeros((D,), jnp.float32), 'Wv': Wv, 'bv': jnp.zeros((D * H,), jnp.float32), 'gamma': jnp.ones((D,), jnp.float32), 'beta': jnp.zeros((D,), jnp.float32)}
    _L2_attn_in = _L2_attn_setup()

    def _L2_ffn_setup():
        import jax, jax.numpy as jnp
        import numpy as np
        DIM = 128

        def _reference_tuple_inner(x, W_r, W_k, W_v, mu_r, mu_k):
            B, T, C = x.shape
            x_prev = jnp.concatenate([jnp.zeros((B, 1, C), x.dtype), x[:, :-1, :]], axis=1)
            xr = mu_r * x + (1.0 - mu_r) * x_prev
            xk = mu_k * x + (1.0 - mu_k) * x_prev
            r = jax.nn.sigmoid(jnp.einsum('btc,dc->btd', xr, W_r))
            k = jnp.einsum('btc,dc->btd', xk, W_k)
            k_act = jnp.square(jax.nn.relu(k))
            out = r * jnp.einsum('btc,dc->btd', k_act, W_v)
            new_state = x[:, -1, :]
            return (out, new_state)
        key = jax.random.key(seed)
        ks = jax.random.split(key, 6)
        B, T, C = (8, 256, DIM)
        x = jax.random.normal(ks[0], (B, T, C), dtype=jnp.float32)
        s = 1.0 / np.sqrt(C)
        W_r = jax.random.uniform(ks[1], (C, C), jnp.float32, -s, s)
        W_k = jax.random.uniform(ks[2], (C, C), jnp.float32, -s, s)
        W_v = jax.random.uniform(ks[3], (C, C), jnp.float32, -s, s)
        mu_r = jax.random.uniform(ks[4], (C,), jnp.float32)
        mu_k = jax.random.uniform(ks[5], (C,), jnp.float32)
        return {'x': x, 'W_r': W_r, 'W_k': W_k, 'W_v': W_v, 'mu_r': mu_r, 'mu_k': mu_k}
    _L2_ffn_in = _L2_ffn_setup()

    def _L3_attn_setup():
        import jax, jax.numpy as jnp
        import numpy as np
        import math
        EMBED_DIM = 128
        NUM_HEADS = 16
        HEAD_DIM = EMBED_DIM // NUM_HEADS
        BLOCK = 64
        SCALE = 1.0 / math.sqrt(HEAD_DIM)

        def _flash_attn(Q, K, V):
            B, H, S, hd = Q.shape
            nkb = S // BLOCK
            Kb = K.reshape(B, H, nkb, BLOCK, hd).transpose(2, 0, 1, 3, 4)
            Vb = V.reshape(B, H, nkb, BLOCK, hd).transpose(2, 0, 1, 3, 4)
            out0 = jnp.zeros_like(Q)
            m0 = jnp.full((B, H, S, 1), -jnp.inf, dtype=Q.dtype)
            l0 = jnp.zeros((B, H, S, 1), dtype=Q.dtype)

            def body(carry, kv):
                out, m, l = carry
                K_blk, V_blk = kv
                scores = jnp.einsum('bhqd,bhkd->bhqk', Q, K_blk) * SCALE
                M_ij = scores.max(axis=-1, keepdims=True)
                m_new = jnp.maximum(m, M_ij)
                corr = jnp.exp(m - m_new)
                exp_scores = jnp.exp(scores - m_new)
                chunk_sum = exp_scores.sum(axis=-1, keepdims=True)
                l_new = chunk_sum * corr + chunk_sum
                out_new = out * corr + jnp.einsum('bhqk,bhkd->bhqd', exp_scores, V_blk)
                return ((out_new, m_new, l_new), None)
            (out, m, l), _ = jax.lax.scan(body, (out0, m0, l0), (Kb, Vb))
            return out / l
        key = jax.random.key(seed)
        ks = jax.random.split(key, 6)
        B, S, E = (4, 256, EMBED_DIM)
        std = 1.0 / math.sqrt(E)
        return {'x': jax.random.normal(ks[0], (B, S, E), dtype=jnp.float32), 'q_w': jax.random.normal(ks[1], (E, E), dtype=jnp.float32) * std, 'k_w': jax.random.normal(ks[2], (E, E), dtype=jnp.float32) * std, 'v_w': jax.random.normal(ks[3], (E, E), dtype=jnp.float32) * std, 'out_w': jax.random.normal(ks[4], (E, E), dtype=jnp.float32) * std, 'out_b': jnp.zeros((E,), dtype=jnp.float32)}
    _L3_attn_in = _L3_attn_setup()

    def _L3_ffn_setup():
        import jax, jax.numpy as jnp
        import numpy as np
        E = 8
        G = 4
        LG = 2
        TOPK = 2
        ROUTE_SCALE = 1.0

        def _grouped_mm(x, w, counts):
            counts = counts.astype(jnp.int32)
            if hasattr(jax.lax, 'ragged_dot'):
                return jax.lax.ragged_dot(x, w, counts)
            offs = jnp.cumsum(counts)
            eid = jnp.searchsorted(offs, jnp.arange(x.shape[0]), side='right')
            oh = jax.nn.one_hot(eid, w.shape[0], dtype=x.dtype)
            return jnp.einsum('nd,ne,edh->nh', x, oh, w)
        key = jax.random.key(seed)
        ks = jax.random.split(key, 8)
        bs, slen, dim, hid, shid = (2, 256, 128, 64, 128)
        std = 0.02
        return {'x': jax.random.normal(ks[0], (bs, slen, dim), jnp.float32), 'w_gate': jax.random.normal(ks[1], (E, dim), jnp.float32) * std, 'w1': jax.random.normal(ks[2], (E, dim, hid), jnp.float32) * std, 'w2': jax.random.normal(ks[3], (E, hid, dim), jnp.float32) * std, 'w3': jax.random.normal(ks[4], (E, dim, hid), jnp.float32) * std, 'sw1': jax.random.normal(ks[5], (shid, dim), jnp.float32) * std, 'sw2': jax.random.normal(ks[6], (dim, shid), jnp.float32) * std, 'sw3': jax.random.normal(ks[7], (shid, dim), jnp.float32) * std, 'expert_bias': jnp.zeros((E,), jnp.float32)}
    _L3_ffn_in = _L3_ffn_setup()
    _d = {'L0_attn_x': _L0_attn_in['x'], 'L0_attn_Wq': _L0_attn_in['Wq'], 'L0_attn_Wk': _L0_attn_in['Wk'], 'L0_attn_Wv': _L0_attn_in['Wv'], 'L0_attn_Wb': _L0_attn_in['Wb'], 'L0_attn_ln_w': _L0_attn_in['ln_w'], 'L0_attn_ln_b': _L0_attn_in['ln_b'], 'L0_ffn_W1': _L0_ffn_in['W1'], 'L0_ffn_b1': _L0_ffn_in['b1'], 'L0_ffn_quantum_phases': _L0_ffn_in['quantum_phases'], 'L0_ffn_quantum_weights_real': _L0_ffn_in['quantum_weights_real'], 'L0_ffn_quantum_weights_imag': _L0_ffn_in['quantum_weights_imag'], 'L0_ffn_W2': _L0_ffn_in['W2'], 'L0_ffn_b2': _L0_ffn_in['b2'], 'L1_attn_W_Q': _L1_attn_in['W_Q'], 'L1_attn_W_KV': _L1_attn_in['W_KV'], 'L1_attn_W1': _L1_attn_in['W1'], 'L1_attn_b1': _L1_attn_in['b1'], 'L1_attn_W2': _L1_attn_in['W2'], 'L1_attn_b2': _L1_attn_in['b2'], 'L1_ffn_gate_w': _L1_ffn_in['gate_w'], 'L1_ffn_gate_b': _L1_ffn_in['gate_b'], 'L1_ffn_expert_w': _L1_ffn_in['expert_w'], 'L1_ffn_expert_b': _L1_ffn_in['expert_b'], 'L2_attn_Wq': _L2_attn_in['Wq'], 'L2_attn_bq': _L2_attn_in['bq'], 'L2_attn_Wk': _L2_attn_in['Wk'], 'L2_attn_bk': _L2_attn_in['bk'], 'L2_attn_Wv': _L2_attn_in['Wv'], 'L2_attn_bv': _L2_attn_in['bv'], 'L2_attn_gamma': _L2_attn_in['gamma'], 'L2_attn_beta': _L2_attn_in['beta'], 'L2_ffn_W_r': _L2_ffn_in['W_r'], 'L2_ffn_W_k': _L2_ffn_in['W_k'], 'L2_ffn_W_v': _L2_ffn_in['W_v'], 'L2_ffn_mu_r': _L2_ffn_in['mu_r'], 'L2_ffn_mu_k': _L2_ffn_in['mu_k'], 'L3_attn_q_w': _L3_attn_in['q_w'], 'L3_attn_k_w': _L3_attn_in['k_w'], 'L3_attn_v_w': _L3_attn_in['v_w'], 'L3_attn_out_w': _L3_attn_in['out_w'], 'L3_attn_out_b': _L3_attn_in['out_b'], 'L3_ffn_w_gate': _L3_ffn_in['w_gate'], 'L3_ffn_w1': _L3_ffn_in['w1'], 'L3_ffn_w2': _L3_ffn_in['w2'], 'L3_ffn_w3': _L3_ffn_in['w3'], 'L3_ffn_sw1': _L3_ffn_in['sw1'], 'L3_ffn_sw2': _L3_ffn_in['sw2'], 'L3_ffn_sw3': _L3_ffn_in['sw3'], 'L3_ffn_expert_bias': _L3_ffn_in['expert_bias']}
    _x0 = _d['L0_attn_x']
    _d['L0_attn_x'] = jax.random.normal(jax.random.fold_in(jax.random.key(seed), 1), (4, 1024, 128), dtype=_x0.dtype)
    del _x0
    return _d

def reference(L0_attn_x, L0_attn_Wq, L0_attn_Wk, L0_attn_Wv, L0_attn_Wb, L0_attn_ln_w, L0_attn_ln_b, L0_ffn_W1, L0_ffn_b1, L0_ffn_quantum_phases, L0_ffn_quantum_weights_real, L0_ffn_quantum_weights_imag, L0_ffn_W2, L0_ffn_b2, L1_attn_W_Q, L1_attn_W_KV, L1_attn_W1, L1_attn_b1, L1_attn_W2, L1_attn_b2, L1_ffn_gate_w, L1_ffn_gate_b, L1_ffn_expert_w, L1_ffn_expert_b, L2_attn_Wq, L2_attn_bq, L2_attn_Wk, L2_attn_bk, L2_attn_Wv, L2_attn_bv, L2_attn_gamma, L2_attn_beta, L2_ffn_W_r, L2_ffn_W_k, L2_ffn_W_v, L2_ffn_mu_r, L2_ffn_mu_k, L3_attn_q_w, L3_attn_k_w, L3_attn_v_w, L3_attn_out_w, L3_attn_out_b, L3_ffn_w_gate, L3_ffn_w1, L3_ffn_w2, L3_ffn_w3, L3_ffn_sw1, L3_ffn_sw2, L3_ffn_sw3, L3_ffn_expert_bias):

    def _L0_attn_ref(x, Wq, Wk, Wv, Wb, ln_w, ln_b):
        import jax, jax.numpy as jnp
        import numpy as np
        B, L, D, H = (2, 128, 128, 8)
        HD = D // H

        def _deltanet(x, Wq, Wk, Wv, Wb, ln_w, ln_b):
            Bb, Ll, Dd = x.shape
            q = (x @ Wq).reshape(Bb, Ll, H, HD)
            k = (x @ Wk).reshape(Bb, Ll, H, HD)
            k = k / jnp.maximum(jnp.linalg.norm(k, axis=-1, keepdims=True), 1e-12)
            v = jax.nn.silu(x @ Wv).reshape(Bb, Ll, H, HD)
            beta = jax.nn.sigmoid(x @ Wb)
            qs = jnp.moveaxis(q, 1, 0)
            ks_ = jnp.moveaxis(k, 1, 0)
            vs = jnp.moveaxis(v, 1, 0)
            bs = jnp.moveaxis(beta, 1, 0)

            def step(S, inp):
                qt, kt, vt, bt = inp
                Sk = jnp.einsum('bhk,bhkv->bhv', kt, S)
                S = S + jnp.einsum('bh,bhk,bhv->bhkv', bt, kt, vt - Sk)
                ot = jnp.einsum('bhk,bhkv->bhv', qt, S)
                return (S, ot)
            S0 = jnp.zeros((Bb, H, HD, HD), x.dtype)
            _, os_ = jax.lax.scan(step, S0, (qs, ks_, vs, bs))
            o = jnp.moveaxis(os_, 0, 1).reshape(Bb, Ll, Dd)
            mu = jnp.mean(o, axis=-1, keepdims=True)
            var = jnp.var(o, axis=-1, keepdims=True)
            return (o - mu) / jnp.sqrt(var + 1e-05) * ln_w + ln_b
        return _deltanet(x, Wq, Wk, Wv, Wb, ln_w, ln_b)

    def _L0_ffn_ref(x, W1, b1, quantum_phases, quantum_weights_real, quantum_weights_imag, W2, b2):
        import jax, jax.numpy as jnp
        import numpy as np
        B, S, D_MODEL, D_FF = (4, 256, 128, 512)

        def _quantum_transform(hidden, theta, w_real, w_imag):
            imag = w_imag * jnp.sin(theta + hidden * 0.1)
            quantum_phase = jnp.cos(theta) * w_real + jnp.sin(theta) * w_imag
            return hidden + quantum_phase * imag * 0.1
        hidden = jnp.einsum('bsd,df->bsf', x, W1) + b1
        q = _quantum_transform(hidden, quantum_phases, quantum_weights_real, quantum_weights_imag)
        act = jax.nn.relu(q)
        return jnp.einsum('bsf,fd->bsd', act, W2) + b2

    def _L1_attn_ref(x, W_Q, W_KV, W1, b1, W2, b2):
        import jax, jax.numpy as jnp
        import numpy as np
        LR = 0.001

        def _mlp(params, h):
            W1, b1, W2, b2 = params
            return jax.nn.silu(h @ W1 + b1) @ W2 + b2
        kv = x @ W_KV
        k, v = jnp.split(kv, 2, axis=-1)
        k = jnp.swapaxes(k, 0, 1)
        v = jnp.swapaxes(v, 0, 1)

        def loss_fn(params, k_t, v_t):
            return jnp.mean((_mlp(params, k_t) - v_t) ** 2)

        def step(params, kvt):
            k_t, v_t = kvt
            g = jax.grad(loss_fn)(params, k_t, v_t)
            new_params = tuple((p - LR * gp for p, gp in zip(params, g)))
            return (new_params, None)
        params, _ = jax.lax.scan(step, (W1, b1, W2, b2), (k, v))
        q = x @ W_Q
        return _mlp(params, q)

    def _L1_ffn_ref(inputs, gate_w, gate_b, expert_w, expert_b):
        import jax, jax.numpy as jnp
        import numpy as np
        THRESHOLD = 0.1
        d = inputs.shape[-1]
        x = inputs.reshape(-1, d)
        gate_logits = jax.nn.softmax(x @ gate_w + gate_b, axis=-1)
        selected = (gate_logits >= THRESHOLD).astype(x.dtype)
        weights = gate_logits * selected
        wsum = jnp.sum(weights, axis=-1, keepdims=True)
        weights = weights / jnp.where(wsum == 0, jnp.ones_like(wsum), wsum)
        E = expert_w.shape[0]
        out = jnp.zeros((x.shape[0], expert_w.shape[-1]), dtype=x.dtype)
        for e in range(E):
            out = out + weights[:, e:e + 1] * (x @ expert_w[e] + expert_b[e])
        return out.reshape(*inputs.shape[:-1], out.shape[-1])

    def _L2_attn_ref(x, Wq, bq, Wk, bk, Wv, bv, gamma, beta):
        import jax, jax.numpy as jnp
        import numpy as np
        H = 8
        LN_EPS = 1e-05
        B, S, D = x.shape
        dk = D // H
        mu = jnp.mean(x, axis=-1, keepdims=True)
        var = jnp.mean(jnp.square(x - mu), axis=-1, keepdims=True)
        xn = (x - mu) * jax.lax.rsqrt(var + LN_EPS) * gamma + beta
        q = (xn @ Wq + bq).reshape(B, S, H, dk).transpose(0, 2, 1, 3)
        k = (xn @ Wk + bk).reshape(B, S, H, dk).transpose(0, 2, 1, 3)
        v = (xn @ Wv + bv).reshape(B, S, H, D).transpose(0, 2, 1, 3)
        scores = jnp.einsum('bhsd,bhtd->bhst', q, k) / jnp.sqrt(jnp.asarray(dk, x.dtype))
        p = jax.nn.softmax(scores, axis=-1)
        att = jnp.einsum('bhst,bhtd->bhsd', p, v)
        out = att.reshape(S, B, D, H).sum(axis=-1).reshape(B, S, D)
        return out

    def _L2_ffn_ref(x, W_r, W_k, W_v, mu_r, mu_k):
        import jax, jax.numpy as jnp
        import numpy as np
        DIM = 128

        def _reference_tuple_inner(x, W_r, W_k, W_v, mu_r, mu_k):
            B, T, C = x.shape
            x_prev = jnp.concatenate([jnp.zeros((B, 1, C), x.dtype), x[:, :-1, :]], axis=1)
            xr = mu_r * x + (1.0 - mu_r) * x_prev
            xk = mu_k * x + (1.0 - mu_k) * x_prev
            r = jax.nn.sigmoid(jnp.einsum('btc,dc->btd', xr, W_r))
            k = jnp.einsum('btc,dc->btd', xk, W_k)
            k_act = jnp.square(jax.nn.relu(k))
            out = r * jnp.einsum('btc,dc->btd', k_act, W_v)
            new_state = x[:, -1, :]
            return (out, new_state)
        return _reference_tuple_inner(x, W_r, W_k, W_v, mu_r, mu_k)[0]

    def _L3_attn_ref(x, q_w, k_w, v_w, out_w, out_b):
        import jax, jax.numpy as jnp
        import numpy as np
        import math
        EMBED_DIM = 128
        NUM_HEADS = 16
        HEAD_DIM = EMBED_DIM // NUM_HEADS
        BLOCK = 64
        SCALE = 1.0 / math.sqrt(HEAD_DIM)

        def _flash_attn(Q, K, V):
            B, H, S, hd = Q.shape
            nkb = S // BLOCK
            Kb = K.reshape(B, H, nkb, BLOCK, hd).transpose(2, 0, 1, 3, 4)
            Vb = V.reshape(B, H, nkb, BLOCK, hd).transpose(2, 0, 1, 3, 4)
            out0 = jnp.zeros_like(Q)
            m0 = jnp.full((B, H, S, 1), -jnp.inf, dtype=Q.dtype)
            l0 = jnp.zeros((B, H, S, 1), dtype=Q.dtype)

            def body(carry, kv):
                out, m, l = carry
                K_blk, V_blk = kv
                scores = jnp.einsum('bhqd,bhkd->bhqk', Q, K_blk) * SCALE
                M_ij = scores.max(axis=-1, keepdims=True)
                m_new = jnp.maximum(m, M_ij)
                corr = jnp.exp(m - m_new)
                exp_scores = jnp.exp(scores - m_new)
                chunk_sum = exp_scores.sum(axis=-1, keepdims=True)
                l_new = chunk_sum * corr + chunk_sum
                out_new = out * corr + jnp.einsum('bhqk,bhkd->bhqd', exp_scores, V_blk)
                return ((out_new, m_new, l_new), None)
            (out, m, l), _ = jax.lax.scan(body, (out0, m0, l0), (Kb, Vb))
            return out / l
        B, S, E = x.shape
        H, hd = (NUM_HEADS, HEAD_DIM)

        def split_heads(t):
            return t.reshape(B, S, H, hd).transpose(0, 2, 1, 3)
        Q = split_heads(x @ q_w.T)
        K = split_heads(x @ k_w.T)
        V = split_heads(x @ v_w.T)
        out = _flash_attn(Q, K, V)
        out = out.transpose(0, 2, 1, 3).reshape(B, S, E)
        return out @ out_w.T + out_b

    def _L3_ffn_ref(x, w_gate, w1, w2, w3, sw1, sw2, sw3, expert_bias):
        import jax, jax.numpy as jnp
        import numpy as np
        E = 8
        G = 4
        LG = 2
        TOPK = 2
        ROUTE_SCALE = 1.0

        def _grouped_mm(x, w, counts):
            counts = counts.astype(jnp.int32)
            if hasattr(jax.lax, 'ragged_dot'):
                return jax.lax.ragged_dot(x, w, counts)
            offs = jnp.cumsum(counts)
            eid = jnp.searchsorted(offs, jnp.arange(x.shape[0]), side='right')
            oh = jax.nn.one_hot(eid, w.shape[0], dtype=x.dtype)
            return jnp.einsum('nd,ne,edh->nh', x, oh, w)
        bs, slen, dim = x.shape
        xf = x.reshape(-1, dim)
        N = xf.shape[0]
        logits = xf @ w_gate.T
        scores = jax.nn.softmax(logits.astype(jnp.float32), axis=-1)
        original = scores
        s = (scores + expert_bias).reshape(N, G, E // G)
        group_scores = jax.lax.top_k(s, 2)[0].sum(-1)
        top_groups = jax.lax.top_k(group_scores, LG)[1]
        keep = jnp.zeros((N, G), bool).at[jnp.arange(N)[:, None], top_groups].set(True)
        masked = jnp.where(keep[:, :, None], s, -jnp.inf).reshape(N, E)
        topk_idx = jax.lax.top_k(masked, TOPK)[1]
        weights = (jnp.take_along_axis(original, topk_idx, axis=1) * ROUTE_SCALE).astype(x.dtype)
        counts = jnp.bincount(topk_idx.reshape(-1), length=E)
        flat_idx = topk_idx.reshape(-1)
        routed_in = xf[flat_idx]
        routed_in = (routed_in.astype(jnp.float32) * weights.reshape(-1, 1)).astype(x.dtype)
        h = jax.nn.silu(_grouped_mm(routed_in, w1, counts)) * _grouped_mm(routed_in, w3, counts)
        routed_out = _grouped_mm(h, w2, counts)
        shared = jax.nn.silu(xf @ sw1.T) * (xf @ sw3.T) @ sw2.T
        out = shared.at[flat_idx].add(routed_out)
        return out.reshape(bs, slen, dim)
    x = L0_attn_x
    x = x + _L0_attn_ref(_layernorm(x, axis=-1), L0_attn_Wq, L0_attn_Wk, L0_attn_Wv, L0_attn_Wb, L0_attn_ln_w, L0_attn_ln_b)
    x = x + _L0_ffn_ref(_layernorm(x, axis=-1), L0_ffn_W1, L0_ffn_b1, L0_ffn_quantum_phases, L0_ffn_quantum_weights_real, L0_ffn_quantum_weights_imag, L0_ffn_W2, L0_ffn_b2)
    x = x + _L1_attn_ref(_layernorm(x, axis=-1), L1_attn_W_Q, L1_attn_W_KV, L1_attn_W1, L1_attn_b1, L1_attn_W2, L1_attn_b2)
    x = x + _L1_ffn_ref(_layernorm(x, axis=-1), L1_ffn_gate_w, L1_ffn_gate_b, L1_ffn_expert_w, L1_ffn_expert_b)
    x = x + _L2_attn_ref(_layernorm(x, axis=-1), L2_attn_Wq, L2_attn_bq, L2_attn_Wk, L2_attn_bk, L2_attn_Wv, L2_attn_bv, L2_attn_gamma, L2_attn_beta)
    x = x + _L2_ffn_ref(_layernorm(x, axis=-1), L2_ffn_W_r, L2_ffn_W_k, L2_ffn_W_v, L2_ffn_mu_r, L2_ffn_mu_k)
    x = x + _L3_attn_ref(_layernorm(x, axis=-1), L3_attn_q_w, L3_attn_k_w, L3_attn_v_w, L3_attn_out_w, L3_attn_out_b)
    x = x + _L3_ffn_ref(_layernorm(x, axis=-1), L3_ffn_w_gate, L3_ffn_w1, L3_ffn_w2, L3_ffn_w3, L3_ffn_sw1, L3_ffn_sw2, L3_ffn_sw3, L3_ffn_expert_bias)
    return x

_drawn_inputs = setup_inputs


def setup_inputs(seed=0):
    import zlib

    import numpy as np

    out = dict(_drawn_inputs(seed))
    spreads = {'L0_attn_ln_w': (1.0, 0.2),
     'L0_attn_ln_b': (0.0, 0.1),
     'L0_ffn_b1': (0.0, 0.1),
     'L0_ffn_b2': (0.0, 0.1),
     'L1_attn_b1': (0.0, 0.1),
     'L1_attn_b2': (0.0, 0.1),
     'L1_ffn_gate_b': (0.0, 0.487),
     'L1_ffn_expert_b': (0.0, 0.1),
     'L2_attn_bq': (0.0, 0.282),
     'L2_attn_bk': (0.0, 0.8),
     'L2_attn_bv': (0.0, 0.1),
     'L2_attn_gamma': (1.0, 0.2),
     'L2_attn_beta': (0.0, 0.1),
     'L3_attn_out_b': (0.0, 0.276),
     'L3_ffn_expert_bias': (0.0, 0.8)}
    factors = {'L0_ffn_quantum_phases': 8.0,
     'L0_ffn_quantum_weights_real': 8.0,
     'L0_ffn_quantum_weights_imag': 8.0,
     'L2_ffn_W_r': 4.704,
     'L2_ffn_mu_r': 8.0,
     'L3_ffn_w_gate': 8.0,
     'L3_ffn_w1': 8.0,
     'L3_ffn_w2': 8.0,
     'L3_ffn_w3': 8.0,
     'L3_ffn_sw1': 8.0,
     'L3_ffn_sw2': 8.0,
     'L3_ffn_sw3': 8.0}
    for name, (base, spread) in spreads.items():
        noise = np.random.default_rng([zlib.crc32(name.encode()), seed]).standard_normal(out[name].shape)
        drawn = base * np.exp(spread * noise) if base else spread * noise
        out[name] = jnp.asarray(drawn.astype(out[name].dtype))
    for name, factor in factors.items():
        out[name] = (out[name] * factor).astype(out[name].dtype)
    return out
```

```python
from contextlib import ExitStack
from math import log, pi

import numpy as np
import concourse.bass as bass
from concourse import mybir

LAYERS = (0, 1, 2, 3, 4, 5, 6, 7)

F32 = mybir.dt.float32
BF16 = mybir.dt.bfloat16
F16 = mybir.dt.float16
I32 = mybir.dt.int32
ALU = mybir.AluOpType
ACT = mybir.ActivationFunctionType
AXX = mybir.AxisListType.X

P = 128
B, S, D = 4, 1024, 128
NT = B * S // P
GROUP = 4
GT = GROUP * P
NG = NT // GROUP
EPS = 1e-5
ROUND = 1.5 * 2.0 ** 23


class Chain:

    def __init__(self, eng, sem):
        self.eng, self.sem, self.n = eng, sem, 0

    def do(self, ins):
        ins.then_inc(self.sem, 1)
        self.n += 1

    def sync(self):
        self.eng.wait_ge(self.sem, self.n)

    def step(self, ins):
        self.do(ins)
        self.sync()

    def restart(self):
        if self.n:
            self.sync()
            self.eng.sem_clear(self.sem)
        self.n = 0


class Core:

    def __init__(self, nc, ctx, dram):
        self.nc, self.ctx, self.dram = nc, ctx, dram
        self.layer_sems = None
        self.sem_ctx = None
        self.programs = {e: [] for e in ("sync", "tensor", "scalar", "vector", "gpsimd")}
        self.X = self.sb("X", [P, NT, D])
        self.XT = self.sb("XT", [P, B * S])
        self.ident = self.sb("ident", [P, P])
        self.ident16 = self.sb("ident16", [P, P], BF16)
        self.mhalf = self.sb("mhalf", [P, P])
        self.ones_row = self.sb("ones_row", [1, P])
        self.psum = ctx.enter_context(nc.psum_tensor("psum", [P, 8, 512], F32))
        self.consts_in = self.sem("consts_in")
        self.ident16_in = self.sem("ident16_in")
        self.held = self.sem("held")
        self.layer_done = self.sem("layer_done")
        self.layers = 0
        self.free = []

    def sb(self, name, shape, dt=F32, ctx=None):
        return (ctx or self.ctx).enter_context(self.nc.sbuf_tensor(name, shape, dt))

    def sem(self, name):
        if self.layer_sems is None:
            return self.ctx.enter_context(self.nc.semaphore(name))
        self.layer_sems.append(self.sem_ctx.enter_context(self.nc.semaphore(name)))
        return self.layer_sems[-1]

    def free_sem(self, name):
        self.free.append(self.sem(name))
        return self.free[-1]

    def add(self, **programs):
        for e, f in programs.items():
            self.programs[e].append(f)

    def plain(self, eng):
        eng.sem_inc(self.held, 1)

    def start(self, eng, layer):
        if layer:
            eng.wait_ge(self.layer_done, layer)
        else:
            eng.wait_ge(self.consts_in, 64)


def layer_norm(k, tag, twice=False, affine=None, affine_in=None):
    nc = k.nc
    tag = f"{tag}_norm"
    ready = [k.sem(f"{tag}_ready{g}") for g in range(2)]
    turned = [k.free_sem(f"{tag}_turned{g}") for g in range(2)]
    written = [k.free_sem(f"{tag}_xt{g}") for g in range(2)]
    var_in, root_out = k.sem(f"{tag}_var"), k.sem(f"{tag}_root")
    own = k.sem(f"{tag}_ln_own")
    ctx = k.layer_ctx
    xn = [k.sb(f"{tag}_xn{g}", [P, GROUP, D], ctx=ctx) for g in range(2)]
    stats = k.sb(f"{tag}_st", [P, NT, 6], ctx=ctx)
    mv = k.sb(f"{tag}_mv", [P, NT, 2], ctx=ctx)
    root = k.sb(f"{tag}_root_buf", [P, NT], ctx=ctx)
    rstd = k.sb(f"{tag}_rs", [P, NT], ctx=ctx)
    tmp = k.sb(f"{tag}_ln_tmp", [P, 2, NT], ctx=ctx)
    layer = k.layers

    def vector(v):
        k.start(v, layer)
        c = Chain(v, own)
        with v.Fori(0, NT // 8) as i:
            for n in range(8):
                c.do(nc.vector.bn_stats(stats[:, bass.ds(i * 8 + n, 1), :], k.X[:, bass.ds(i * 8 + n, 1), :]))
            c.restart()
        for n in range(NT):
            c.do(nc.vector.bn_aggr(mv[:, n, :], stats[:, n, :]))
        c.sync()
        nc.vector.tensor_scalar(tmp[:, 0, :], mv[:, :, 1], EPS, None, ALU.add).then_inc(var_in, 1)
        v.wait_ge(root_out, 1)
        if twice:
            c.step(nc.vector.tensor_tensor(tmp[:, 0, :], rstd[:, :], rstd[:, :], ALU.mult))
            c.step(nc.vector.tensor_tensor(tmp[:, 1, :], tmp[:, 0, :], mv[:, :, 1], ALU.mult))
            nc.vector.tensor_scalar(tmp[:, 0, :], tmp[:, 1, :], EPS, None, ALU.add).then_inc(var_in, 1)
            v.wait_ge(root_out, 2)
            c.step(nc.vector.tensor_tensor(rstd[:, :], rstd[:, :], root[:, :], ALU.mult))
        c.restart()
        with v.Fori(0, NG // 2) as i:
            for g in range(2):
                v.wait_ge(turned[g], i + 1)
                for n in range(GROUP):
                    t = i * 2 * GROUP + g * GROUP + n
                    last = nc.vector.tensor_scalar(xn[g][:, n, :], k.X[:, bass.ds(t, 1), :], mv[:, bass.ds(t, 1), 0],
                                                   rstd[:, bass.ds(t, 1)], ALU.subtract, ALU.mult)
                    if n < GROUP - 1:
                        c.do(last)
                c.sync()
                last.then_inc(ready[g], 1)
            c.restart()

    def tensor(t):
        k.start(t, layer)
        with t.Fori(0, NG // 2) as i:
            for g in range(2):
                t.wait_ge(ready[g], i + 1)
                t.wait_ge(written[g], i + 1)
                for n in range(GROUP):
                    last = nc.tensor.transpose(k.psum[:, g, n * P:(n + 1) * P], xn[g][:, n, :], k.ident[:, :])
                last.then_inc(turned[g], 1)

    def scalar(a):
        k.start(a, layer)
        if affine_in is not None:
            a.wait_ge(*affine_in)
        with a.Fori(0, NG // 2) as i:
            for g in range(2):
                a.wait_ge(turned[g], i + 2)
                dst = k.XT[:, bass.ds(i * 2 * GT + g * GT, GT)]
                if affine is None:
                    nc.scalar.copy(dst, k.psum[:, g, :]).then_inc(written[g], 1)
                else:
                    nc.scalar.activation(dst, k.psum[:, g, :], ACT.Identity, scale=affine[0],
                                         bias=affine[1]).then_inc(written[g], 1)

    def gpsimd(p):
        k.start(p, layer)
        for q in range(2 if twice else 1):
            p.wait_ge(var_in, q + 1)
            nc.gpsimd.tensor_tensor((root if q else rstd)[:, :], tmp[:, 0, :], k.mhalf[:, 0:NT], ALU.pow).then_inc(root_out, 1)

    k.add(vector=vector, tensor=tensor, scalar=scalar, gpsimd=gpsimd)
    return written


def sine_ffn(k):
    nc, d, ctx = k.nc, k.dram, k.layer_ctx
    FF = d["L0_ffn_W1"].shape[1]
    NF = FF // P
    w1 = k.sb("sf_w1", [P, FF], ctx=ctx)
    w2 = k.sb("sf_w2", [P, NF, D], ctx=ctx)
    cols = k.sb("sf_cols", [P, 4, NF], ctx=ctx)
    b2 = k.sb("sf_b2", [1, GT], ctx=ctx)
    tmp = k.sb("sf_tmp", [P, 4, NF], ctx=ctx)
    sc = k.sb("sf_sincos", [P, 2, NF], ctx=ctx)
    turn0 = k.sb("sf_turn0", [P, NF], ctx=ctx)
    coef = k.sb("sf_coef", [P, NF], ctx=ctx)
    y = [k.sb(f"sf_y{j}", [P, GT], ctx=ctx) for j in range(2)]
    r = [k.sb(f"sf_r{j}", [P, GT], ctx=ctx) for j in range(2)]
    sn = [k.sb(f"sf_sn{j}", [P, GT], ctx=ctx) for j in range(2)]
    q = [k.sb(f"sf_q{j}", [P, GT], ctx=ctx) for j in range(2)]
    act = [k.sb(f"sf_act{j}", [P, NF, GT], ctx=ctx) for j in range(2)]
    w_in, own, pre, presin = (k.sem(f"sf_{n}") for n in ("w_in", "own", "pre", "presin"))
    hid = [k.sem(f"sf_hid{j}") for j in range(2)]
    frac = [k.sem(f"sf_frac{j}") for j in range(2)]
    sine = [k.free_sem(f"sf_sine{j}") for j in range(2)]
    gated = [k.free_sem(f"sf_gated{j}") for j in range(2)]
    relu = [k.sem(f"sf_relu{g}") for g in range(2)]
    outp = [k.free_sem(f"sf_out{g}") for g in range(2)]
    added = [k.free_sem(f"sf_added{g}") for g in range(2)]
    layer = k.layers
    xt = layer_norm(k, "sf")

    def sync(s):
        if layer:
            s.wait_ge(k.layer_done, layer)
        s.dma_start(w1[:, :], d["L0_ffn_W1"]).then_inc(w_in, 16)
        s.dma_start(w2[:, :, :], d["L0_ffn_W2"].rearrange("(f p) d -> p f d", p=P)).then_inc(w_in, 16)
        s.dma_start(cols[:, :, :], d["sf_cols"]).then_inc(w_in, 16)
        s.dma_start(b2[:, :], d["sf_b2"]).then_inc(w_in, 16)

    C1 = 6.28125
    C2 = 2 * pi - C1

    def vector(v):
        c = Chain(v, own)
        v.wait_ge(w_in, 64)
        th = cols[:, 1, :]
        c.step(nc.vector.tensor_scalar(tmp[:, 0, :], th, 1 / (2 * pi), ROUND, ALU.mult, ALU.add))
        c.step(nc.vector.tensor_scalar(tmp[:, 1, :], tmp[:, 0, :], ROUND, None, ALU.subtract))
        c.step(nc.vector.scalar_tensor_tensor(tmp[:, 2, :], tmp[:, 1, :], -C1, th, ALU.mult, ALU.add))
        c.step(nc.vector.scalar_tensor_tensor(tmp[:, 3, :], tmp[:, 1, :], -C2, tmp[:, 2, :], ALU.mult, ALU.add))
        c.step(nc.vector.tensor_scalar(turn0[:, :], tmp[:, 3, :], 1 / (2 * pi), None, ALU.mult))
        c.step(nc.vector.tensor_scalar(tmp[:, 0, :], turn0[:, :], ROUND, ROUND, ALU.add, ALU.subtract))
        c.step(nc.vector.tensor_tensor(tmp[:, 2, :], turn0[:, :], tmp[:, 0, :], ALU.subtract))
        c.step(nc.vector.tensor_scalar(tmp[:, 1, :], turn0[:, :], 0.25, None, ALU.add))
        c.step(nc.vector.tensor_scalar(tmp[:, 0, :], tmp[:, 1, :], ROUND, ROUND, ALU.add, ALU.subtract))
        c.step(nc.vector.tensor_tensor(tmp[:, 3, :], tmp[:, 1, :], tmp[:, 0, :], ALU.subtract))
        nc.vector.tensor_scalar(tmp[:, 0, :], cols[:, 3, :], 0.1, None, ALU.mult).then_inc(pre, 1)
        v.wait_ge(pre, 1)
        v.wait_ge(presin, 1)
        c.step(nc.vector.tensor_tensor(tmp[:, 1, :], sc[:, 0, :], cols[:, 3, :], ALU.mult))
        c.step(nc.vector.tensor_tensor(tmp[:, 2, :], sc[:, 1, :], cols[:, 2, :], ALU.mult))
        c.step(nc.vector.tensor_tensor(tmp[:, 3, :], tmp[:, 1, :], tmp[:, 2, :], ALU.add))
        c.step(nc.vector.tensor_tensor(coef[:, :], tmp[:, 3, :], tmp[:, 0, :], ALU.mult))
        c.step(nc.vector.scalar_tensor_tensor(tmp[:, 1, :], cols[:, 0, :], 0.1 / (2 * pi), turn0[:, :], ALU.mult, ALU.add))
        c.restart()
        with v.Fori(0, NG // 2) as i:
            for g in range(2):
                for f in range(NF):
                    j, m = f % 2, g * (NF // 2) + f // 2
                    use = i * NF + m
                    v.wait_ge(hid[j], use + 1)
                    v.wait_ge(sine[j], use + 1)
                    h = k.psum[:, 2 + j, :]
                    c.step(nc.vector.tensor_scalar(y[j][:, :], h, 0.1 / (2 * pi), tmp[:, 1, f:f + 1], ALU.mult, ALU.add))
                    c.step(nc.vector.tensor_scalar(r[j][:, :], y[j][:, :], ROUND, ROUND, ALU.add, ALU.subtract))
                    nc.vector.tensor_tensor(r[j][:, :], y[j][:, :], r[j][:, :], ALU.subtract).then_inc(frac[j], 1)
                    v.wait_ge(sine[j], use + 2)
                    nc.vector.scalar_tensor_tensor(q[j][:, :], sn[j][:, :], coef[:, f:f + 1], h,
                                                   ALU.mult, ALU.add).then_inc(gated[j], 1)
                v.wait_ge(outp[g], i + 2)
                xs = k.X[:, bass.ds(i * 2 * GROUP + g * GROUP, GROUP), :]
                nc.vector.tensor_tensor(xs, xs, k.psum[:, 4 + g, :].rearrange("p (n d) -> p n d", d=D),
                                        ALU.add).then_inc(added[g], 1)
            c.restart()
        v.wait_ge(added[0], NG // 2 + 1)
        v.wait_ge(added[1], NG // 2 + 1)
        nc.vector.tensor_copy(tmp[:, 0, 0:1], tmp[:, 0, 0:1]).then_inc(k.layer_done, 1)

    def scalar(a):
        a.wait_ge(pre, 1)
        nc.scalar.activation(sc[:, :, :], tmp[:, 2:4, :], ACT.Sin, scale=6.283185).then_inc(presin, 1)
        with a.Fori(0, NG // 2) as i:
            for g in range(2):
                for f in range(NF):
                    j, m = f % 2, g * (NF // 2) + f // 2
                    use = i * NF + m
                    a.wait_ge(frac[j], use + 1)
                    nc.scalar.activation(sn[j][:, :], r[j][:, :], ACT.Sin, scale=6.283185).then_inc(sine[j], 1)
                    if f == 0:
                        a.wait_ge(outp[g], i + 1)
                    a.wait_ge(gated[j], use + 2)
                    nc.scalar.activation(act[g][:, f, :], q[j][:, :], ACT.Relu,
                                         bias=cols[:, 0, f:f + 1]).then_inc(relu[g], 1)

    def tensor(t):
        t.wait_ge(w_in, 64)
        for g in range(2):
            t.wait_ge(xt[g], NG // 2 + 1)
        with t.Fori(0, NG // 2) as i:
            for g in range(2):
                for f in range(NF):
                    j, m = f % 2, g * (NF // 2) + f // 2
                    use = i * NF + m
                    t.wait_ge(gated[j], use + 1)
                    nc.tensor.matmul(k.psum[:, 2 + j, :], w1[:, f * P:(f + 1) * P],
                                     k.XT[:, bass.ds(i * 2 * GT + g * GT, GT)], start=True, stop=True).then_inc(hid[j], 1)
                t.wait_ge(added[g], i + 1)
                t.wait_ge(relu[g], (i + 1) * NF)
                nc.tensor.matmul(k.psum[:, 4 + g, :], k.ones_row[:, :], b2[:, :], start=True, stop=True)
                for n in range(GROUP):
                    for f in range(NF):
                        last = nc.tensor.matmul(k.psum[:, 4 + g, n * D:(n + 1) * D], act[g][:, f, n * P:(n + 1) * P],
                                                w2[:, f, :], start=False, stop=True, skip_group_check=True)
                last.then_inc(outp[g], 1)

    k.add(sync=sync, vector=vector, scalar=scalar, tensor=tensor)


def delta_net(k):
    nc, d, ctx = k.nc, k.dram, k.layer_ctx
    H = d["L0_attn_Wb"].shape[1]
    HD = D // H
    R = P // (B * H)
    V = HD // R
    BH = P // B
    C = P
    NC = S // C
    wk = k.sb("dn_wk", [P, HD, BH], ctx=ctx)
    wq = k.sb("dn_wq", [P, HD, BH], ctx=ctx)
    wv = k.sb("dn_wv", [P, V, BH], ctx=ctx)
    wb = k.sb("dn_wb", [P, BH], ctx=ctx)
    lnw = k.sb("dn_lnw", [P, D], ctx=ctx)
    lnb = k.sb("dn_lnb", [P, D], ctx=ctx)
    stage = k.sb("dn_stage", [P, B, C], ctx=ctx)
    kraw = k.sb("dn_kraw", [P, C, HD], ctx=ctx)
    sq = k.sb("dn_sq", [P, C, HD], ctx=ctx)
    ss = k.sb("dn_ss", [P, C], ctx=ctx)
    norm = k.sb("dn_norm", [P, C], ctx=ctx)
    beta = k.sb("dn_beta", [P, C], ctx=ctx)
    vraw = k.sb("dn_vraw", [P, C, V], ctx=ctx)
    vsig = k.sb("dn_vsig", [P, C, V], ctx=ctx)
    kn = [k.sb(f"dn_kn{g}", [P, C, HD], ctx=ctx) for g in range(2)]
    kb = [k.sb(f"dn_kb{g}", [P, C, HD], ctx=ctx) for g in range(2)]
    q = [k.sb(f"dn_q{g}", [P, C, HD], ctx=ctx) for g in range(2)]
    vb = [k.sb(f"dn_vb{g}", [P, C, V], ctx=ctx) for g in range(2)]
    hist = [k.sb(f"dn_hist{g}", [P, C + 1, V * HD], ctx=ctx) for g in range(2)]
    prod = k.sb("dn_prod", [P, V, HD], ctx=ctx)
    ks = k.sb("dn_ks", [P, V], ctx=ctx)
    u = k.sb("dn_u", [P, V], ctx=ctx)
    outer = k.sb("dn_outer", [P, V, HD], ctx=ctx)
    OQ = 4
    qs = k.sb("dn_qs", [P, C // OQ, V, HD], ctx=ctx)
    o = k.sb("dn_o", [P, C, V], ctx=ctx)
    om = k.XT[:, :].rearrange("p (b c d) -> p b c d", b=B, c=NC)
    PIECES = 2 * HD // V + 2
    (w_in, staged, raw_in, prepared, states, o_ready, post, root_in, root_out, own, pool_own,
     hist_ready) = (
        k.sem(f"dn_{n}") for n in ("w_in", "staged", "raw_in", "prepared", "states", "o_ready",
                                   "post", "root_in", "root_out", "own", "pool_own", "hist_ready"))
    projected = [k.sem(f"dn_projected{g}") for g in range(2)]
    emptied = [k.free_sem(f"dn_emptied{g}") for g in range(2)]
    stage_free, raw_free = k.free_sem("dn_stage_free"), k.free_sem("dn_raw_free")
    chunk_free = [k.free_sem(f"dn_chunk_free{g}") for g in range(2)]
    keys_free = [k.free_sem(f"dn_keys_free{g}") for g in range(2)]
    o_rows = k.free_sem("dn_o_rows")
    rows_free = k.free_sem("dn_rows_free")
    layer = k.layers
    xt = layer_norm(k, "dn")
    xt_v = k.XT[:, :].rearrange("p (b c t) -> p b c t", b=B, c=NC)

    def one_ahead(eng, ahead, behind):
        ahead(0, 0)
        with eng.Fori(0, NC // 2 - 1) as i:
            ahead(i, 1)
            behind(i, 0)
            ahead(i + 1, 0)
            behind(i, 1)
        last = NC // 2 - 1
        ahead(last, 1)
        behind(last, 0)
        behind(last, 1)

    def sync(s):
        if layer:
            s.wait_ge(k.layer_done, layer)
        for dst, src in ((wk, "dn_wk"), (wq, "dn_wq"), (wv, "dn_wv"), (wb, "dn_wb"), (lnw, "dn_lnw"), (lnb, "dn_lnb")):
            full = dst[:, :, :] if len(dst.shape) == 3 else dst[:, :]
            s.dma_start(full, d[src]).then_inc(w_in, 16)

    def tensor(t):
        t.wait_ge(w_in, 96)

        def project(i, par):
            t.wait_ge(staged, 2 * i + par + 1)
            weights = ([wk[:, V * m:V * m + V, :] for m in range(HD // V)] + [wq[:, V * m:V * m + V, :] for m in range(HD // V)]
                       + [wv[:, :, :], wb[:, :]])
            for m, w in enumerate(weights):
                g = m % 2
                t.wait_ge(emptied[g], (2 * i + par) * (PIECES // 2) + m // 2 + 1)
                cols = [w[:, f, :] for f in range(V)] if m < PIECES - 1 else [w]
                for f, wf in enumerate(cols):
                    for b in range(B):
                        last = nc.tensor.matmul(k.psum[b * BH:(b + 1) * BH, g, f * C:(f + 1) * C], wf, stage[:, b, :],
                                                start=True, stop=True)
                last.then_inc(projected[g], 1)

        def turn(i, par):
            t.wait_ge(o_ready, 2 * i + par + 1)
            t.wait_ge(rows_free, 2 * i + par + 1)
            for f in range(V):
                last = nc.tensor.transpose(k.psum[:, 2, f * P:(f + 1) * P], o[:, :, f], k.ident[:, :])
            last.then_inc(o_rows, 1)

        one_ahead(t, project, turn)

    def scalar(a):
        for g in range(2):
            a.wait_ge(xt[g], NG // 2 + 1)

        def take_in(i, par):
            n = 2 * i + par
            a.wait_ge(stage_free, n + 1)
            k.plain(a)
            nc.scalar.copy(stage[:, :, :], xt_v[:, :, bass.ds(n, 1), :]).then_inc(staged, 1)
            a.wait_ge(raw_free, n + 1)
            a.wait_ge(chunk_free[par], i + 1)
            M = HD // V
            for m in range(PIECES):
                g = m % 2
                a.wait_ge(projected[g], n * (PIECES // 2) + m // 2 + 1)
                bank = k.psum[:, g, :].rearrange("p (f t) -> p f t", f=V)
                if m < 2 * M:
                    dst = (kraw if m < M else q[par])[:, :, (m % M) * V:(m % M) * V + V]
                    nc.scalar.copy(dst.rearrange("p t f -> p f t"), bank).then_inc(emptied[g], 1)
                elif m == 2 * M:
                    nc.scalar.copy(vraw[:, :, :].rearrange("p t f -> p f t"), bank)
                    nc.scalar.activation(vsig[:, :, :].rearrange("p t f -> p f t"), bank, ACT.Sigmoid).then_inc(emptied[g], 1)
                else:
                    nc.scalar.activation(beta[:, :], k.psum[:, g, 0:C], ACT.Sigmoid).then_inc(emptied[g], 1)
            for g in range(2):
                a.wait_ge(emptied[g], (n + 1) * (PIECES // 2) + 1)
            a.sem_inc(stage_free, 1)
            a.sem_inc(raw_in, 1)

        def put_rows(i, par):
            n = 2 * i + par
            a.wait_ge(o_rows, n + 2)
            k.plain(a)
            nc.scalar.copy(om[:, :, bass.ds(n, 1), :].rearrange("p b c (r f) -> p b (c r) f", f=V),
                           k.psum[:, 2, :].rearrange("p (f b r) -> p b r f", f=V, b=B)).then_inc(rows_free, 1)

        one_ahead(a, take_in, put_rows)

    def gpsimd(p):
        c = Chain(p, pool_own)

        def halve(x, width):
            while width > 2:
                width //= 2
                c.step(nc.gpsimd.tensor_tensor(x[:, :, 0:width], x[:, :, 0:width], x[:, :, width:2 * width], ALU.add))

        def prepare(i, par):
            n = 2 * i + par
            p.wait_ge(raw_in, n + 1)
            p.wait_ge(keys_free[par], i + 1)
            c.step(nc.gpsimd.tensor_tensor(sq[:, :, :], kraw[:, :, :], kraw[:, :, :], ALU.mult))
            halve(sq[:, :, :], HD)
            c.step(nc.gpsimd.tensor_tensor(ss[:, :], sq[:, :, 0], sq[:, :, 1], ALU.add))
            c.step(nc.gpsimd.tensor_scalar(ss[:, :], ss[:, :], 1e-24, None, ALU.max))
            c.step(nc.gpsimd.tensor_tensor(norm[:, :], ss[:, :], k.mhalf[:, 0:C], ALU.pow))
            c.step(nc.gpsimd.tensor_tensor(vsig[:, :, :], vsig[:, :, :], vraw[:, :, :], ALU.mult))
            c.do(nc.gpsimd.tensor_tensor(vb[par][:, :, :], vsig[:, :, :], beta[:, :].unsqueeze(2).to_broadcast([P, C, V]), ALU.mult))
            c.step(nc.gpsimd.tensor_tensor(kn[par][:, :, :], kraw[:, :, :], norm[:, :].unsqueeze(2).to_broadcast([P, C, HD]), ALU.mult))
            c.step(nc.gpsimd.tensor_tensor(kb[par][:, :, :], kn[par][:, :, :], beta[:, :].unsqueeze(2).to_broadcast([P, C, HD]), ALU.mult))
            c.restart()
            p.sem_inc(raw_free, 1)
            p.sem_inc(prepared, 1)

        def read_out(i, par):
            n = 2 * i + par
            p.wait_ge(states, n + 1)
            for z in range(OQ):
                t0 = z * (C // OQ)
                c.step(nc.gpsimd.tensor_tensor(qs[:, :, :, :], hist[par][:, 1 + t0:1 + t0 + C // OQ, :].rearrange("p t (j d) -> p t j d", j=V),
                                               q[par][:, t0:t0 + C // OQ, :].unsqueeze(2).to_broadcast([P, C // OQ, V, HD]), ALU.mult))
                if z == 0:
                    p.wait_ge(o_rows, n + 1)
                qf = qs[:, :, :, :].rearrange("p t j d -> p (t j) d")
                halve(qf, HD)
                c.step(nc.gpsimd.tensor_tensor(o[:, t0:t0 + C // OQ, :].rearrange("p t j -> p (t j)"), qf[:, :, 0], qf[:, :, 1], ALU.add))
            c.restart()
            p.sem_inc(o_ready, 1)
            p.sem_inc(chunk_free[par], 1)

        one_ahead(p, prepare, read_out)
        p.wait_ge(root_in, 1)
        nc.gpsimd.tensor_tensor(root[:, :], var[:, :], k.mhalf[:, 0:NT], ALU.pow).then_inc(root_out, 1)

    var = k.sb("dn_var", [P, NT], ctx=ctx)
    root = k.sb("dn_root2", [P, NT], ctx=ctx)
    stats = k.sb("dn_stats2", [P, NT, 6], ctx=ctx)
    mv = k.sb("dn_mv2", [P, NT, 2], ctx=ctx)

    def vector(v):
        c = Chain(v, own)
        c.step(nc.vector.memset(hist[0][:, 0, :], 0.0))
        c.restart()
        STEPS = 8
        with v.Fori(0, NC // 2) as i:
            for par in range(2):
                n = 2 * i + par
                kn3, kb3, vb3, hs = kn[par], kb[par], vb[par], hist[par]
                v.wait_ge(prepared, n + 1)
                k.plain(v)
                with v.Fori(0, C // STEPS) as m:
                    for z in range(STEPS):
                        t = m * STEPS + z
                        S3 = hs[:, bass.ds(t, 1), :].rearrange("p t (j d) -> p (t j) d", j=V)
                        kbt = kb3[:, bass.ds(t, 1), :].to_broadcast([P, V, HD])
                        knt = kn3[:, bass.ds(t, 1), :].to_broadcast([P, V, HD])
                        c.step(nc.vector.tensor_tensor(prod[:, :, :], S3, kbt, ALU.mult))
                        c.step(nc.vector.tensor_reduce(ks[:, :], prod[:, :, :], AXX, ALU.add))
                        c.step(nc.vector.tensor_tensor(u[:, :], vb3[:, bass.ds(t, 1), :].rearrange("p t f -> p (t f)"), ks[:, :], ALU.subtract))
                        c.step(nc.vector.tensor_tensor(outer[:, :, :], knt, u[:, :].unsqueeze(2).to_broadcast([P, V, HD]), ALU.mult))
                        c.step(nc.vector.tensor_tensor(hs[:, bass.ds(t + 1, 1), :].rearrange("p t (j d) -> p (t j) d", j=V), S3, outer[:, :, :], ALU.add))
                    c.restart()
                v.wait_ge(chunk_free[1 - par], i + 1)
                c.step(nc.vector.tensor_copy(hist[1 - par][:, 0, :], hist[par][:, C, :]))
                c.restart()
                v.sem_inc(states, 1)
                v.sem_inc(keys_free[par], 1)
        v.wait_ge(rows_free, NC + 1)
        omt = om[:, :, :, :].rearrange("p b c d -> p (b c) d")
        for n in range(NT):
            c.do(nc.vector.bn_stats(stats[:, n, :], omt[:, n, :]))
        c.sync()
        for n in range(NT):
            c.do(nc.vector.bn_aggr(mv[:, n, :], stats[:, n, :]))
        c.sync()
        nc.vector.tensor_scalar(var[:, :], mv[:, :, 1], EPS, None, ALU.add).then_inc(root_in, 1)
        v.wait_ge(root_out, 1)
        for n in range(NT):
            c.do(nc.vector.tensor_scalar(omt[:, n, :], omt[:, n, :], mv[:, n, 0:1], root[:, n:n + 1], ALU.subtract, ALU.mult))
        c.sync()
        HALF = NT // 2
        for h in range(2):
            part, xs = omt[:, h * HALF:(h + 1) * HALF, :], k.X[:, h * HALF:(h + 1) * HALF, :]
            c.step(nc.vector.tensor_tensor(part, part, lnw[:, :].unsqueeze(1).to_broadcast([P, HALF, D]), ALU.mult))
            c.step(nc.vector.tensor_tensor(part, part, lnb[:, :].unsqueeze(1).to_broadcast([P, HALF, D]), ALU.add))
            last = nc.vector.tensor_tensor(xs, xs, part, ALU.add)
            if h == 0:
                c.step(last)
        last.then_inc(k.layer_done, 1)

    k.add(sync=sync, vector=vector, scalar=scalar, tensor=tensor, gpsimd=gpsimd)


def channel_mix(k):
    nc, d, ctx = k.nc, k.dram, k.layer_ctx
    wr, wk, wv = (k.sb(f"cm_{n}", [P, D], ctx=ctx) for n in ("wr", "wk", "wv"))
    mu = k.sb("cm_mu", [P, 2], ctx=ctx)
    one_less = k.sb("cm_one_less", [P, 2], ctx=ctx)
    part = [k.sb(f"cm_part{q}", [P, GT], ctx=ctx) for q in range(2)]
    mixed = [[k.sb(f"cm_mix{g}{q}", [P, GT], ctx=ctx) for q in range(2)] for g in range(2)]
    relu = k.sb("cm_relu", [P, GT], ctx=ctx)
    kact = [k.sb(f"cm_kact{g}", [P, GT], ctx=ctx) for g in range(2)]
    gate = [k.sb(f"cm_gate{g}", [P, GT], ctx=ctx) for g in range(2)]
    gated = k.sb("cm_gated", [P, GT], ctx=ctx)
    w_in, own, a_own = (k.sem(f"cm_{n}") for n in ("w_in", "own", "a_own"))
    mix_in = [k.sem(f"cm_mix_in{g}") for g in range(2)]
    rk = [k.free_sem(f"cm_rk{g}") for g in range(2)]
    acted = [k.free_sem(f"cm_acted{g}") for g in range(2)]
    kv = [k.free_sem(f"cm_kv{g}") for g in range(2)]
    added = [k.free_sem(f"cm_added{g}") for g in range(2)]
    layer = k.layers
    xt = layer_norm(k, "cm")

    def sync(s):
        if layer:
            s.wait_ge(k.layer_done, layer)
        for dst, src in ((wr, "cm_wr"), (wk, "cm_wk"), (wv, "cm_wv"), (mu, "cm_mu")):
            s.dma_start(dst[:, :], d[src]).then_inc(w_in, 16)

    def vector(v):
        c = Chain(v, own)
        v.wait_ge(w_in, 64)
        for g in range(2):
            v.wait_ge(xt[g], NG // 2 + 1)
        c.step(nc.vector.tensor_scalar(one_less[:, :], mu[:, :], -1.0, 1.0, ALU.mult, ALU.add))
        c.restart()

        def mix(i, g):
            v.wait_ge(rk[g], i + 1)
            x = k.XT[:, bass.ds(i * S + g * GT, GT)]
            for q in range(2):
                c.do(nc.vector.tensor_scalar(part[q][:, :], x, mu[:, q:q + 1], None, ALU.mult))
            c.sync()
            lo = 1 - g
            for q in range(2):
                prev = k.XT[:, bass.ds(i * S + g * GT + lo - 1, GT - lo)]
                last = nc.vector.scalar_tensor_tensor(mixed[g][q][:, lo:GT], prev, one_less[:, q:q + 1], part[q][:, lo:GT],
                                                      ALU.mult, ALU.add)
                c.do(last)
                if lo:
                    c.do(nc.vector.tensor_copy(mixed[g][q][:, 0:1], part[q][:, 0:1]))
            c.sync()
            v.sem_inc(mix_in[g], 1)

        def add(i, g):
            v.wait_ge(kv[g], i + 2)
            v.wait_ge(acted[g], i + 2)
            c.step(nc.vector.tensor_tensor(gated[:, :], gate[g][:, :], k.psum[:, 6 + g, :], ALU.mult))
            xs = k.X[:, bass.ds(i * 2 * GROUP + g * GROUP, GROUP), :]
            c.step(nc.vector.tensor_tensor(xs, xs, gated[:, :].rearrange("p (n d) -> p n d", d=D), ALU.add))
            v.sem_inc(added[g], 1)

        with v.Fori(0, B) as i:
            for g in range(2):
                mix(i, g)
            for g in range(2):
                add(i, g)
            c.restart()
        nc.vector.tensor_copy(part[0][:, 0:1], part[0][:, 0:1]).then_inc(k.layer_done, 1)

    def tensor(t):
        t.wait_ge(w_in, 64)
        with t.Fori(0, B) as i:
            for g in range(2):
                t.wait_ge(mix_in[g], i + 1)
                t.wait_ge(acted[g], i + 1)
                for n in range(GROUP):
                    nc.tensor.matmul(k.psum[:, 2 + g, n * D:(n + 1) * D], mixed[g][0][:, n * P:(n + 1) * P], wr[:, :],
                                     start=True, stop=True)
                nc.tensor.matmul(k.psum[:, 4 + g, :], wk[:, :], mixed[g][1][:, :], start=True, stop=True).then_inc(rk[g], 1)
            for g in range(2):
                t.wait_ge(acted[g], i + 2)
                t.wait_ge(added[g], i + 1)
                for n in range(GROUP):
                    last = nc.tensor.matmul(k.psum[:, 6 + g, n * D:(n + 1) * D], kact[g][:, n * P:(n + 1) * P], wv[:, :],
                                            start=True, stop=True)
                last.then_inc(kv[g], 1)

    def scalar(a):
        c = Chain(a, a_own)
        with a.Fori(0, B) as i:
            for g in range(2):
                a.wait_ge(rk[g], i + 2)
                a.wait_ge(kv[g], i + 1)
                c.do(nc.scalar.activation(relu[:, :], k.psum[:, 4 + g, :], ACT.Relu))
                a.wait_ge(added[g], i + 1)
                c.do(nc.scalar.activation(gate[g][:, :], k.psum[:, 2 + g, :], ACT.Sigmoid))
                c.sync()
                c.step(nc.scalar.activation(kact[g][:, :], relu[:, :], ACT.Square))
                a.sem_inc(acted[g], 1)
            c.restart()

    k.add(sync=sync, vector=vector, scalar=scalar, tensor=tensor)


def dense_experts(k):
    nc, d, ctx = k.nc, k.dram, k.layer_ctx
    E = d["L1_ffn_gate_w"].shape[1]
    THRESHOLD = 0.1
    gw = k.sb("de_gw", [P, E], ctx=ctx)
    gb = k.sb("de_gb", [1, GROUP * E], ctx=ctx)
    ew = k.sb("de_ew", [P, E * D], ctx=ctx)
    eb = k.sb("de_eb", [E, D], ctx=ctx)
    stage = [k.sb(f"de_stage{g}", [P, GT], ctx=ctx) for g in range(2)]
    lg, pr, w = (k.sb(f"de_{n}", [P, NT, E], ctx=ctx) for n in ("lg", "pr", "w"))
    m, zs = (k.sb(f"de_{n}", [P, NT], ctx=ctx) for n in ("m", "zs"))
    wst = [k.sb(f"de_wst{g}", [P, GROUP, E], ctx=ctx) for g in range(2)]
    wT = [k.sb(f"de_wT{g}", [E, GT], ctx=ctx) for g in range(2)]
    w_in, own, centred, exped, weighed, a_own = (k.sem(f"de_{n}") for n in ("w_in", "own", "centred", "exped", "weighed", "a_own"))
    staged = [k.sem(f"de_staged{g}") for g in range(2)]
    gated = [k.free_sem(f"de_gated{g}") for g in range(2)]
    taken = [k.free_sem(f"de_taken{g}") for g in range(2)]
    staged2 = [k.sem(f"de_staged2{g}") for g in range(2)]
    turned = [k.sem(f"de_turned{g}") for g in range(2)]
    wT_in = [k.sem(f"de_wT_in{g}") for g in range(2)]
    biased = [k.free_sem(f"de_biased{g}") for g in range(2)]
    expert = [k.sem(f"de_expert{g}") for g in range(2)]
    summed = [k.free_sem(f"de_summed{g}") for g in range(2)]
    group_done = [k.free_sem(f"de_group_done{g}") for g in range(2)]
    wst_free = [k.free_sem(f"de_wst_free{g}") for g in range(2)]
    layer = k.layers
    xt = layer_norm(k, "de")

    def sync(s):
        if layer:
            s.wait_ge(k.layer_done, layer)
        for dst, src in ((gw, "L1_ffn_gate_w"), (gb, "de_gb"), (ew, "de_ew"), (eb, "L1_ffn_expert_b")):
            s.dma_start(dst[:, :], d[src]).then_inc(w_in, 16)

    def gpsimd(p):
        for g in range(2):
            p.wait_ge(xt[g], NG // 2 + 1)
        with p.Fori(0, NG // 2) as i:
            for g in range(2):
                p.wait_ge(gated[g], i + 1)
                k.plain(p)
                nc.gpsimd.tensor_copy(stage[g][:, :], k.XT[:, bass.ds(i * 2 * GT + g * GT, GT)]).then_inc(staged[g], 1)
        p.wait_ge(weighed, 1)
        for g in range(2):
            p.wait_ge(gated[g], NG // 2 + 1)
        with p.Fori(0, NG // 2) as i:
            for g in range(2):
                p.wait_ge(group_done[g], i + 1)
                p.wait_ge(wst_free[g], i + 1)
                k.plain(p)
                nc.gpsimd.tensor_copy(stage[g][:, :], k.XT[:, bass.ds(i * 2 * GT + g * GT, GT)])
                nc.gpsimd.tensor_copy(wst[g][:, :, :], w[:, bass.ds(i * 2 * GROUP + g * GROUP, GROUP), :]).then_inc(staged2[g], 1)

    def tensor(t):
        t.wait_ge(w_in, 64)
        with t.Fori(0, NG // 2) as i:
            for g in range(2):
                t.wait_ge(staged[g], i + 1)
                t.wait_ge(taken[g], i + 1)
                bank = k.psum[:, g, 0:GROUP * E]
                nc.tensor.matmul(bank, k.ones_row[:, :], gb[:, :], start=True, stop=True)
                for n in range(GROUP):
                    last = nc.tensor.matmul(bank[:, n * E:(n + 1) * E], stage[g][:, n * P:(n + 1) * P], gw[:, :],
                                            start=False, stop=True, skip_group_check=True)
                last.then_inc(gated[g], 1)
        for g in range(2):
            t.wait_ge(taken[g], NG // 2 + 1)
        with t.Fori(0, NG // 2) as i:
            for g in range(2):
                t.wait_ge(staged2[g], i + 1)
                t.wait_ge(biased[g], i + 1)
                for n in range(GROUP):
                    last = nc.tensor.transpose(k.psum[0:E, g, n * P:(n + 1) * P], wst[g][:, n, :], k.ident[:, :])
                last.then_inc(turned[g], 1)
                t.wait_ge(wT_in[g], i + 1)
                for n in range(GROUP):
                    last = nc.tensor.matmul(k.psum[:, g, n * D:(n + 1) * D], wT[g][:, n * P:(n + 1) * P], eb[:, :],
                                            start=True, stop=True)
                last.then_inc(turned[g], 1)
                for n in range(GROUP):
                    u = n % 2
                    use = i * 4 + g * 2 + n // 2
                    t.wait_ge(summed[u], use + 1)
                    for h in range(2):
                        last = nc.tensor.matmul(k.psum[:, 2 + 2 * u + h, :], stage[g][:, n * P:(n + 1) * P],
                                                ew[:, h * 512:(h + 1) * 512], start=True, stop=True)
                    last.then_inc(expert[u], 1)
                t.wait_ge(expert[1], i * 4 + g * 2 + 2)
                t.sem_inc(group_done[g], 1)

    def scalar(a):
        a.wait_ge(centred, 1)
        nc.scalar.activation(pr[:, :, :], lg[:, :, :], ACT.Exp).then_inc(exped, 1)
        with a.Fori(0, NG // 2) as i:
            for g in range(2):
                a.wait_ge(turned[g], 2 * i + 1)
                nc.scalar.copy(wT[g][:, :], k.psum[0:E, g, :]).then_inc(wT_in[g], 1)

    def vector(v):
        c = Chain(v, own)
        with v.Fori(0, NG // 2) as i:
            for g in range(2):
                v.wait_ge(gated[g], i + 2)
                nc.vector.tensor_copy(lg[:, bass.ds(i * 2 * GROUP + g * GROUP, GROUP), :],
                                      k.psum[:, g, 0:GROUP * E].rearrange("p (n e) -> p n e", e=E)).then_inc(taken[g], 1)
        for g in range(2):
            v.wait_ge(taken[g], NG // 2 + 1)
        wide = lambda x: x[:, :].unsqueeze(2).to_broadcast([P, NT, E])
        c.step(nc.vector.tensor_reduce(m[:, :], lg[:, :, :], AXX, ALU.max))
        nc.vector.tensor_tensor(lg[:, :, :], lg[:, :, :], wide(m), ALU.subtract).then_inc(centred, 1)
        v.wait_ge(exped, 1)
        c.step(nc.vector.tensor_reduce(zs[:, :], pr[:, :, :], AXX, ALU.add))
        c.step(nc.vector.reciprocal(m[:, :], zs[:, :]))
        c.step(nc.vector.tensor_tensor(pr[:, :, :], pr[:, :, :], wide(m), ALU.mult))
        c.step(nc.vector.scalar_tensor_tensor(w[:, :, :], pr[:, :, :], THRESHOLD, pr[:, :, :], ALU.is_ge, ALU.mult))
        c.step(nc.vector.tensor_reduce(zs[:, :], w[:, :, :], AXX, ALU.add))
        c.step(nc.vector.scalar_tensor_tensor(zs[:, :], zs[:, :], 0.0, zs[:, :], ALU.is_equal, ALU.add))
        c.step(nc.vector.reciprocal(m[:, :], zs[:, :]))
        c.step(nc.vector.tensor_tensor(w[:, :, :], w[:, :, :], wide(m), ALU.mult))
        v.sem_inc(weighed, 1)
        c.restart()
        with v.Fori(0, NG // 2) as i:
            for g in range(2):
                v.wait_ge(turned[g], 2 * i + 2)
                xs = k.X[:, bass.ds(i * 2 * GROUP + g * GROUP, GROUP), :]
                c.step(nc.vector.tensor_tensor(xs, xs, k.psum[:, g, :].rearrange("p (n d) -> p n d", d=D), ALU.add))
                v.sem_inc(biased[g], 1)
                for h in range(2):
                    for u in range(2):
                        v.wait_ge(expert[u], i * 4 + g * 2 + h + 1)
                    k.plain(v)
                    for e in range(E):
                        for u in range(2):
                            tile = i * 2 * GROUP + g * GROUP + 2 * h + u
                            x1 = k.X[:, bass.ds(tile, 1), :].rearrange("p n d -> p (n d)")
                            c.do(nc.vector.scalar_tensor_tensor(x1, k.psum[:, 2 + 2 * u + e // 4, (e % 4) * D:(e % 4 + 1) * D],
                                                                wst[g][:, 2 * h + u, e:e + 1], x1, ALU.mult, ALU.add))
                        c.sync()
                    for u in range(2):
                        v.sem_inc(summed[u], 1)
                v.sem_inc(wst_free[g], 1)
            c.restart()
        nc.vector.tensor_copy(m[:, 0:1], m[:, 0:1]).then_inc(k.layer_done, 1)

    k.add(sync=sync, vector=vector, scalar=scalar, tensor=tensor, gpsimd=gpsimd)


def test_time_mlp(k):
    nc, d, ctx = k.nc, k.dram, k.layer_ctx
    LR = 0.001
    ETA = LR * 2 / (B * D)
    TOL2 = (1e-4) ** 2
    T = P // B
    NCH = S // T
    SWEEPS = 3
    R = 3 * P
    wkv = k.sb("tt_wkv", [P, 2 * D], ctx=ctx)
    wq = k.sb("tt_wq", [P, D], ctx=ctx)
    WN = 3 * D + 2
    w0 = k.sb("tt_w0", [P, WN], ctx=ctx)
    ws = k.sb("tt_ws", [P, WN], ctx=ctx)
    earlier = k.sb("tt_earlier", [P, P], ctx=ctx)
    ones = k.sb("tt_ones", [P, 1], ctx=ctx)
    stage = [k.sb(f"tt_stage{g}", [P, B, T], ctx=ctx) for g in range(2)]
    kv = [k.sb(f"tt_kv{g}", [P, R], ctx=ctx) for g in range(2)]
    gm = [k.sb(f"tt_gm{g}", [P, P], ctx=ctx) for g in range(2)]
    sg, aT, sp, tsp, usp, pm, dyT, qm, dhT = (k.sb(f"tt_{n}", [P, P], ctx=ctx) for n in
                                               ("sg", "aT", "sp", "tsp", "usp", "pm", "dyT", "qm", "dhT"))
    rowb = [k.sb(f"tt_rows{g}", [P, R], ctx=ctx) for g in range(2)]
    diff, dsum, vsum, sqr = (k.sb(f"tt_{n}", [P, R], ctx=ctx) for n in ("diff", "dsum", "vsum", "sqr"))
    verdict = k.sb("tt_verdict", [P, 6], ctx=ctx)
    vrow = k.sb("tt_vrow", [1, 8], ctx=ctx)
    flag = k.sb("tt_flag", [1, 1], I32, ctx=ctx)
    w1, w2, w2t = (ws[:, n * D:(n + 1) * D] for n in range(3))
    b1, b2 = ws[:, 3 * D:3 * D + 1], ws[:, 3 * D + 1:3 * D + 2]
    bank = lambda n: k.psum[:, n, :]
    PREP, HB, PB, YB, QB, DB, TB, WB = range(8)
    w_in = k.sem("tt_w_in")
    layer = k.layers
    xt = layer_norm(k, "tt")
    xt_v = k.XT[:, :].rearrange("p (b c t) -> p b c t", b=B, c=NCH)

    def sync(s):
        if layer:
            s.wait_ge(k.layer_done, layer)
        for dst, src in ((wkv, "L1_attn_W_KV"), (wq, "L1_attn_W_Q"), (w0, "tt_w0"), (earlier, "tt_earlier"), (ones, "tt_ones")):
            s.dma_start(dst[:, :], d[src]).then_inc(w_in, 16)

    class Run:

        def __init__(self, tag, sweeps, unrolled):
            names = ("staged", "kv_psum", "kv_in", "gram", "gm_in", "h", "sig", "a", "gate", "p", "pm", "y", "dy", "q", "qm",
                     "da", "dh", "turned", "rows", "grads", "weights", "own", "p_own", "judged")
            self.sweeps, self.unrolled = sweeps, unrolled
            (self.staged, self.kv_psum, self.kv_in, self.gram, self.gm_in, self.h, self.sig, self.a, self.gate, self.p,
             self.pm, self.y, self.dy, self.q, self.qm, self.da, self.dh, self.turned, self.rows, self.grads, self.weights,
             self.own, self.p_own, self.judged) = (k.sem(f"tt{tag}_{n}") for n in names)

        def chunks(self, eng, first, body):
            first()
            with eng.Fori(0, NCH // 2 - 1) as i:
                body(2 * i, 0, True)
                body(2 * i + 1, 1, True)
            body(NCH - 2, 0, True)
            body(NCH - 1, 1, False)

        def each(self, eng, c, sweep):
            N = self.sweeps
            if self.unrolled:
                for s in range(N):
                    sweep(c * N + s, c * (N - 1) + s - 1 if s else None, s)
            else:
                sweep(c * N, None, 0)
                with eng.Fori(0, N - 1) as s:
                    sweep(c * N + s + 1, c * (N - 1) + s, -1)

        def buf(self, s):
            return rowb[s % 2 if self.unrolled else 0]

        def before(self, s):
            return rowb[(s - 1) % 2 if self.unrolled else 0]

        def tensor(self, t):
            def prep_a(c, g):
                t.wait_ge(self.staged, c + 1)
                for lhsT, rhs, o in ((wkv[:, 0:D], stage[g][:, :, :], 0), (wkv[:, D:2 * D], stage[g][:, :, :], P)):
                    nc.tensor.matmul(bank(PREP)[:, o:o + P], lhsT, rhs, start=True, stop=True)
                nc.tensor.matmul(bank(PREP)[:, 2 * P:3 * P], stage[g][:, :, :], wkv[:, 0:D], start=True, stop=True).then_inc(self.kv_psum, 1)

            def prep_b(c, g):
                t.wait_ge(self.kv_in, c + 1)
                nc.tensor.matmul(bank(PREP)[:, 3 * P:4 * P], kv[g][:, 0:P], kv[g][:, 0:P], start=True, stop=True).then_inc(self.gram, 1)

            def first():
                prep_a(0, 0)
                prep_b(0, 0)

            def body(c, g, more):
                def sweep(n, m, s):
                    if s == 0:
                        t.wait_ge(self.gm_in, c + 1)
                        t.wait_ge(self.weights, c + 1)
                        nc.tensor.matmul(bank(HB)[:, 0:P], w1, kv[g][:, 0:P], start=True, stop=True).then_inc(self.h, 1)
                        if more:
                            prep_a(c + 1, 1 - g)
                    else:
                        nc.tensor.matmul(bank(HB)[:, 0:P], w1, kv[g][:, 0:P], start=True, stop=False)
                        t.wait_ge(self.rows, n)
                        nc.tensor.matmul(bank(HB)[:, 0:P], self.before(s)[:, 2 * P:3 * P], gm[g][:, :], start=False,
                                         stop=True).then_inc(self.h, 1)
                    t.wait_ge(self.a, n + 1)
                    if s:
                        nc.tensor.matmul(bank(PB)[:, 0:P], aT[:, :], aT[:, :], start=True, stop=True).then_inc(self.p, 1)
                        nc.tensor.matmul(bank(YB)[:, 0:P], w2, aT[:, :], start=True, stop=False)
                        t.wait_ge(self.pm, m + 1)
                        nc.tensor.matmul(bank(YB)[:, 0:P], self.before(s)[:, P:2 * P], pm[:, :], start=False,
                                         stop=True).then_inc(self.y, 1)
                    else:
                        nc.tensor.matmul(bank(YB)[:, 0:P], w2, aT[:, :], start=True, stop=True).then_inc(self.y, 1)
                        if more:
                            prep_b(c + 1, 1 - g)
                    nc.tensor.transpose(bank(TB)[:, 0:P], aT[:, :], k.ident[:, :])
                    t.wait_ge(self.dy, n + 1)
                    if s:
                        nc.tensor.matmul(bank(QB)[:, 0:P], dyT[:, :], dyT[:, :], start=True, stop=True).then_inc(self.q, 1)
                        nc.tensor.matmul(bank(DB)[:, 0:P], w2t, dyT[:, :], start=True, stop=False)
                        t.wait_ge(self.qm, m + 1)
                        nc.tensor.matmul(bank(DB)[:, 0:P], self.before(s)[:, 0:P], qm[:, :], start=False,
                                         stop=True).then_inc(self.da, 1)
                    else:
                        nc.tensor.matmul(bank(DB)[:, 0:P], w2t, dyT[:, :], start=True, stop=True).then_inc(self.da, 1)
                    nc.tensor.transpose(bank(TB)[:, P:2 * P], dyT[:, :], k.ident[:, :])
                    t.wait_ge(self.dh, n + 1)
                    nc.tensor.transpose(bank(TB)[:, 2 * P:3 * P], dhT[:, :], k.ident[:, :]).then_inc(self.turned, 1)

                self.each(t, c, sweep)
                r = self.buf(self.sweeps - 1)
                t.wait_ge(self.rows, (c + 1) * self.sweeps)
                for lhsT, rhs, o, n in ((kv[g][:, 2 * P:3 * P], r[:, 2 * P:3 * P], 0, P), (r[:, 0:P], r[:, P:2 * P], D, P),
                                        (r[:, P:2 * P], r[:, 0:P], 2 * D, P), (r[:, 2 * P:3 * P], ones[:, :], 3 * D, 1),
                                        (r[:, P:2 * P], ones[:, :], 3 * D + 1, 1)):
                    last = nc.tensor.matmul(bank(WB)[:, o:o + n], lhsT, rhs, start=True, stop=True)
                last.then_inc(self.grads, 1)

            self.chunks(t, first, body)

        def scalar(self, a):
            def take_kv(c, g):
                a.wait_ge(self.kv_psum, c + 1)
                nc.scalar.copy(kv[g][:, :], bank(PREP)[:, 0:R]).then_inc(self.kv_in, 1)

            def body(c, g, more):
                def sweep(n, m, s):
                    a.wait_ge(self.h, n + 1)
                    nc.scalar.activation(sg[:, :], bank(HB)[:, 0:P], ACT.Sigmoid, bias=b1).then_inc(self.sig, 1)
                    if s == 0 and more:
                        take_kv(c + 1, 1 - g)
                    if self.unrolled and s == 1:
                        a.wait_ge(self.judged, c + 1)
                    a.wait_ge(self.turned, n + 1)
                    r = self.buf(s)
                    nc.scalar.copy(r[:, 0:P], bank(TB)[:, 0:P])
                    nc.scalar.mul(r[:, P:R], bank(TB)[:, P:R], -ETA).then_inc(self.rows, 1)

                self.each(a, c, sweep)

            self.chunks(a, lambda: take_kv(0, 0), body)

        def gpsimd(self, p):
            c_ = Chain(p, self.p_own)

            def put_stage(c, g):
                k.plain(p)
                nc.gpsimd.tensor_copy(stage[g][:, :, :], xt_v[:, :, bass.ds(c, 1), :]).then_inc(self.staged, 1)

            def body(c, g, more):
                def sweep(n, m, s):
                    if s == 0 and more:
                        p.wait_ge(self.gm_in, c + 1)
                        put_stage(c + 1, 1 - g)
                    p.wait_ge(self.a, n + 1)
                    c_.do(nc.gpsimd.tensor_tensor(tsp[:, :], aT[:, :], sg[:, :], ALU.mult))
                    c_.do(nc.gpsimd.tensor_tensor(usp[:, :], aT[:, :], sg[:, :], ALU.add))
                    c_.sync()
                    c_.step(nc.gpsimd.tensor_tensor(sp[:, :], usp[:, :], tsp[:, :], ALU.subtract))
                    c_.restart()
                    p.sem_inc(self.gate, 1)

                self.each(p, c, sweep)
                if self.unrolled:
                    new, old = self.buf(self.sweeps - 1), self.before(self.sweeps - 1)
                    p.wait_ge(self.rows, (c + 1) * self.sweeps)
                    c_.do(nc.gpsimd.tensor_tensor(diff[:, :], new[:, :], old[:, :], ALU.subtract))
                    c_.do(nc.gpsimd.tensor_tensor(sqr[:, :], new[:, :], new[:, :], ALU.mult))
                    c_.sync()
                    p.sem_inc(self.judged, 1)
                    c_.do(nc.gpsimd.tensor_tensor(diff[:, :], diff[:, :], diff[:, :], ALU.mult))
                    c_.do(nc.gpsimd.tensor_tensor(vsum[:, :], vsum[:, :], sqr[:, :], ALU.add))
                    c_.sync()
                    c_.step(nc.gpsimd.tensor_tensor(dsum[:, :], dsum[:, :], diff[:, :], ALU.add))
                    c_.restart()

            self.chunks(p, lambda: put_stage(0, 0), body)
            p.sem_inc(self.judged, 1)

        def vector(self, v):
            c_ = Chain(v, self.own)

            def take_gram(c, g):
                v.wait_ge(self.gram, c + 1)
                nc.vector.scalar_tensor_tensor(gm[g][:, :], bank(PREP)[:, 3 * P:4 * P], 1.0, earlier[:, :], ALU.add,
                                               ALU.mult).then_inc(self.gm_in, 1)

            def body(c, g, more):
                def sweep(n, m, s):
                    v.wait_ge(self.sig, n + 1)
                    nc.vector.scalar_tensor_tensor(aT[:, :], bank(HB)[:, 0:P], b1, sg[:, :], ALU.add, ALU.mult).then_inc(self.a, 1)
                    if s:
                        v.wait_ge(self.p, m + 1)
                        nc.vector.scalar_tensor_tensor(pm[:, :], bank(PB)[:, 0:P], 1.0, earlier[:, :], ALU.add, ALU.mult).then_inc(self.pm, 1)
                    v.wait_ge(self.y, n + 1)
                    nc.vector.scalar_tensor_tensor(dyT[:, :], bank(YB)[:, 0:P], b2, kv[g][:, P:2 * P], ALU.add, ALU.subtract).then_inc(self.dy, 1)
                    if s:
                        v.wait_ge(self.q, m + 1)
                        nc.vector.scalar_tensor_tensor(qm[:, :], bank(QB)[:, 0:P], -ETA, earlier[:, :], ALU.mult, ALU.mult).then_inc(self.qm, 1)
                    elif more:
                        take_gram(c + 1, 1 - g)
                    v.wait_ge(self.gate, n + 1)
                    v.wait_ge(self.da, n + 1)
                    nc.vector.tensor_tensor(dhT[:, :], bank(DB)[:, 0:P], sp[:, :], ALU.mult).then_inc(self.dh, 1)

                self.each(v, c, sweep)
                v.wait_ge(self.grads, c + 1)
                nc.vector.tensor_tensor(ws[:, :], ws[:, :], bank(WB)[:, 0:WN], ALU.add).then_inc(self.weights, 1)

            def first():
                nc.vector.tensor_copy(ws[:, :], w0[:, :]).then_inc(self.weights, 1)
                take_gram(0, 0)

            self.chunks(v, first, body)
            v.wait_ge(self.weights, NCH + 1)

    fast = Run("f", SWEEPS, True)
    exact = Run("e", T, False)
    (zeroed, fold, summed, flagged, q_in, bias_row, own2, done_e) = (
        k.sem(f"tt_{n}") for n in ("zeroed", "fold", "summed", "flagged", "q_in", "bias_row", "own2", "done_e"))
    settle = k.sem("tt_settle")

    def branch(eng, run):
        eng.wait_ge(flagged, 1)
        redo = eng.value_load(flag[0:1, 0:1], min_val=0, max_val=1)
        with eng.If(redo != 0):
            run(eng)

    def vector_judge(v):
        c = Chain(v, own2)
        v.wait_ge(w_in, 80)
        fast.vector(v)
        v.wait_ge(fast.judged, NCH + 2)
        c.do(nc.vector.tensor_reduce(verdict[:, 0:3], dsum[:, :].rearrange("p (q r) -> p q r", q=3), AXX, ALU.add))
        c.do(nc.vector.tensor_reduce(verdict[:, 3:6], vsum[:, :].rearrange("p (q r) -> p q r", q=3), AXX, ALU.add))
        c.sync()
        v.sem_inc(summed, 1)
        v.wait_ge(fold, 1)
        tot = k.psum[0:1, PREP, 0:6]
        c.step(nc.vector.tensor_copy(vrow[:, 0:6], tot))
        c.step(nc.vector.scalar_tensor_tensor(vrow[:, 0:3], vrow[:, 3:6], TOL2, vrow[:, 0:3], ALU.mult, ALU.is_ge))
        c.step(nc.vector.tensor_scalar(vrow[:, 3:6], vrow[:, 3:6], 1e30, None, ALU.is_lt))
        c.step(nc.vector.tensor_tensor(vrow[:, 0:3], vrow[:, 0:3], vrow[:, 3:6], ALU.mult))
        c.step(nc.vector.tensor_tensor(vrow[:, 6:7], vrow[:, 0:1], vrow[:, 1:2], ALU.mult))
        c.step(nc.vector.tensor_tensor(vrow[:, 7:8], vrow[:, 6:7], vrow[:, 2:3], ALU.mult))
        nc.vector.tensor_scalar(flag[:, :], vrow[:, 7:8], -1.0, 1.0, ALU.mult, ALU.add).then_inc(flagged, 1)
        branch(v, exact.vector)

    b2row = k.sb("tt_b2row", [1, GT], ctx=ctx)
    qT = [k.sb(f"tt_qT{g}", [P, GT], ctx=ctx) for g in range(2)]
    sgq = [k.sb(f"tt_sgq{g}", [P, GT], ctx=ctx) for g in range(2)]
    aq = [k.sb(f"tt_aq{g}", [P, GT], ctx=ctx) for g in range(2)]
    q_psum, hq, sq, a_q, yq = ([k.sem(f"tt_{n}{g}") for g in range(2)] for n in ("q_psum", "hq", "sq", "a_q", "yq"))
    qT_in = [k.sem(f"tt_qT_in{g}") for g in range(2)]
    added = [k.free_sem(f"tt_added{g}") for g in range(2)]

    def vector(v):
        vector_judge(v)
        v.sem_inc(settle, 1)
        v.wait_ge(bias_row, 1)
        for n in range(GROUP):
            last = nc.vector.tensor_copy(b2row[:, n * D:(n + 1) * D], k.psum[0:1, WB, 0:D])
        last.then_inc(bias_row, 1)
        with v.Fori(0, NG // 2) as i:
            for g in range(2):
                v.wait_ge(sq[g], i + 1)
                nc.vector.scalar_tensor_tensor(aq[g][:, :], bank(2 + g), b1, sgq[g][:, :], ALU.add, ALU.mult).then_inc(a_q[g], 1)
            for g in range(2):
                v.wait_ge(yq[g], i + 1)
                xs = k.X[:, bass.ds(i * 2 * GROUP + g * GROUP, GROUP), :]
                nc.vector.tensor_tensor(xs, xs, bank(4 + g).rearrange("p (n d) -> p n d", d=D), ALU.add).then_inc(added[g], 1)
        for g in range(2):
            v.wait_ge(added[g], NG // 2 + 1)
        nc.vector.tensor_copy(vrow[:, 0:1], vrow[:, 0:1]).then_inc(k.layer_done, 1)

    def tensor(t):
        t.wait_ge(w_in, 80)
        fast.tensor(t)
        t.wait_ge(summed, 1)
        nc.tensor.matmul(k.psum[0:1, PREP, 0:6], ones[:, :], verdict[:, :], start=True, stop=True).then_inc(fold, 1)
        branch(t, exact.tensor)
        t.wait_ge(settle, 1)
        nc.tensor.transpose(k.psum[0:1, WB, 0:D], b2, k.ident[:, :]).then_inc(bias_row, 1)
        t.wait_ge(bias_row, 2)
        with t.Fori(0, NG // 2) as i:
            for g in range(2):
                t.wait_ge(added[g], i + 1)
                nc.tensor.matmul(bank(g), wq[:, :], k.XT[:, bass.ds(i * 2 * GT + g * GT, GT)], start=True, stop=True).then_inc(q_psum[g], 1)
            for g in range(2):
                t.wait_ge(qT_in[g], i + 1)
                nc.tensor.matmul(bank(2 + g), w1, qT[g][:, :], start=True, stop=True).then_inc(hq[g], 1)
            for g in range(2):
                t.wait_ge(a_q[g], i + 1)
                nc.tensor.matmul(bank(4 + g), k.ones_row[:, :], b2row[:, :], start=True, stop=True)
                for n in range(GROUP):
                    last = nc.tensor.matmul(bank(4 + g)[:, n * D:(n + 1) * D], aq[g][:, n * P:(n + 1) * P], w2,
                                            start=False, stop=True, skip_group_check=True)
                last.then_inc(yq[g], 1)

    def scalar(a):
        fast.scalar(a)
        branch(a, exact.scalar)
        a.wait_ge(settle, 1)
        with a.Fori(0, NG // 2) as i:
            for g in range(2):
                a.wait_ge(q_psum[g], i + 1)
                nc.scalar.copy(qT[g][:, :], bank(g)).then_inc(qT_in[g], 1)
            for g in range(2):
                a.wait_ge(hq[g], i + 1)
                nc.scalar.activation(sgq[g][:, :], bank(2 + g), ACT.Sigmoid, bias=b1).then_inc(sq[g], 1)

    def gpsimd(p):
        for g in range(2):
            p.wait_ge(xt[g], NG // 2 + 1)
        nc.gpsimd.memset(dsum[:, :], 0.0).then_inc(zeroed, 1)
        nc.gpsimd.memset(vsum[:, :], 0.0).then_inc(zeroed, 1)
        p.wait_ge(zeroed, 2)
        p.sem_inc(fast.judged, 1)
        fast.gpsimd(p)
        branch(p, exact.gpsimd)

    k.add(sync=sync, vector=vector, scalar=scalar, tensor=tensor, gpsimd=gpsimd)


def attention(k, tag, H, HD, blocked):
    nc, d, ctx = k.nc, k.dram, k.layer_ctx
    BLOCK = 64
    N = B * H
    DV = HD
    KR = 6 * HD
    MR = 96
    ROWS = MR + 3
    V1 = DV + 1
    V3 = 3 * V1
    LAG = 3
    NPT = LAG + 1
    BY_POOL, BY_DVE, WHOLE = (0, 1, 3, 5, 6), (4, 7), (2,)
    ROW_HALVES = (2, 3, 4, 4, 3, 0, 0, 0)
    LIFT = 12 * log(2)
    SCALE = float(HD) ** -0.5
    NTB = S // P
    w = {n: k.sb(f"{tag}_w{n}", [P, D], ctx=ctx) for n in "qkv"}
    bias = k.sb(f"{tag}_bias", [P, 3], ctx=ctx) if not blocked else None
    gamma_beta = k.sb(f"{tag}_gamma_beta", [P, 2], ctx=ctx) if not blocked else None
    x = {n: [k.sb(f"{tag}_x{n}{g}", [P, GT], ctx=ctx) for g in range(2)] for n in "qkv"}
    parts = {n: [k.sb(f"{tag}_p{n}{g}", [P, 3, GT], BF16, ctx=ctx) for g in range(2)] for n in "qk"}
    rest = {n: k.sb(f"{tag}_r{n}", [P, GT], ctx=ctx) for n in "qk"}
    vrows = k.sb(f"{tag}_vrows", [P, B, H, NTB, V1], ctx=ctx)
    NST = 4
    qs = [k.sb(f"{tag}_qs{g}", [P, S], BF16, ctx=ctx) for g in range(NST)]
    kst = [k.sb(f"{tag}_ks{g}", [P, S], BF16, ctx=ctx) for g in range(NST)]
    vparts = k.sb(f"{tag}_vparts", [P, N * NTB, 3, V1], BF16, ctx=ctx)
    vrest = k.sb(f"{tag}_vrest", [P, N * NTB, V1], ctx=ctx)
    vh = [k.sb(f"{tag}_vh{g}", [P, NTB, V1], ctx=ctx) for g in range(2)]
    v3 = [k.sb(f"{tag}_v3{g}", [P, NTB, 3, V1], BF16, ctx=ctx) for g in range(2)]
    pt = [k.sb(f"{tag}_pt{g}", [P, S], ctx=ctx) for g in range(NPT)]
    upper = [t_[:, :].bitcast(BF16).rearrange("p (s two) -> p two s", two=2)[:, 1, :] for t_ in pt]
    prest = [k.sb(f"{tag}_prest{g}", [P, S], F16, ctx=ctx) for g in range(NPT)]
    oT = [k.sb(f"{tag}_oT{g}", [V3, S], ctx=ctx) for g in range(2)]
    osum = k.sb(f"{tag}_osum", [P, NTB, V1], ctx=ctx)
    NM = 3 if blocked else 2
    mx = [k.sb(f"{tag}_mx{g}", [P, NTB, NM], ctx=ctx) for g in range(2)]
    m1 = k.sb(f"{tag}_m1", [P, 4, NTB], ctx=ctx)
    mp = k.sb(f"{tag}_mp", [P, NTB, 3], BF16, ctx=ctx)
    corr = [k.sb(f"{tag}_corr{g}", [P, NTB], ctx=ctx) for g in range(2)]
    dcorr = [k.sb(f"{tag}_dcorr{g}", [P, NTB], ctx=ctx) for g in range(2)]
    den = k.sb(f"{tag}_den", [P, NTB], ctx=ctx)
    onorm = k.sb(f"{tag}_onorm", [P, NTB, DV], ctx=ctx)
    stk = {n: nc.dram_tensor(f"{tag}_{n}stk", (N, KR, S), BF16, kind="Internal").ap() for n in "qk"}
    bank = lambda n: k.psum[:, n, :]
    mk = lambda n: k.sem(f"{tag}_{n}")
    pair = lambda n, free=False: [(k.free_sem if free else k.sem)(f"{tag}_{n}{g}") for g in range(2)]
    (w_in, ready_w, own, p_own) = map(mk, ("w_in", "ready_w", "own", "p_own"))
    qkv_psum, x_in, v_turned = pair("qkv_psum"), pair("x_in", True), pair("v_turned", True)
    split, stored, v_done = pair("split"), pair("stored", True), pair("v_done", True)
    hi_in = pair("hi_in")
    vh_in = pair("vh_in")
    loaded = [k.sem(f"{tag}_loaded{g}") for g in range(NST)]
    s_psum, s_read = pair("s_psum"), pair("s_read", True)
    st_psum, pt_in = pair("st_psum"), pair("pt_in", True)
    pv = [k.free_sem(f"{tag}_pv{g}") for g in range(NPT)]
    pv_all = lambda n: (pv[NPT - 1], n * (NTB // NPT) + 1)
    rest_v, rest_p, v_split = mk("rest_v"), mk("rest_p"), mk("v_split")
    oT_in = k.free_sem(f"{tag}_oT_in")
    all_done = mk("all_done")
    corr_used = k.free_sem(f"{tag}_corr_used")
    neg_in, m_turned, m_in, o_turned, head_done, corr_in, corr_exp = map(
        mk, ("neg_in", "m_turned", "m_in", "o_turned", "head_done", "corr_in", "corr_exp"))
    layer = k.layers
    if blocked:
        xt = layer_norm(k, tag)
        n_w = 3
        O = k.XT
    else:
        aff_in = k.sem(f"{tag}_aff_in")
        xt = layer_norm(k, tag, twice=True, affine=(gamma_beta[:, 0:1], gamma_beta[:, 1:2]), affine_in=(aff_in, 16))
        n_w = 5
        wv_full = k.sb(f"{tag}_wv_full", [P, D, 8], ctx=ctx)
        bv_full = k.sb(f"{tag}_bv_full", [P, 8], ctx=ctx)

    def loop(eng, first, body):
        def at(n, i, m, **ends):
            body(n, lambda r, ahead=0: (i * (NST // r) + (m + ahead) // r, (m + ahead) % r), **ends)
        first()
        at(0, 0, 0, begins=True)
        at(1, 0, 1)
        with eng.Fori(0, N // NST - 1) as i:
            for m in range(2, 2 + NST):
                at(i * NST + m, i, m)
        at(N - 2, 0, N - 2)
        at(N - 1, 0, N - 1, more=False)

    def sync(s):
        if layer:
            s.wait_ge(k.layer_done, layer)
        if blocked:
            for n in "qkv":
                s.dma_start(w[n][:, :], d[f"{tag}_w{n}"]).then_inc(w_in, 16)
        else:
            s.dma_start(gamma_beta[:, :], d[f"{tag}_gamma_beta"]).then_inc(aff_in, 16)
            for n in "qk":
                s.dma_start(w[n][:, :], d[f"{tag}_w{n}"]).then_inc(w_in, 16)
            s.dma_start(bias[:, 0:2], d[f"{tag}_bias"]).then_inc(w_in, 16)
            s.dma_start(wv_full[:, :, :], d["L2_attn_Wv"].rearrange("p (c u) -> p c u", u=8)).then_inc(w_in, 16)
            s.dma_start(bv_full[:, :], d["L2_attn_bv"].rearrange("(c u) -> c u", u=8)).then_inc(w_in, 16)
        order = {"q": (0, 0, 0, 1, 1, 2), "k": (0, 1, 2, 0, 1, 0)}
        with s.Fori(0, B) as i:
            for g in range(2):
                s.wait_ge(split[g], i + 1)
                k.plain(s)
                for n in "qk":
                    for blk, part in enumerate(order[n]):
                        dst = stk[n][bass.ds(i * H, H), blk * HD:(blk + 1) * HD, g * GT:(g + 1) * GT]
                        s.dma_start(dst, parts[n][g][:, part, :]).then_inc(stored[g], 16)
        for g in range(2):
            s.wait_ge(stored[g], B * 12 * 16 + 1)
        s.wait_ge(ready_w, 2)

        def load(n, g):
            s.dma_start(qs[g][0:KR, :], stk["q"][bass.ds(n, 1), :, :].rearrange("n r s -> (n r) s")).then_inc(loaded[g], 16)
            s.dma_start(kst[g][0:KR, :], stk["k"][bass.ds(n, 1), :, :].rearrange("n r s -> (n r) s")).then_inc(loaded[g], 16)

        for g in range(NST):
            load(g, g)
        with s.Fori(1, N // NST) as i:
            for g in range(NST):
                s.wait_ge(st_psum[1], (i * NST + g - NST + 1) * (NTB // 2))
                k.plain(s)
                load(NST * i + g, g)

    def tensor(t):
        t.wait_ge(ready_w, 2)
        t.wait_ge(k.ident16_in, 1)
        for g in range(2):
            t.wait_ge(xt[g], NG // 2 + 1)
        with t.Fori(0, B) as i:
            for g in range(2):
                t.wait_ge(x_in[g], i + 1)
                for z, n in enumerate("qkv"):
                    last = nc.tensor.matmul(bank(3 * g + z), w[n][:, :], k.XT[:, bass.ds(i * S + g * GT, GT)],
                                            start=True, stop=True)
                last.then_inc(qkv_psum[g], 1)
            for g in range(2):
                t.wait_ge(x_in[g], i + 2)
                t.wait_ge(v_done[g], i + 1)
                for n in range(GROUP):
                    last = nc.tensor.transpose(bank(6 + g)[:, n * P:(n + 1) * P], x["v"][g][:, n * P:(n + 1) * P], k.ident[:, :])
                last.then_inc(v_turned[g], 1)
        for g in range(2):
            t.wait_ge(v_done[g], B + 1)

        t.wait_ge(v_split, 1)

        def rows_scores(n, b, half):
            st, h = half // 2, half % 2
            t.wait_ge(s_read[h], n * NTB + st + 1)
            nc.tensor.matmul(bank(h), qs[b][0:KR, st * P:(st + 1) * P], kst[b][0:KR, h * 512:(h + 1) * 512],
                             start=True, stop=True).then_inc(s_psum[h], 1)

        def max_rows(n):
            t.wait_ge(neg_in, n + 1)
            for st in range(NTB):
                last = nc.tensor.matmul(k.psum[MR:ROWS, st // 4, (st % 4) * P:(st % 4 + 1) * P], mp[:, st, :], k.ident16[:, :],
                                        start=True, stop=True)
            last.then_inc(m_turned, 1)

        def values(n, g, tt, between=None):
            c, u = tt % 2, n * (NTB // 2) + tt // 2
            buf = tt % NPT
            t.wait_ge(pt_in[c], u + 2)
            if tt in BY_DVE:
                t.wait_ge(rest_v, n * len(BY_DVE) + BY_DVE.index(tt) + 1)
            if tt in BY_POOL:
                t.wait_ge(rest_p, n * len(BY_POOL) + BY_POOL.index(tt) + 1)
            if tt == 0:
                t.wait_ge(oT_in, n + 1)
            for h in range(2):
                cols = slice(h * 512, (h + 1) * 512)
                if tt in WHOLE:
                    last = nc.tensor.matmul(k.psum[0:V1, 6 + h, :], vh[g][:, tt, :], pt[buf][:, cols], start=False, stop=False,
                                            skip_group_check=True)
                else:
                    lhsT = v3[g][:, tt, :, :].rearrange("p q e -> p (q e)")
                    nc.tensor.matmul(k.psum[0:V3, 6 + h, :], lhsT, upper[buf][:, cols], start=tt == 0, stop=False)
                    last = nc.tensor.matmul(k.psum[0:V3, 6 + h, :], lhsT, prest[buf][:, cols], start=False, stop=tt == NTB - 1)
                if h == 0 and between:
                    between()
            last.then_inc(pv[buf], 1)

        def turn_out(n, g, more=True):
            t.wait_ge(oT_in, n + 2)
            t.wait_ge(s_read[0], (n + 3) * NTB + 1 if more else N * NTB + 1)
            k.plain(t)
            for r in range(NTB):
                src = oT[g][:, :].rearrange("p (a r) -> p r a", r=NTB)[:, r, :] if not blocked else oT[g][:, r * P:(r + 1) * P]
                last = nc.tensor.transpose(bank(0)[:, r * V3:(r + 1) * V3], src, k.ident[0:V3, 0:V3])
            last.then_inc(o_turned, 1)

        def first():
            t.wait_ge(loaded[0], 32)
            for half in range(2 * NTB):
                rows_scores(0, 0, half)
            max_rows(0)

        def body(n, turn, begins=False, more=True):
            (i, g), (used, b), (used_next, b_next) = turn(2), turn(NST), turn(NST, 1)
            done = 0

            def ahead(x, count):
                nonlocal done
                for _ in range(min(count, sum(ROW_HALVES[:x + 1]) - done) if more else 0):
                    rows_scores(n + 1, b_next, done)
                    done += 1

            for x in range(NTB):
                c, u = x % 2, n * (NTB // 2) + x // 2
                if x == 0 and not begins:
                    values(n - 1, 1 - g, x - LAG + NTB)
                if x == 0:
                    t.wait_ge(m_in, n + 1)
                    if more:
                        t.wait_ge(loaded[b_next], used_next * 32 + 32)
                if x == LAG:
                    t.wait_ge(vh_in[g], i + 1)
                t.wait_ge(pt_in[c], u + 1)
                for h in range(2):
                    last = nc.tensor.matmul(bank(2 + 2 * c + h), kst[b][0:ROWS, x * P:(x + 1) * P],
                                            qs[b][0:ROWS, h * 512:(h + 1) * 512], start=True, stop=True)
                last.then_inc(st_psum[c], 1)
                ahead(x, 1)
                if x >= LAG:
                    values(n, g, x - LAG, lambda: ahead(x, 1))
                elif x and not begins:
                    values(n - 1, 1 - g, x - LAG + NTB, lambda: ahead(x, 1))
                ahead(x, 2 * NTB)
                if x == NTB - 3 and not begins:
                    turn_out(n - 1, 1 - g, more)
                if x == NTB - 2 and more:
                    if not begins:
                        t.wait_ge(head_done, n)
                    max_rows(n + 1)

        loop(t, first, body)
        for tt in range(NTB - LAG, NTB):
            values(N - 1, 1, tt)
        t.wait_ge(head_done, N - 1)
        turn_out(N - 1, 1, more=False)
        t.wait_ge(head_done, N)

    def scalar(a):
        with a.Fori(0, B) as i:
            for g in range(2):
                a.wait_ge(qkv_psum[g], i + 1)
                a.wait_ge(v_turned[g], i + 1)
                a.wait_ge(stored[g], i * 192 + 1)
                for z, n in enumerate("qkv"):
                    if blocked:
                        last = nc.scalar.copy(x[n][g][:, :], bank(3 * g + z))
                    else:
                        last = nc.scalar.activation(x[n][g][:, :], bank(3 * g + z), ACT.Identity, bias=bias[:, z:z + 1])
                    last.then_inc(own_a, 1)
                a.wait_ge(own_a, 3)
                a.sem_clear(own_a)
                a.sem_inc(x_in[g], 1)
            for g in range(2):
                a.wait_ge(v_turned[g], i + 2)
                src = bank(6 + g).rearrange("p (n h e) -> p h n e", n=GROUP, h=H)
                dst = vrows[:, bass.ds(i, 1), :, g * GROUP:(g + 1) * GROUP, 0:DV]
                k.plain(a)
                for n in range(GROUP):
                    last = nc.scalar.copy(dst[:, :, :, n, :].rearrange("p o h e -> p (o h) e"), src[:, :, n, :])
                last.then_inc(v_done[g], 1)

        def max_in(n, b):
            a.wait_ge(m_turned, n + 1)
            nc.scalar.copy(qs[b][MR:ROWS, :], k.psum[MR:ROWS, 0:2, :].rearrange("p b s -> p (b s)")).then_inc(m_in, 1)

        def correction(n, g, begins):
            a.wait_ge(corr_in, n + 1)
            if not begins:
                a.wait_ge(corr_used, n)
            nc.scalar.activation(corr[g][:, :], dcorr[g][:, :], ACT.Exp, scale=SCALE).then_inc(corr_exp, 1)

        def take_out(n, g):
            a.wait_ge(*pv_all(n + 1))
            nc.scalar.copy(oT[g][:, :], k.psum[0:V3, 6:8, :].rearrange("p b s -> p (b s)")).then_inc(oT_in, 1)

        def body(n, turn, begins=False, more=True):
            g = turn(2)[1]
            for x in range(NTB):
                c, u = x % 2, n * (NTB // 2) + x // 2
                a.wait_ge(st_psum[c], u + 1)
                a.wait_ge(pv[x % NPT], n * (NTB // NPT) + x // NPT + 1)
                nc.scalar.activation(pt[x % NPT][:, :], k.psum[:, 2 + 2 * c:4 + 2 * c, :].rearrange("p b s -> p (b s)"), ACT.Exp,
                                     scale=SCALE).then_inc(pt_in[c], 1)
                if x == LAG - 1 and not begins:
                    take_out(n - 1, 1 - g)
                if x == NTB - 2 and more:
                    max_in(n + 1, turn(NST, 1)[1])
                if x == NTB // 2 and blocked:
                    correction(n, g, begins)

        loop(a, lambda: max_in(0, 0), body)
        take_out(N - 1, 1)

    own_a = mk("own_a")

    def gpsimd(p):
        c_ = Chain(p, p_own)
        for g in range(NST):
            c_.do(nc.gpsimd.memset(qs[g][:, :], 0.0))
            c_.do(nc.gpsimd.memset(kst[g][:, :], 0.0))
        c_.do(nc.gpsimd.memset(vrows[:, :, :, :, :], 0.0 if blocked else 1.0))
        c_.sync()
        for g in range(NST):
            c_.step(nc.gpsimd.memset(kst[g][MR:ROWS, :], 1.0))
        if blocked:
            for b in range(B):
                c_.step(nc.gpsimd.memset(vrows[P - BLOCK:P, b, :, NTB - 1, DV:V1], 1.0))
        c_.sync()
        c_.restart()
        p.sem_inc(ready_w, 1)
        for g in range(2):
            p.wait_ge(v_done[g], B + 1)

        p.wait_ge(v_split, 1)

        def stage_v(n, g, first=False):
            if not first:
                p.wait_ge(*pv_all(n - 1))
                k.plain(p)
            nc.gpsimd.tensor_copy(vh[g][:, :, :], vrows[:, :, :, :, :].rearrange("p b h n e -> p (b h) n e")[:, bass.ds(n, 1), :, :])
            nc.gpsimd.tensor_copy(v3[g][:, :, :, :].rearrange("p n q e -> p (n q e)"),
                                  vparts[:, bass.ds(n * NTB, NTB), :, :].rearrange("p n q e -> p (n q e)")).then_inc(vh_in[g], 1)

        def body(n, turn, begins=False, more=True):
            for x in BY_POOL:
                p.wait_ge(pt_in[x % 2], n * (NTB // 2) + x // 2 + 2)
                nc.gpsimd.tensor_tensor(prest[x % NPT][:, :], pt[x % NPT][:, :], upper[x % NPT], ALU.subtract).then_inc(rest_p, 1)
            if more:
                stage_v(n + 1, turn(2, 1)[1])

        loop(p, lambda: stage_v(0, 0, first=True), body)

    def vector(v):
        c_ = Chain(v, own)
        v.wait_ge(w_in, 16 * n_w)
        if not blocked:
            c_.do(nc.vector.tensor_reduce(w["v"][:, :], wv_full[:, :, :], AXX, ALU.add))
            c_.do(nc.vector.tensor_reduce(bias[:, 2:3], bv_full[:, :], AXX, ALU.add))
            c_.restart()
        v.sem_inc(ready_w, 1)
        for g in range(2):
            v.wait_ge(xt[g], NG // 2 + 1)
        with v.Fori(0, B) as i:
            for g in range(2):
                v.wait_ge(x_in[g], i + 2)
                v.wait_ge(stored[g], i * 192 + 1)
                for n in "qk":
                    c_.do(nc.vector.tensor_copy(parts[n][g][:, 0, :], x[n][g][:, :]))
                c_.sync()
                for n in "qk":
                    c_.do(nc.vector.tensor_tensor(rest[n][:, :], x[n][g][:, :], parts[n][g][:, 0, :], ALU.subtract))
                c_.sync()
                for n in "qk":
                    c_.do(nc.vector.tensor_copy(parts[n][g][:, 1, :], rest[n][:, :]))
                c_.sync()
                for n in "qk":
                    c_.do(nc.vector.tensor_tensor(parts[n][g][:, 2, :], rest[n][:, :], parts[n][g][:, 1, :], ALU.subtract))
                c_.sync()
                v.sem_inc(split[g], 1)
            c_.restart()
        for g in range(2):
            v.wait_ge(v_done[g], B + 1)
        v.wait_ge(ready_w, 2)
        vv = vrows[:, :, :, :, :].rearrange("p b h n e -> p (b h n) e")
        c_.step(nc.vector.tensor_copy(vparts[:, :, 0, :], vv))
        c_.step(nc.vector.tensor_tensor(vrest[:, :, :], vv, vparts[:, :, 0, :], ALU.subtract))
        c_.step(nc.vector.tensor_copy(vparts[:, :, 1, :], vrest[:, :, :]))
        c_.step(nc.vector.tensor_tensor(vparts[:, :, 2, :], vrest[:, :, :], vparts[:, :, 1, :], ALU.subtract))
        v.sem_inc(v_split, 1)
        c_.restart()

        def row_max(n, g, half):
            st, h = half // 2, half % 2
            v.wait_ge(s_psum[h], n * NTB + st + 1)
            if blocked and h == 1:
                c_.do(nc.vector.tensor_reduce(mx[g][:, st, 1:2], bank(1)[:, 0:512 - BLOCK], AXX, ALU.max))
                ins = nc.vector.tensor_reduce(mx[g][:, st, 2:3], bank(1)[:, 512 - BLOCK:512], AXX, ALU.max)
            else:
                ins = nc.vector.tensor_reduce(mx[g][:, st, h:h + 1], bank(h), AXX, ALU.max)
            ins.then_inc(s_read[h], 1)

        def negate(n, g):
            for h in range(2):
                v.wait_ge(s_read[h], (n + 1) * NTB + 1)
            c_.sync()
            prev, mm, r1 = m1[:, 0, :], m1[:, 1, :], m1[:, 2, :]
            c_.step(nc.vector.tensor_tensor(prev, mx[g][:, :, 0], mx[g][:, :, 1], ALU.max))
            if blocked:
                c_.step(nc.vector.tensor_tensor(mm, prev, mx[g][:, :, 2], ALU.max))
                nc.vector.tensor_tensor(dcorr[g][:, :], prev, mm, ALU.subtract).then_inc(corr_in, 1)
            else:
                mm = prev
            neg = m1[:, 3, :]
            c_.step(nc.vector.tensor_scalar(neg, mm, -1.0, LIFT / SCALE, ALU.mult, ALU.add))
            c_.step(nc.vector.tensor_copy(mp[:, :, 0], neg))
            c_.step(nc.vector.tensor_tensor(r1, neg, mp[:, :, 0], ALU.subtract))
            c_.step(nc.vector.tensor_copy(mp[:, :, 1], r1))
            nc.vector.tensor_tensor(mp[:, :, 2], r1, mp[:, :, 1], ALU.subtract).then_inc(neg_in, 1)
            c_.restart()

        def first():
            for half in range(2 * NTB):
                row_max(0, 0, half)
            negate(0, 0)

        def finish(n, g):
            v.wait_ge(o_turned, n + 1)
            k.plain(v)
            c_.step(nc.vector.tensor_reduce(osum[:, :, :], bank(0)[:, 0:NTB * V3].rearrange("p (r q e) -> p r e q", q=3, e=V1), AXX, ALU.add))
            v.sem_inc(head_done, 1)
            if blocked:
                v.wait_ge(corr_exp, n + 1)
                c_.step(nc.vector.scalar_tensor_tensor(den[:, :], corr[g][:, :], 1.0, osum[:, :, DV], ALU.add, ALU.mult))
                v.sem_inc(corr_used, 1)
                c_.step(nc.vector.reciprocal(den[:, :], den[:, :]))
                c_.step(nc.vector.tensor_tensor(O[:, bass.ds(n * (NTB * DV), NTB * DV)].rearrange("p (r e) -> p r e", e=DV),
                                                osum[:, :, 0:DV], den[:, :].unsqueeze(2).to_broadcast([P, NTB, DV]), ALU.mult))
            else:
                c_.step(nc.vector.reciprocal(den[:, :], osum[:, :, DV]))
                c_.step(nc.vector.tensor_tensor(onorm[:, :, :], osum[:, :, 0:DV], den[:, :].unsqueeze(2).to_broadcast([P, NTB, DV]), ALU.mult))
                xs = k.X[:, bass.ds(n, 1), :].rearrange("p n d -> p (n d)")
                c_.step(nc.vector.tensor_tensor(xs, xs, onorm[:, :, :].rearrange("p r e -> p (r e)"), ALU.add))
            c_.restart()

        def take_rest(n, x):
            v.wait_ge(pt_in[x % 2], n * (NTB // 2) + x // 2 + 2)
            nc.vector.tensor_tensor(prest[x % NPT][:, :], pt[x % NPT][:, :], upper[x % NPT], ALU.subtract).then_inc(rest_v, 1)

        def body(n, turn, begins=False, more=True):
            done, g = 0, turn(2)[1]
            for x in range(NTB):
                if x == 0 and not begins and NTB - 1 in BY_DVE:
                    take_rest(n - 1, NTB - 1)
                if more:
                    for _ in range(ROW_HALVES[x]):
                        row_max(n + 1, 1 - g, done)
                        done += 1
                if x - 1 in BY_DVE:
                    take_rest(n, x - 1)
                if x == NTB - 3 and more:
                    v.wait_ge(m_turned, n + 1)
                    if blocked and not begins:
                        v.wait_ge(corr_exp, n)
                    negate(n + 1, 1 - g)
                if x == NTB - 3 and not begins:
                    finish(n - 1, 1 - g)

        loop(v, first, body)
        take_rest(N - 1, NTB - 1)
        finish(N - 1, 1)
        if blocked:
            v.sem_inc(all_done, 1)
        else:
            nc.vector.tensor_copy(den[:, 0:1], den[:, 0:1]).then_inc(k.layer_done, 1)

    k.add(sync=sync, vector=vector, scalar=scalar, tensor=tensor, gpsimd=gpsimd)
    if blocked:
        project_out(k, tag, O, H, HD, all_done, 1)


def project_out(k, tag, O, H, HD, head_done, N):
    nc, d, ctx = k.nc, k.dram, k.layer_ctx
    NTB = S // P
    ow = k.sb(f"{tag}_ow", [P, D], ctx=ctx)
    ob = k.sb(f"{tag}_ob", [1, GT], ctx=ctx)
    stage = [k.sb(f"{tag}_ostage{g}", [P, GROUP, D], ctx=ctx) for g in range(2)]
    oT = [k.sb(f"{tag}_ooT{g}", [P, GT], ctx=ctx) for g in range(2)]
    w_in = k.sem(f"{tag}_ow_in")
    staged, oT_in, outp = ([k.sem(f"{tag}_{n}{g}") for g in range(2)] for n in ("ostaged", "ooT_in", "ooutp"))
    turned, added = ([k.free_sem(f"{tag}_{n}{g}") for g in range(2)] for n in ("oturned", "oadded"))
    Ov = O[:, :].rearrange("p (b h n e) -> p b n h e", b=B, h=H, n=NTB)

    def sync(s):
        s.dma_start(ow[:, :], d[f"{tag}_ow"]).then_inc(w_in, 16)
        s.dma_start(ob[:, :], d[f"{tag}_ob"]).then_inc(w_in, 16)

    def gpsimd(p):
        p.wait_ge(head_done, N)
        with p.Fori(0, B) as i:
            for g in range(2):
                p.wait_ge(turned[g], i + 1)
                k.plain(p)
                for n in range(GROUP):
                    last = nc.gpsimd.tensor_copy(stage[g][:, n, :].rearrange("p (h e) -> p h e", h=H),
                                                 Ov[:, bass.ds(i, 1), g * GROUP + n, :, :].rearrange("p b h e -> p (b h) e"))
                last.then_inc(staged[g], 1)

    def tensor(t):
        t.wait_ge(w_in, 32)
        with t.Fori(0, B) as i:
            for g in range(2):
                t.wait_ge(staged[g], i + 1)
                for n in range(GROUP):
                    last = nc.tensor.transpose(k.psum[:, g, n * P:(n + 1) * P], stage[g][:, n, :], k.ident[:, :])
                last.then_inc(turned[g], 1)
                t.wait_ge(oT_in[g], i + 1)
                t.wait_ge(added[g], i + 1)
                nc.tensor.matmul(k.psum[:, 2 + g, :], k.ones_row[:, :], ob[:, :], start=True, stop=True)
                for n in range(GROUP):
                    last = nc.tensor.matmul(k.psum[:, 2 + g, n * D:(n + 1) * D], oT[g][:, n * P:(n + 1) * P], ow[:, :],
                                            start=False, stop=True, skip_group_check=True)
                last.then_inc(outp[g], 1)

    def scalar(a):
        with a.Fori(0, B) as i:
            for g in range(2):
                a.wait_ge(turned[g], i + 2)
                nc.scalar.copy(oT[g][:, :], k.psum[:, g, :]).then_inc(oT_in[g], 1)

    def vector(v):
        with v.Fori(0, B) as i:
            for g in range(2):
                v.wait_ge(outp[g], i + 1)
                xs = k.X[:, bass.ds(i * 2 * GROUP + g * GROUP, GROUP), :]
                nc.vector.tensor_tensor(xs, xs, k.psum[:, 2 + g, :].rearrange("p (n d) -> p n d", d=D), ALU.add).then_inc(added[g], 1)
        for g in range(2):
            v.wait_ge(added[g], B + 1)
        nc.vector.memset(oT[0][0:1, 0:1], 0.0).then_inc(k.layer_done, 1)

    k.add(sync=sync, vector=vector, scalar=scalar, tensor=tensor, gpsimd=gpsimd)


def routed_ffn(k):
    nc, d, ctx = k.nc, k.dram, k.layer_ctx
    E, _, HID = d["L3_ffn_w1"].shape
    G, KEEP, K = 4, 2, 2
    PAIR = NT * K
    sw1, sw2, sw3 = (k.sb(f"rf_sw{n}", [P, D], ctx=ctx) for n in (1, 2, 3))
    gw = k.sb("rf_gw", [P, E], ctx=ctx)
    eb = k.sb("rf_eb", [P, E], ctx=ctx)
    w13 = k.sb("rf_w13", [P, E, 2 * HID], ctx=ctx)
    w2 = k.sb("rf_w2", [HID, E, D], ctx=ctx)
    consts = k.sb("rf_consts", [P, G * G + E * E + PAIR + E * K * E + 2 + P], ctx=ctx)
    o0 = 0
    def const(n):
        nonlocal o0
        o0 += n
        return consts[:, o0 - n:o0]
    tri4, tri8, pos, delta, half, ones = const(G * G), const(E * E), const(PAIR), const(E * K * E), const(2), const(P)
    assert o0 == consts.shape[1], o0
    stage = [k.sb(f"rf_stage{g}", [P, GT], ctx=ctx) for g in range(2)]
    sg = [k.sb(f"rf_sg{g}", [P, GT], ctx=ctx) for g in range(2)]
    g1 = [k.sb(f"rf_g1{g}", [P, GT], ctx=ctx) for g in range(2)]
    uT = [k.sb(f"rf_uT{g}", [P, GT], ctx=ctx) for g in range(2)]
    lg, pr, sc = (k.sb(f"rf_{n}", [P, NT, E], ctx=ctx) for n in ("lg", "pr", "sc"))
    m = k.sb("rf_m", [P, NT], ctx=ctx)
    gs, gc, keep = (k.sb(f"rf_{n}", [P, NT, G], ctx=ctx) for n in ("gs", "gc", "keep"))
    gg, ge = (k.sb(f"rf_{n}", [P, NT, G, G], ctx=ctx) for n in ("gg", "ge"))
    ee, eq = (k.sb(f"rf_{n}", [P, NT, E, E], ctx=ctx) for n in ("ee", "eq"))
    cnt, keep8 = (k.sb(f"rf_{n}", [P, NT, E], ctx=ctx) for n in ("cnt", "keep8"))
    oh = k.sb("rf_oh", [P, NT, K, E], ctx=ctx)
    ohp = k.sb("rf_ohp", [P, NT, K, E], ctx=ctx)
    wts = k.sb("rf_wts", [P, NT, K], ctx=ctx)
    sel = k.sb("rf_sel", [P, NT, E], ctx=ctx)
    local = k.sb("rf_local", [P, E], ctx=ctx)
    offs = k.sb("rf_offs", [P, E], ctx=ctx)
    gx = k.sb("rf_gx", [P, PAIR, E + 1], ctx=ctx)
    ghot = k.sb("rf_ghot", [P, PAIR, E], ctx=ctx)
    spots = k.sb("rf_spots", [P, NT, K, E, E], ctx=ctx)
    xg = k.sb("rf_xg", [P, E, K * E, E], ctx=ctx)
    table = k.sb("rf_table", [P, K, 2 * HID], ctx=ctx)
    zero = k.sb("rf_zero", [P, P], ctx=ctx)
    ost = [k.sb(f"rf_ost{g}", [P, GROUP, P], ctx=ctx) for g in range(2)]
    oht = [k.sb(f"rf_oht{g}", [P, GT], ctx=ctx) for g in range(2)]
    wst = [k.sb(f"rf_wst{g}", [P, GROUP * K], ctx=ctx) for g in range(2)]
    wa = [k.sb(f"rf_wa{g}", [P, GROUP * K, 2 * HID], ctx=ctx) for g in range(2)]
    sh = [k.sb(f"rf_sh{g}", [P, GROUP * K, HID], ctx=ctx) for g in range(2)]
    th = [k.sb(f"rf_th{g}", [P, GROUP * K, HID], ctx=ctx) for g in range(2)]
    hh = [k.sb(f"rf_hh{g}", [P, GROUP * K, HID], ctx=ctx) for g in range(2)]
    hs = k.sb("rf_hs", [P, 2, HID], ctx=ctx)
    ht = k.sb("rf_ht", [HID, 2, E * E], ctx=ctx)
    pair = lambda n, free=False: [(k.free_sem if free else k.sem)(f"rf_{n}{g}") for g in range(2)]
    one = lambda n: k.sem(f"rf_{n}")
    w_in, own, p_own, centred, exped, counted, counts, xg_in, table_ps, table_in, routed, zeroed, folded, hs_in, ht_ps, ht_in, last_ps = map(
        one, ("w_in", "own", "p_own", "centred", "exped", "counted", "counts", "xg_in", "table_ps", "table_in", "routed",
              "zeroed", "folded", "hs_in", "ht_ps", "ht_in", "last_ps"))
    staged, hid, sig, u_in, outp = pair("staged"), pair("hid"), pair("sig"), pair("u_in", True), pair("outp", True)
    gated, taken, added = pair("gated", True), pair("taken", True), pair("added", True)
    spot_in, spot_t, oht_in, looked = pair("spot_in"), pair("spot_t"), pair("oht_in"), pair("looked")
    scaled, sig2, h_in, fold, th_in = pair("scaled", True), pair("sig2"), pair("h_in"), pair("fold", True), pair("th_in")
    layer = k.layers
    xt = layer_norm(k, "rf")
    bank = lambda n: k.psum[:, n, :]

    def sync(s):
        if layer:
            s.wait_ge(k.layer_done, layer)
        for dst, src in ((sw1, "rf_sw1"), (sw2, "rf_sw2"), (sw3, "rf_sw3"), (gw, "rf_gw"), (eb, "rf_eb"), (consts, "rf_consts")):
            s.dma_start(dst[:, :], d[src]).then_inc(w_in, 16)
        s.dma_start(w13[:, :, :], d["rf_w13"]).then_inc(w_in, 16)
        s.dma_start(w2[:, :, :], d["rf_w2"]).then_inc(w_in, 16)

    def gpsimd(p):
        c = Chain(p, p_own)
        for g in range(2):
            p.wait_ge(xt[g], NG // 2 + 1)
        with p.Fori(0, NG // 2) as i:
            for g in range(2):
                p.wait_ge(gated[g], i + 1)
                k.plain(p)
                nc.gpsimd.tensor_copy(stage[g][:, :], k.XT[:, bass.ds(i * 2 * GT + g * GT, GT)]).then_inc(staged[g], 1)
        nc.gpsimd.memset(zero[:, :], 0.0).then_inc(zeroed, 1)
        p.wait_ge(routed, 1)
        with p.Fori(0, NG // 2) as i:
            for g in range(2):
                p.wait_ge(fold[g], i + 1)
                p.wait_ge(scaled[g], i + 1)
                k.plain(p)
                at = bass.ds(i * 2 * GROUP + g * GROUP, GROUP)
                nc.gpsimd.tensor_copy(ost[g][:, :, :], spots[:, at, :, :, :].rearrange("p n q g e -> p n (q g e)"))
                nc.gpsimd.tensor_copy(wst[g][:, :], wts[:, at, :].rearrange("p n q -> p (n q)")).then_inc(spot_in[g], 1)
            for g in range(2):
                p.wait_ge(sig2[g], i + 1)
                c.step(nc.gpsimd.tensor_tensor(th[g][:, :, :], wa[g][:, :, 0:HID], sh[g][:, :, :], ALU.mult))
                nc.gpsimd.tensor_tensor(hh[g][:, :, :], th[g][:, :, :], wa[g][:, :, HID:2 * HID], ALU.mult).then_inc(h_in[g], 1)
            c.restart()

    def tensor(t):
        t.wait_ge(w_in, 128)
        for g in range(2):
            t.wait_ge(xt[g], NG // 2 + 1)
        with t.Fori(0, NG // 2) as i:
            for g in range(2):
                t.wait_ge(u_in[g], i + 1)
                x = k.XT[:, bass.ds(i * 2 * GT + g * GT, GT)]
                nc.tensor.matmul(bank(2 * g), sw1[:, :], x, start=True, stop=True)
                nc.tensor.matmul(bank(2 * g + 1), sw3[:, :], x, start=True, stop=True).then_inc(hid[g], 1)
            for g in range(2):
                t.wait_ge(staged[g], i + 1)
                t.wait_ge(taken[g], i + 1)
                for n in range(GROUP):
                    last = nc.tensor.matmul(bank(4 + g)[:, n * E:(n + 1) * E], stage[g][:, n * P:(n + 1) * P], gw[:, :],
                                            start=True, stop=True)
                last.then_inc(gated[g], 1)
            for g in range(2):
                t.wait_ge(u_in[g], i + 2)
                t.wait_ge(added[g], i + 1)
                for n in range(GROUP):
                    last = nc.tensor.matmul(bank(6 + g)[:, n * D:(n + 1) * D], uT[g][:, n * P:(n + 1) * P], sw2[:, :],
                                            start=True, stop=True)
                last.then_inc(outp[g], 1)
        t.wait_ge(xg_in, 1)
        for g in range(2):
            t.wait_ge(u_in[g], NG // 2 + 1)
            t.wait_ge(taken[g], NG // 2 + 1)
            t.wait_ge(added[g], NG // 2 + 1)
        for e in range(E):
            last = nc.tensor.matmul(bank(0)[:, 0:2 * HID], xg[:, e, :, :].rearrange("p q e -> p (q e)"), w13[:, e, :],
                                    start=e == 0, stop=e == E - 1)
        last.then_inc(table_ps, 1)
        t.wait_ge(counted, 1)
        nc.tensor.matmul(bank(1)[:, 0:E], ones, local[:, :], start=True, stop=True).then_inc(counts, 1)
        t.wait_ge(zeroed, 1)
        nc.tensor.matmul(bank(7)[:, 0:P], zero[:, :], zero[:, :], start=True, stop=True)
        t.wait_ge(table_in, 1)
        t.wait_ge(routed, 1)
        with t.Fori(0, NG // 2) as i:
            for g in range(2):
                t.wait_ge(spot_in[g], i + 1)
                for n in range(GROUP):
                    last = nc.tensor.transpose(bank(5 + g)[:, n * P:(n + 1) * P], ost[g][:, n, :], k.ident[:, :])
                last.then_inc(spot_t[g], 1)
            for g in range(2):
                t.wait_ge(oht_in[g], i + 1)
                t.wait_ge(scaled[g], i + 1)
                for n in range(GROUP):
                    last = nc.tensor.matmul(k.psum[:, 2 * g + n // 2, (n % 2) * 2 * P:(n % 2 + 1) * 2 * P],
                                            oht[g][:, n * P:(n + 1) * P], table[:, :, :].rearrange("p q h -> p (q h)"),
                                            start=True, stop=True)
                last.then_inc(looked[g], 1)
            for g in range(2):
                t.wait_ge(h_in[g], i + 1)
                for n in range(GROUP):
                    last = nc.tensor.matmul(bank(7)[:, 0:P], ost[g][:, n, :], hh[g][:, n * K:(n + 1) * K, :].rearrange("p q h -> p (q h)"),
                                            start=False, stop=True, skip_group_check=True)
                last.then_inc(fold[g], 1)
        t.wait_ge(fold[0], NG // 2 + 1)
        t.wait_ge(fold[1], NG // 2 + 1)
        t.sem_inc(folded, 1)
        t.wait_ge(hs_in, 1)
        nc.tensor.transpose(k.psum[0:HID, 0, 0:P], hs[:, 0, :], k.ident[:, :]).then_inc(ht_ps, 1)
        t.wait_ge(ht_in, 1)
        for e in range(E):
            last = nc.tensor.matmul(k.psum[0:E, 1, 0:D], ht[:, 0, e * E:(e + 1) * E], w2[:, e, :], start=e == 0, stop=e == E - 1)
        last.then_inc(last_ps, 1)

    def scalar(a):
        with a.Fori(0, NG // 2) as i:
            for g in range(2):
                a.wait_ge(hid[g], i + 1)
                nc.scalar.activation(sg[g][:, :], bank(2 * g), ACT.Sigmoid).then_inc(sig[g], 1)
        a.wait_ge(centred, 1)
        nc.scalar.activation(pr[:, :, :], lg[:, :, :], ACT.Exp).then_inc(exped, 1)
        with a.Fori(0, NG // 2) as i:
            for g in range(2):
                a.wait_ge(spot_t[g], i + 1)
                nc.scalar.copy(oht[g][:, :], bank(5 + g)).then_inc(oht_in[g], 1)
            for g in range(2):
                a.wait_ge(scaled[g], i + 2)
                nc.scalar.activation(sh[g][:, :, :], wa[g][:, :, 0:HID], ACT.Sigmoid).then_inc(sig2[g], 1)

    def vector(v):
        c = Chain(v, own)
        V = nc.vector
        with v.Fori(0, NG // 2) as i:
            for g in range(2):
                v.wait_ge(sig[g], i + 1)
                c.step(V.tensor_tensor(g1[g][:, :], bank(2 * g), sg[g][:, :], ALU.mult))
                c.step(V.tensor_tensor(uT[g][:, :], bank(2 * g + 1), g1[g][:, :], ALU.mult))
                v.sem_inc(u_in[g], 1)
            for g in range(2):
                v.wait_ge(gated[g], i + 2)
                V.tensor_copy(lg[:, bass.ds(i * 2 * GROUP + g * GROUP, GROUP), :],
                              bank(4 + g)[:, 0:GROUP * E].rearrange("p (n e) -> p n e", e=E)).then_inc(taken[g], 1)
            for g in range(2):
                v.wait_ge(outp[g], i + 2)
                xs = k.X[:, bass.ds(i * 2 * GROUP + g * GROUP, GROUP), :]
                V.tensor_tensor(xs, xs, bank(6 + g).rearrange("p (n d) -> p n d", d=D), ALU.add).then_inc(added[g], 1)
            c.restart()
        for g in range(2):
            v.wait_ge(taken[g], NG // 2 + 1)
            v.wait_ge(added[g], NG // 2 + 1)
        v.wait_ge(w_in, 128)
        V.tensor_tensor(xg[:, :, :, :].rearrange("p g q e -> p (g q) e"), k.XT[:, 0:E].unsqueeze(1).to_broadcast([P, E * K * E, E]),
                        delta.unsqueeze(2).to_broadcast([P, E * K * E, E]), ALU.mult).then_inc(xg_in, 1)
        wide = lambda x: x.unsqueeze(2).to_broadcast([P, NT, E])
        c.step(V.tensor_reduce(m[:, :], lg[:, :, :], AXX, ALU.max))
        V.tensor_tensor(lg[:, :, :], lg[:, :, :], wide(m[:, :]), ALU.subtract).then_inc(centred, 1)
        v.wait_ge(exped, 1)
        c.step(V.tensor_reduce(m[:, :], pr[:, :, :], AXX, ALU.add))
        c.step(V.reciprocal(m[:, :], m[:, :]))
        c.step(V.tensor_tensor(pr[:, :, :], pr[:, :, :], wide(m[:, :]), ALU.mult))
        c.step(V.tensor_tensor(sc[:, :, :], pr[:, :, :], eb[:, :].unsqueeze(1).to_broadcast([P, NT, E]), ALU.add))
        s2 = sc[:, :, :].rearrange("p n (g e) -> p n g e", g=G)
        c.step(V.tensor_tensor(gs[:, :, :], s2[:, :, :, 0], s2[:, :, :, 1], ALU.add))
        other = gs[:, :, :].unsqueeze(2).to_broadcast([P, NT, G, G])
        this = gs[:, :, :].unsqueeze(3).to_broadcast([P, NT, G, G])
        c.do(V.tensor_tensor(gg[:, :, :, :], other, this, ALU.is_gt))
        c.do(V.tensor_tensor(ge[:, :, :, :], other, this, ALU.is_equal))
        c.sync()
        flat = lambda x: x[:, :, :, :].rearrange("p n a b -> p n (a b)")
        c.step(V.tensor_tensor(flat(ge), flat(ge), tri4.unsqueeze(1).to_broadcast([P, NT, G * G]), ALU.mult))
        c.step(V.tensor_tensor(flat(gg), flat(gg), flat(ge), ALU.add))
        c.step(V.tensor_reduce(gc[:, :, :], gg[:, :, :, :], AXX, ALU.add))
        c.step(V.tensor_scalar(keep[:, :, :], gc[:, :, :], float(KEEP), None, ALU.is_lt))
        c.step(V.tensor_copy(keep8[:, :, :].rearrange("p n (g e) -> p n g e", g=G), keep[:, :, :].unsqueeze(3).to_broadcast([P, NT, G, E // G])))
        other = sc[:, :, :].unsqueeze(2).to_broadcast([P, NT, E, E])
        this = sc[:, :, :].unsqueeze(3).to_broadcast([P, NT, E, E])
        c.do(V.tensor_tensor(ee[:, :, :, :], other, this, ALU.is_gt))
        c.do(V.tensor_tensor(eq[:, :, :, :], other, this, ALU.is_equal))
        c.sync()
        c.step(V.tensor_tensor(flat(eq), flat(eq), tri8.unsqueeze(1).to_broadcast([P, NT, E * E]), ALU.mult))
        c.step(V.tensor_tensor(flat(ee), flat(ee), flat(eq), ALU.add))
        c.step(V.tensor_tensor(ee[:, :, :, :], ee[:, :, :, :], keep8[:, :, :].unsqueeze(2).to_broadcast([P, NT, E, E]), ALU.mult))
        c.step(V.tensor_reduce(cnt[:, :, :], ee[:, :, :, :], AXX, ALU.add))
        for q in range(K):
            c.do(V.scalar_tensor_tensor(oh[:, :, q, :], cnt[:, :, :], float(q), keep8[:, :, :], ALU.is_equal, ALU.mult))
        c.sync()
        for q in range(K):
            c.do(V.tensor_tensor(ohp[:, :, q, :], oh[:, :, q, :], pr[:, :, :], ALU.mult))
        c.step(V.tensor_tensor(sel[:, :, :], oh[:, :, 0, :], oh[:, :, 1, :], ALU.add))
        c.step(V.tensor_reduce(wts[:, :, :], ohp[:, :, :, :], AXX, ALU.add))
        V.tensor_reduce(local[:, :], sel[:, :, :].rearrange("p n e -> p e n"), AXX, ALU.add).then_inc(counted, 1)
        v.wait_ge(table_ps, 1)
        for q in range(K):
            last = V.tensor_scalar(table[:, q, :], bank(0)[:, 0:2 * HID], half[:, q:q + 1], None, ALU.mult)
            last.then_inc(own, 1)
            c.n += 1
        c.sync()
        v.sem_inc(table_in, 1)
        v.wait_ge(counts, 1)
        c.step(V.tensor_copy(offs[:, :], bank(1)[:, 0:E]))
        for e in range(1, E):
            c.step(V.tensor_tensor(offs[:, e:e + 1], offs[:, e - 1:e], offs[:, e:e + 1], ALU.add))
        c.do(V.memset(gx[:, :, 0:1], 1.0))
        c.do(V.tensor_tensor(gx[:, :, 1:E + 1], pos.unsqueeze(2).to_broadcast([P, PAIR, E]),
                             offs[:, :].unsqueeze(1).to_broadcast([P, PAIR, E]), ALU.is_ge))
        c.sync()
        c.step(V.tensor_tensor(ghot[:, :, :], gx[:, :, 0:E], gx[:, :, 1:E + 1], ALU.subtract))
        c.step(V.tensor_tensor(spots[:, :, :, :, :].rearrange("p n q g e -> p (n q) g e"), ghot[:, :, :].unsqueeze(3).to_broadcast([P, PAIR, E, E]),
                               oh[:, :, :, :].rearrange("p n q e -> p (n q) e").unsqueeze(2).to_broadcast([P, PAIR, E, E]), ALU.mult))
        v.sem_inc(routed, 1)
        c.restart()
        with v.Fori(0, NG // 2) as i:
            for g in range(2):
                v.wait_ge(looked[g], i + 1)
                V.tensor_tensor(wa[g][:, :, :], k.psum[:, 2 * g:2 * g + 2, :].rearrange("p b (q h) -> p (b q) h", h=2 * HID),
                                wst[g][:, :].unsqueeze(2).to_broadcast([P, GROUP * K, 2 * HID]), ALU.mult).then_inc(scaled[g], 1)
        v.wait_ge(folded, 1)
        c.step(V.tensor_scalar(hs[:, 1, :], bank(7)[:, 0:HID], half[:, 0:1], None, ALU.mult))
        V.scalar_tensor_tensor(hs[:, 0, :], bank(7)[:, HID:2 * HID], half[:, 1:2], hs[:, 1, :], ALU.mult, ALU.add).then_inc(hs_in, 1)
        v.wait_ge(ht_ps, 1)
        c.step(V.tensor_copy(ht[:, 1, :], k.psum[0:HID, 0, 0:E * E]))
        V.tensor_tensor(ht[:, 0, :], k.psum[0:HID, 0, E * E:K * E * E], ht[:, 1, :], ALU.add).then_inc(ht_in, 1)
        v.wait_ge(last_ps, 1)
        c.step(V.tensor_tensor(k.X[0:E, 0, :], k.X[0:E, 0, :], k.psum[0:E, 1, 0:D], ALU.add))
        V.memset(m[:, 0:1], 0.0).then_inc(k.layer_done, 1)

    k.add(sync=sync, vector=vector, scalar=scalar, tensor=tensor, gpsimd=gpsimd)


BUILDERS = {7: routed_ffn, 4: lambda k: attention(k, "sa", 8, 16, False), 6: lambda k: attention(k, "ba", 16, 8, True),
            2: test_time_mlp, 3: dense_experts, 5: channel_mix, 0: delta_net, 1: sine_ffn}


def build(nc, dram, out):
    with ExitStack() as ctx:
        k = Core(nc, ctx, dram)
        stored = k.sem("stored")

        def halves(g):
            g.wait_ge(k.consts_in, 64)
            nc.gpsimd.tensor_copy(k.ident16[:, :], k.ident[:, :]).then_inc(k.ident16_in, 1)

        k.add(gpsimd=halves)

        def load(s):
            s.dma_start(k.mhalf[:, :], dram["mhalf"]).then_inc(k.consts_in, 16)
            s.dma_start(k.X[:, :, :], dram["L0_attn_x"].rearrange("b (t p) d -> p (b t) d", p=P)).then_inc(k.consts_in, 16)
            s.dma_start(k.ident[:, :], dram["ident"]).then_inc(k.consts_in, 16)
            s.dma_start(k.ones_row[:, :], dram["ones_row"]).then_inc(k.consts_in, 16)

        k.add(sync=load)
        arrived, opened = {e: k.sem(f"arrived_{e}") for e in k.programs}, k.sem("opened")
        kept = []
        contexts = {}

        def turn_over(s, n):
            if n:
                for e in k.programs:
                    s.wait_ge(arrived[e], n)
                s.wait_ge(k.layer_done, n)
                for x in kept[n - 1][0]:
                    s.sem_clear(x)
            for m in (n + 1,) if n else (0, 1):
                if m < len(kept):
                    for f in kept[m][1]:
                        s.sem_inc(f, 1)
                    s.sem_inc(opened, 1)

        for n, which in enumerate(LAYERS):
            if n >= 2:
                contexts[n - 2].close()
            k.sem_ctx = contexts[n] = ExitStack()
            k.layer_sems, k.free = [], []
            for e in k.programs:
                if e == "sync":
                    k.programs[e].append(lambda s, n=n: turn_over(s, n))
                k.programs[e].append(lambda eng, n=n: eng.wait_ge(opened, n + 1))
            with ExitStack() as layer_ctx:
                k.layer_ctx = layer_ctx
                BUILDERS[which](k)
                k.layers += 1
            kept.append((k.layer_sems, k.free))
            for e in k.programs:
                k.programs[e].append(lambda eng, e=e: eng.sem_inc(arrived[e], 1))
        n_layers = k.layers

        def store(s):
            s.wait_ge(k.layer_done, n_layers)
            s.dma_start(out.rearrange("b (t p) d -> p (b t) d", p=P), k.X[:, :, :]).then_inc(stored, 16)
            s.wait_ge(stored, 16)

        k.add(sync=store)
        block = ctx.enter_context(nc.Block())

        @block.sync
        def _(s):
            for f in k.programs["sync"]:
                f(s)

        @block.tensor
        def _(t):
            for f in k.programs["tensor"]:
                f(t)

        @block.scalar
        def _(a):
            for f in k.programs["scalar"]:
                f(a)

        @block.vector
        def _(v):
            for f in k.programs["vector"]:
                f(v)

        @block.gpsimd
        def _(g):
            for f in k.programs["gpsimd"]:
                f(g)


def lay_out(inputs):
    f = np.float32
    a = {n: np.ascontiguousarray(v) for n, v in inputs.items()}
    a["mhalf"] = np.full((P, P), -0.5, f)
    a["ident"] = np.eye(P, dtype=f)
    a["ones_row"] = np.ones((1, P), f)
    col = lambda n: a[n].reshape(-1, P).T
    a["sf_cols"] = np.ascontiguousarray(np.stack([col("L0_ffn_b1"), col("L0_ffn_quantum_phases"),
                                                  col("L0_ffn_quantum_weights_real"), col("L0_ffn_quantum_weights_imag")], 1))
    a["sf_b2"] = np.tile(a["L0_ffn_b2"], GROUP)[None]
    H, R, HD = 8, 4, 16
    rep = lambda w: np.repeat(w, R, axis=-1)
    for n in ("k", "q"):
        w = a[f"L0_attn_W{n}"].reshape(D, H, HD).transpose(0, 2, 1)
        a[f"dn_w{n}"] = np.ascontiguousarray(rep(w))
    a["dn_wv"] = np.ascontiguousarray(a["L0_attn_Wv"].reshape(D, H * R, HD // R).transpose(0, 2, 1))
    a["dn_wb"] = np.ascontiguousarray(rep(a["L0_attn_Wb"]))
    a["dn_lnw"] = np.tile(a["L0_attn_ln_w"], (P, 1))
    a["dn_lnb"] = np.tile(a["L0_attn_ln_b"], (P, 1))
    for n in ("r", "k", "v"):
        a[f"cm_w{n}"] = np.ascontiguousarray(a[f"L2_ffn_W_{n}"].T)
    a["cm_mu"] = np.ascontiguousarray(np.stack([a["L2_ffn_mu_r"], a["L2_ffn_mu_k"]], 1))
    a["de_gb"] = np.tile(a["L1_ffn_gate_b"], GROUP)[None]
    a["de_ew"] = np.ascontiguousarray(a["L1_ffn_expert_w"].transpose(1, 0, 2).reshape(D, -1))
    b = lambda n: a[n][:, None]
    a["tt_w0"] = np.concatenate([a["L1_attn_W1"], a["L1_attn_W2"], a["L1_attn_W2"].T, b("L1_attn_b1"), b("L1_attn_b2")], 1)
    step = np.arange(P) % (P // B)
    a["tt_earlier"] = (step[:, None] < step[None, :]).astype(f)
    a["tt_ones"] = np.ones((P, 1), f)
    a["sa_wq"], a["sa_wk"] = a["L2_attn_Wq"], a["L2_attn_Wk"]
    a["sa_bias"] = np.ascontiguousarray(np.stack([a["L2_attn_bq"], a["L2_attn_bk"]], 1))
    a["sa_gamma_beta"] = np.ascontiguousarray(np.stack([a["L2_attn_gamma"], a["L2_attn_beta"]], 1))
    for n in "qkv":
        a[f"ba_w{n}"] = np.ascontiguousarray(a[f"L3_attn_{n}_w"].T)
    a["ba_ow"] = np.ascontiguousarray(a["L3_attn_out_w"].T)
    a["ba_ob"] = np.tile(a["L3_attn_out_b"], GROUP)[None]
    E, G, K = 8, 4, 2
    for n in (1, 2, 3):
        a[f"rf_sw{n}"] = np.ascontiguousarray(a[f"L3_ffn_sw{n}"].T)
    a["rf_gw"] = np.ascontiguousarray(a["L3_ffn_w_gate"].T)
    a["rf_eb"] = np.tile(a["L3_ffn_expert_bias"], (P, 1))
    a["rf_w13"] = np.ascontiguousarray(np.concatenate([a["L3_ffn_w1"], a["L3_ffn_w3"]], 2).transpose(1, 0, 2))
    a["rf_w2"] = np.ascontiguousarray(a["L3_ffn_w2"].transpose(1, 0, 2))
    before = lambda n: np.tile((np.arange(n)[None, :] < np.arange(n)[:, None]).astype(f).reshape(-1), (P, 1))
    pos = K * (np.arange(NT)[None, :, None] * P + np.arange(P)[:, None, None]) + np.arange(K)[None, None, :]
    delta = np.zeros((E, K, E), f)
    delta[np.arange(E), :, np.arange(E)] = 1
    half = np.stack([np.arange(P) < P // 2, np.arange(P) >= P // 2], 1)
    a["rf_consts"] = np.concatenate([before(G), before(E), pos.reshape(P, -1).astype(f), np.tile(delta.reshape(-1), (P, 1)),
                                     half.astype(f), np.ones((P, P), f)], 1)
    return a


def kernel(**inputs):
    import concourse.bacc as bacc
    from concourse.bass_utils import run_bass_kernel_spmd as run

    nc = bacc.Bacc("TRN2", target_bir_lowering=False, num_devices=1)
    arrays = lay_out(inputs)
    dram = {n: nc.dram_tensor(f"in_{n}", v.shape, mybir.dt.from_np(v.dtype), kind="ExternalInput").ap()
            for n, v in arrays.items()}
    out = nc.dram_tensor("out_x", (B, S, D), F32, kind="ExternalOutput").ap()
    build(nc, dram, out)
    r = run(nc, [{f"in_{n}": v for n, v in arrays.items()}], core_ids=[0])
    return r.results[0]["out_x"]
```

```python
from contextlib import ExitStack
from math import log, pi

import numpy as np
import concourse.bass as bass
from concourse import mybir

LAYERS = (0, 1, 2, 3, 4, 5, 6, 7)

F32 = mybir.dt.float32
BF16 = mybir.dt.bfloat16
F16 = mybir.dt.float16
I32 = mybir.dt.int32
ALU = mybir.AluOpType
ACT = mybir.ActivationFunctionType
AXX = mybir.AxisListType.X

P = 128
B, S, D = 4, 1024, 128
NT = B * S // P
GROUP = 4
GT = GROUP * P
NG = NT // GROUP
EPS = 1e-5
ROUND = 1.5 * 2.0 ** 23


class Chain:

    def __init__(self, eng, sem):
        self.eng, self.sem, self.n = eng, sem, 0

    def do(self, ins):
        ins.then_inc(self.sem, 1)
        self.n += 1

    def sync(self):
        self.eng.wait_ge(self.sem, self.n)

    def step(self, ins):
        self.do(ins)
        self.sync()

    def restart(self):
        if self.n:
            self.sync()
            self.eng.sem_clear(self.sem)
        self.n = 0


class Core:

    def __init__(self, nc, ctx, dram):
        self.nc, self.ctx, self.dram = nc, ctx, dram
        self.layer_sems = None
        self.sem_ctx = None
        self.programs = {e: [] for e in ("sync", "tensor", "scalar", "vector", "gpsimd")}
        self.X = self.sb("X", [P, NT, D])
        self.XT = self.sb("XT", [P, B * S])
        self.ident = self.sb("ident", [P, P])
        self.ident16 = self.sb("ident16", [P, P], BF16)
        self.mhalf = self.sb("mhalf", [P, P])
        self.ones_row = self.sb("ones_row", [1, P])
        self.psum = ctx.enter_context(nc.psum_tensor("psum", [P, 8, 512], F32))
        self.consts_in = self.sem("consts_in")
        self.ident16_in = self.sem("ident16_in")
        self.held = self.sem("held")
        self.layer_done = self.sem("layer_done")
        self.layers = 0
        self.free = []

    def sb(self, name, shape, dt=F32, ctx=None):
        return (ctx or self.ctx).enter_context(self.nc.sbuf_tensor(name, shape, dt))

    def sem(self, name):
        if self.layer_sems is None:
            return self.ctx.enter_context(self.nc.semaphore(name))
        self.layer_sems.append(self.sem_ctx.enter_context(self.nc.semaphore(name)))
        return self.layer_sems[-1]

    def free_sem(self, name):
        self.free.append(self.sem(name))
        return self.free[-1]

    def add(self, **programs):
        for e, f in programs.items():
            self.programs[e].append(f)

    def plain(self, eng):
        eng.sem_inc(self.held, 1)

    def start(self, eng, layer):
        if layer:
            eng.wait_ge(self.layer_done, layer)
        else:
            eng.wait_ge(self.consts_in, 64)


def layer_norm(k, tag, twice=False, affine=None, affine_in=None):
    nc = k.nc
    tag = f"{tag}_norm"
    ready = [k.sem(f"{tag}_ready{g}") for g in range(2)]
    turned = [k.free_sem(f"{tag}_turned{g}") for g in range(2)]
    written = [k.free_sem(f"{tag}_xt{g}") for g in range(2)]
    var_in, root_out = k.sem(f"{tag}_var"), k.sem(f"{tag}_root")
    own = k.sem(f"{tag}_ln_own")
    ctx = k.layer_ctx
    xn = [k.sb(f"{tag}_xn{g}", [P, GROUP, D], ctx=ctx) for g in range(2)]
    stats = k.sb(f"{tag}_st", [P, NT, 6], ctx=ctx)
    mv = k.sb(f"{tag}_mv", [P, NT, 2], ctx=ctx)
    root = k.sb(f"{tag}_root_buf", [P, NT], ctx=ctx)
    rstd = k.sb(f"{tag}_rs", [P, NT], ctx=ctx)
    tmp = k.sb(f"{tag}_ln_tmp", [P, 2, NT], ctx=ctx)
    layer = k.layers

    def vector(v):
        k.start(v, layer)
        c = Chain(v, own)
        with v.Fori(0, NT // 8) as i:
            for n in range(8):
                c.do(nc.vector.bn_stats(stats[:, bass.ds(i * 8 + n, 1), :], k.X[:, bass.ds(i * 8 + n, 1), :]))
            c.restart()
        for n in range(NT):
            c.do(nc.vector.bn_aggr(mv[:, n, :], stats[:, n, :]))
        c.sync()
        nc.vector.tensor_scalar(tmp[:, 0, :], mv[:, :, 1], EPS, None, ALU.add).then_inc(var_in, 1)
        v.wait_ge(root_out, 1)
        if twice:
            c.step(nc.vector.tensor_tensor(tmp[:, 0, :], rstd[:, :], rstd[:, :], ALU.mult))
            c.step(nc.vector.tensor_tensor(tmp[:, 1, :], tmp[:, 0, :], mv[:, :, 1], ALU.mult))
            nc.vector.tensor_scalar(tmp[:, 0, :], tmp[:, 1, :], EPS, None, ALU.add).then_inc(var_in, 1)
            v.wait_ge(root_out, 2)
            c.step(nc.vector.tensor_tensor(rstd[:, :], rstd[:, :], root[:, :], ALU.mult))
        c.restart()
        with v.Fori(0, NG // 2) as i:
            for g in range(2):
                v.wait_ge(turned[g], i + 1)
                for n in range(GROUP):
                    t = i * 2 * GROUP + g * GROUP + n
                    last = nc.vector.tensor_scalar(xn[g][:, n, :], k.X[:, bass.ds(t, 1), :], mv[:, bass.ds(t, 1), 0],
                                                   rstd[:, bass.ds(t, 1)], ALU.subtract, ALU.mult)
                    if n < GROUP - 1:
                        c.do(last)
                c.sync()
                last.then_inc(ready[g], 1)
            c.restart()

    def tensor(t):
        k.start(t, layer)
        with t.Fori(0, NG // 2) as i:
            for g in range(2):
                t.wait_ge(ready[g], i + 1)
                t.wait_ge(written[g], i + 1)
                for n in range(GROUP):
                    last = nc.tensor.transpose(k.psum[:, g, n * P:(n + 1) * P], xn[g][:, n, :], k.ident[:, :])
                last.then_inc(turned[g], 1)

    def scalar(a):
        k.start(a, layer)
        if affine_in is not None:
            a.wait_ge(*affine_in)
        with a.Fori(0, NG // 2) as i:
            for g in range(2):
                a.wait_ge(turned[g], i + 2)
                dst = k.XT[:, bass.ds(i * 2 * GT + g * GT, GT)]
                if affine is None:
                    nc.scalar.copy(dst, k.psum[:, g, :]).then_inc(written[g], 1)
                else:
                    nc.scalar.activation(dst, k.psum[:, g, :], ACT.Identity, scale=affine[0],
                                         bias=affine[1]).then_inc(written[g], 1)

    def gpsimd(p):
        k.start(p, layer)
        for q in range(2 if twice else 1):
            p.wait_ge(var_in, q + 1)
            nc.gpsimd.tensor_tensor((root if q else rstd)[:, :], tmp[:, 0, :], k.mhalf[:, 0:NT], ALU.pow).then_inc(root_out, 1)

    k.add(vector=vector, tensor=tensor, scalar=scalar, gpsimd=gpsimd)
    return written


def one_ahead(eng, count, ahead, behind):
    ahead(0, 0, 0)
    with eng.Fori(0, count // 2 - 1) as i:
        ahead(2 * i + 1, i, 1)
        behind(2 * i, i, 0)
        ahead(2 * i + 2, i + 1, 0)
        behind(2 * i + 1, i, 1)
    last = count // 2 - 1
    ahead(count - 1, last, 1)
    behind(count - 2, last, 0)
    behind(count - 1, last, 1)


def sine_ffn(k):
    nc, d, ctx = k.nc, k.dram, k.layer_ctx
    FF = d["L0_ffn_W1"].shape[1]
    NF = FF // P
    w1 = k.sb("sf_w1", [P, FF], ctx=ctx)
    w2 = k.sb("sf_w2", [P, NF, D], ctx=ctx)
    cols = k.sb("sf_cols", [P, 4, NF], ctx=ctx)
    b2 = k.sb("sf_b2", [1, GT], ctx=ctx)
    tmp = k.sb("sf_tmp", [P, 4, NF], ctx=ctx)
    sc = k.sb("sf_sincos", [P, 2, NF], ctx=ctx)
    turn0 = k.sb("sf_turn0", [P, NF], ctx=ctx)
    coef = k.sb("sf_coef", [P, NF], ctx=ctx)
    y, r, sn, q = ([k.sb(f"sf_{n}{j}", [P, GT], ctx=ctx) for j in range(NF)] for n in ("y", "r", "sn", "q"))
    act = [k.sb(f"sf_act{j}", [P, NF, GT], ctx=ctx) for j in range(2)]
    w_in, own, pre, presin, coef_in = (k.sem(f"sf_{n}") for n in ("w_in", "own", "pre", "presin", "coef_in"))
    hid, y_in, frac, sine = ([k.sem(f"sf_{n}{j}") for j in range(NF)] for n in ("hid", "y_in", "frac", "sine"))
    gated = [k.free_sem(f"sf_gated{j}") for j in range(NF)]
    relu = [k.sem(f"sf_relu{g}") for g in range(2)]
    outp = [k.free_sem(f"sf_out{g}") for g in range(2)]
    added = [k.free_sem(f"sf_added{g}") for g in range(2)]
    hidden = [k.psum[:, b, :] for b in (2, 3, 6, 7)]
    layer = k.layers
    xt = layer_norm(k, "sf")

    def sync(s):
        if layer:
            s.wait_ge(k.layer_done, layer)
        s.dma_start(w1[:, :], d["L0_ffn_W1"]).then_inc(w_in, 16)
        s.dma_start(w2[:, :, :], d["L0_ffn_W2"].rearrange("(f p) d -> p f d", p=P)).then_inc(w_in, 16)
        s.dma_start(cols[:, :, :], d["sf_cols"]).then_inc(w_in, 16)
        s.dma_start(b2[:, :], d["sf_b2"]).then_inc(w_in, 16)

    def groups(eng, body):
        body(0, 0, 0, first=True)
        body(1, 0, 1)
        with eng.Fori(1, NG // 2) as i:
            body(2 * i, i, 0)
            body(2 * i + 1, i, 1)

    def behind(n, g, f, skew):
        return (n, g, f - skew) if f >= skew else (n - 1, 1 - g, f - skew + NF)

    C1 = 6.28125
    C2 = 2 * pi - C1

    def vector(v):
        c = Chain(v, own)
        v.wait_ge(w_in, 64)
        th = cols[:, 1, :]
        c.step(nc.vector.tensor_scalar(tmp[:, 0, :], th, 1 / (2 * pi), ROUND, ALU.mult, ALU.add))
        c.step(nc.vector.tensor_scalar(tmp[:, 1, :], tmp[:, 0, :], ROUND, None, ALU.subtract))
        c.step(nc.vector.scalar_tensor_tensor(tmp[:, 2, :], tmp[:, 1, :], -C1, th, ALU.mult, ALU.add))
        c.step(nc.vector.scalar_tensor_tensor(tmp[:, 3, :], tmp[:, 1, :], -C2, tmp[:, 2, :], ALU.mult, ALU.add))
        c.step(nc.vector.tensor_scalar(turn0[:, :], tmp[:, 3, :], 1 / (2 * pi), None, ALU.mult))
        c.step(nc.vector.tensor_scalar(tmp[:, 0, :], turn0[:, :], ROUND, ROUND, ALU.add, ALU.subtract))
        c.step(nc.vector.tensor_tensor(tmp[:, 2, :], turn0[:, :], tmp[:, 0, :], ALU.subtract))
        c.step(nc.vector.tensor_scalar(tmp[:, 1, :], turn0[:, :], 0.25, None, ALU.add))
        c.step(nc.vector.tensor_scalar(tmp[:, 0, :], tmp[:, 1, :], ROUND, ROUND, ALU.add, ALU.subtract))
        c.step(nc.vector.tensor_tensor(tmp[:, 3, :], tmp[:, 1, :], tmp[:, 0, :], ALU.subtract))
        nc.vector.tensor_scalar(tmp[:, 0, :], cols[:, 3, :], 0.1, None, ALU.mult).then_inc(pre, 1)
        v.wait_ge(pre, 1)
        v.wait_ge(presin, 1)
        c.step(nc.vector.tensor_tensor(tmp[:, 1, :], sc[:, 0, :], cols[:, 3, :], ALU.mult))
        c.step(nc.vector.tensor_tensor(tmp[:, 2, :], sc[:, 1, :], cols[:, 2, :], ALU.mult))
        c.step(nc.vector.tensor_tensor(tmp[:, 3, :], tmp[:, 1, :], tmp[:, 2, :], ALU.add))
        c.step(nc.vector.tensor_tensor(coef[:, :], tmp[:, 3, :], tmp[:, 0, :], ALU.mult))
        c.step(nc.vector.scalar_tensor_tensor(tmp[:, 1, :], cols[:, 0, :], 0.1 / (2 * pi), turn0[:, :], ALU.mult, ALU.add))
        c.restart()
        v.sem_inc(coef_in, 1)

        def gate(n, g, f):
            v.wait_ge(sine[f], n + 1)
            nc.vector.scalar_tensor_tensor(q[f][:, :], sn[f][:, :], coef[:, f:f + 1], hidden[f], ALU.mult, ALU.add).then_inc(gated[f], 1)

        def add(i, g):
            v.wait_ge(outp[g], i + 2)
            xs = k.X[:, bass.ds(i * 2 * GROUP + g * GROUP, GROUP), :]
            nc.vector.tensor_tensor(xs, xs, k.psum[:, 4 + g, :].rearrange("p (n d) -> p n d", d=D), ALU.add).then_inc(added[g], 1)

        def body(n, i, g, first=False):
            for f in range(NF):
                v.wait_ge(y_in[f], n + 1)
                if not first:
                    v.wait_ge(sine[f], n)
                k.plain(v)
                c.do(nc.vector.tensor_scalar(r[f][:, :], y[f][:, :], ROUND, ROUND, ALU.add, ALU.subtract))
                made = c.n
                if f >= 2 or not first:
                    gate(*behind(n, g, f, 2))
                v.wait_ge(own, made)
                nc.vector.tensor_tensor(r[f][:, :], y[f][:, :], r[f][:, :], ALU.subtract).then_inc(frac[f], 1)
                if f == 1 and not (isinstance(i, int) and i == 0):
                    add(i - 1, g)
            c.restart()

        groups(v, body)
        for f in (NF - 2, NF - 1):
            gate(NG - 1, 1, f)
        for g in range(2):
            add(NG // 2 - 1, g)
        v.wait_ge(added[0], NG // 2 + 1)
        v.wait_ge(added[1], NG // 2 + 1)
        nc.vector.tensor_copy(tmp[:, 0, 0:1], tmp[:, 0, 0:1]).then_inc(k.layer_done, 1)

    def scalar(a):
        a.wait_ge(pre, 1)
        nc.scalar.activation(sc[:, :, :], tmp[:, 2:4, :], ACT.Sin, scale=6.283185).then_inc(presin, 1)

        def turns(n, g, f, first):
            a.wait_ge(hid[f], n + 1)
            if not first:
                a.wait_ge(frac[f], n)
            nc.scalar.activation(y[f][:, :], hidden[f], ACT.Identity, scale=0.1 / (2 * pi), bias=tmp[:, 1, f:f + 1]).then_inc(y_in[f], 1)

        def take_sine(n, g, f):
            a.wait_ge(frac[f], n + 1)
            a.wait_ge(gated[f], n + 1)
            nc.scalar.activation(sn[f][:, :], r[f][:, :], ACT.Sin, scale=6.283185).then_inc(sine[f], 1)

        def rectify(n, g, f):
            a.wait_ge(gated[f], n + 2)
            nc.scalar.activation(act[g][:, f, :], q[f][:, :], ACT.Relu, bias=cols[:, 0, f:f + 1]).then_inc(relu[g], 1)

        def body(n, i, g, first=False):
            for f in range(NF):
                turns(n, g, f, first)
                if f >= 1 or not first:
                    take_sine(*behind(n, g, f, 1))
                if f == 3:
                    a.wait_ge(outp[g], i + 1)
                if f >= 3 or not first:
                    rectify(*behind(n, g, f, 3))

        a.wait_ge(coef_in, 1)
        groups(a, body)
        take_sine(NG - 1, 1, NF - 1)
        for f in range(1, NF):
            rectify(NG - 1, 1, f)

    def tensor(t):
        t.wait_ge(w_in, 64)

        def first_product(n, i, g):
            t.wait_ge(xt[g], i + 2)
            for f in range(NF):
                t.wait_ge(gated[f], n + 1)
                nc.tensor.matmul(hidden[f], w1[:, f * P:(f + 1) * P], k.XT[:, bass.ds(i * 2 * GT + g * GT, GT)],
                                 start=True, stop=True).then_inc(hid[f], 1)

        def second_product(n, i, g):
            t.wait_ge(added[g], i + 1)
            t.wait_ge(relu[g], (i + 1) * NF)
            nc.tensor.matmul(k.psum[:, 4 + g, :], k.ones_row[:, :], b2[:, :], start=True, stop=True)
            for n_ in range(GROUP):
                for f in range(NF):
                    last = nc.tensor.matmul(k.psum[:, 4 + g, n_ * D:(n_ + 1) * D], act[g][:, f, n_ * P:(n_ + 1) * P],
                                            w2[:, f, :], start=False, stop=True, skip_group_check=True)
            last.then_inc(outp[g], 1)

        one_ahead(t, NG, first_product, second_product)

    k.add(sync=sync, vector=vector, scalar=scalar, tensor=tensor)


def delta_net(k):
    nc, d, ctx = k.nc, k.dram, k.layer_ctx
    H = d["L0_attn_Wb"].shape[1]
    HD = D // H
    N = B * H
    R = P // N
    V = HD // R
    C = 8
    NBLK = S // C
    CB = 8
    NCH = NBLK // CB
    X2 = 2 * HD
    W3 = 3 * D
    wqkv = k.sb("dn_wqkv", [P, W3 + H], ctx=ctx)
    lnw = k.sb("dn_lnw", [P, D], ctx=ctx)
    lnb = k.sb("dn_lnb", [P, D], ctx=ctx)
    stage = k.sb("dn_stage", [P, C, NBLK], ctx=ctx)
    arena = k.sb("dn_arena", [P, 34000], ctx=ctx)
    place = [0]

    def take(*shape):
        size = int(np.prod(shape))
        flat = arena[:, place[0]:place[0] + size]
        place[0] += size
        names = "abcde"[:len(shape)]
        if len(shape) == 1:
            return flat
        return flat.rearrange(f"p ({' '.join(names)}) -> p {' '.join(names)}", **{n: s for n, s in zip(names, shape)})

    raw = [take(3, H, C, HD) for _ in range(2)]
    sig = [take(H, C, HD) for _ in range(2)]
    beta = [take(H, C) for _ in range(2)]
    sq, norm = take(H * C, HD), take(H * C)
    L, Pm = take(H, C, C), take(H, C, C)
    WU, GF = take(H, C, X2), take(H, C, X2)
    prod = [take(H * C * X2) for _ in range(2)]
    red = take(H, X2)
    rec = [take(H, 3, C * HD) for _ in range(2)]
    recu = [take(R, H, 2, C * V) for _ in range(2)]
    place[0] = 0
    stream = [take(CB, 3, C * HD) for _ in range(2)]
    ustream = [take(CB, C * V) for _ in range(2)]
    fstream = [take(CB, C * V) for _ in range(2)]
    pa = [take(CB, C * V, HD + 1) for _ in range(2)]
    pb = [take(CB, V * HD, C + 1) for _ in range(2)]
    qs = [take(CB, C * V, HD) for _ in range(2)]
    o = take(2 * CB * C, V)
    osum = k.sb("dn_osum", [P, CB * C * V], ctx=ctx)
    u = k.sb("dn_u", [P, 2, C * V], ctx=ctx)
    wkg = nc.dram_tensor("dn_wkg", (N, NBLK, 3 * C * HD), F32, kind="Internal").ap()
    uf = nc.dram_tensor("dn_uf", (R, N, NBLK, 2 * C * V), F32, kind="Internal").ap()
    om = k.XT[:, :].rearrange("p (t d) -> p t d", d=D)
    (w_in, staged, own, pool_own) = (k.sem(f"dn_{n}") for n in ("w_in", "staged", "own", "pool_own"))
    pairs = lambda n, free=False: [(k.free_sem if free else k.sem)(f"dn_{n}{g}") for g in range(2)]
    projected, emptied = pairs("projected"), pairs("emptied", True)
    raw_in, prepared, solved = pairs("raw_in"), pairs("prepared"), pairs("solved")
    packed, stored = pairs("packed", True), pairs("stored", True)
    loaded, f_loaded, filled = pairs("loaded"), pairs("f_loaded"), pairs("filled")
    scanned, states_read, qs_in = pairs("scanned", True), pairs("states_read", True), pairs("qs_in")
    summed = pairs("summed", True)
    o_ready, root_in, root_out = k.sem("dn_o_ready"), k.sem("dn_root_in"), k.sem("dn_root_out")
    o_turned, rows_in = k.free_sem("dn_o_turned"), k.free_sem("dn_rows_in")
    layer = k.layers
    xt = layer_norm(k, "dn")

    def sync(s):
        if layer:
            s.wait_ge(k.layer_done, layer)
        for dst, src in ((wqkv, "dn_wqkv"), (lnw, "dn_lnw"), (lnb, "dn_lnb")):
            s.dma_start(dst[:, :], d[src]).then_inc(w_in, 16)
        with s.Fori(0, B // 2) as i:
            for g in range(2):
                b = 2 * i + g
                s.wait_ge(packed[g], i + 2)
                k.plain(s)
                s.dma_start(wkg[bass.ds(b * H, H), :, :].rearrange("h k e -> k h e"),
                            rec[g][:, :, :, :].rearrange("p h z e -> p h (z e)")).then_inc(stored[g], 16)
                for r in range(R):
                    s.dma_start(uf[r, bass.ds(b * H, H), :, :].rearrange("h k e -> k h e"),
                                recu[g][:, r, :, :, :].rearrange("p h z e -> p h (z e)")).then_inc(stored[g], 16)
        for g in range(2):
            s.wait_ge(stored[g], B // 2 * (R + 1) * 16 + 1)
        with s.Fori(0, NCH // 2) as i:
            for g in range(2):
                n = 2 * i + g
                s.wait_ge(scanned[g], i + 1)
                s.wait_ge(states_read[g], i + 1)
                k.plain(s)
                for r in range(R):
                    s.dma_start(stream[g][r * N:(r + 1) * N, :, :, :].rearrange("p k z e -> p k (z e)"),
                                wkg[:, bass.ds(n * CB, CB), :]).then_inc(loaded[g], 16)
                chunk = uf[:, :, bass.ds(n * CB, CB), :].rearrange("r n k e -> (r n) k e")
                s.dma_start(ustream[g][:, :, :], chunk[:, :, 0:C * V]).then_inc(loaded[g], 16)
                s.wait_ge(summed[g], i + 1)
                k.plain(s)
                s.dma_start(fstream[g][:, :, :], chunk[:, :, C * V:2 * C * V]).then_inc(f_loaded[g], 16)

    def tensor(t):
        t.wait_ge(w_in, 48)
        with t.Fori(0, B) as i:
            t.wait_ge(staged, i + 1)
            for j in range(C):
                g = j % 2
                t.wait_ge(emptied[g], i * (C // 2) + j // 2 + 1)
                nc.tensor.matmul(k.psum[:, g, 0:W3 + H], stage[:, j, :], wqkv[:, :], start=True, stop=True).then_inc(projected[g], 1)
        with t.Fori(0, NCH // 2) as i:
            t.wait_ge(o_ready, i + 1)
            t.wait_ge(rows_in, i + 1)
            for f in range(V):
                last = nc.tensor.transpose(k.psum[:, 2, f * P:(f + 1) * P], o[:, :, f], k.ident[:, :])
            last.then_inc(o_turned, 1)

    def scalar(a):
        def take_in(b, i, g):
            for z in range(2):
                a.wait_ge(xt[z], b + 2)
            for z in range(2):
                a.wait_ge(emptied[z], b * (C // 2) + 1)
            k.plain(a)
            nc.scalar.copy(stage[:, :, :], k.XT[:, bass.ds(b * S, S)].rearrange("p (k j) -> p j k", j=C)).then_inc(staged, 1)
            a.wait_ge(packed[g], i + 1)
            for j in range(C):
                z = j % 2
                a.wait_ge(projected[z], b * (C // 2) + j // 2 + 1)
                nc.scalar.copy(raw[g][:, :, :, j, :], k.psum[:, z, 0:W3].rearrange("p (z h e) -> p z h e", z=3, h=H))
                nc.scalar.activation(sig[g][:, :, j, :], k.psum[:, z, 2 * D:W3].rearrange("p (h e) -> p h e", h=H), ACT.Sigmoid)
                nc.scalar.activation(beta[g][:, :, j], k.psum[:, z, W3:W3 + H], ACT.Sigmoid).then_inc(emptied[z], 1)
            for z in range(2):
                a.wait_ge(emptied[z], (b + 1) * (C // 2) + 1)
            a.sem_inc(raw_in[g], 1)

        def pack(b, i, g):
            a.wait_ge(solved[g], i + 1)
            a.wait_ge(stored[g], i * (R + 1) * 16 + 1)
            k.plain(a)
            blk = lambda x: x.rearrange("p h (j e) -> p h j e", j=C)
            nc.scalar.copy(blk(rec[g][:, :, 0, :]), WU[:, :, :, 0:HD])
            nc.scalar.copy(blk(rec[g][:, :, 1, :]), GF[:, :, :, 0:HD])
            nc.scalar.copy(blk(rec[g][:, :, 2, :]), raw[g][:, 0, :, :, :])
            for r in range(R):
                cols = slice(HD + r * V, HD + (r + 1) * V)
                nc.scalar.copy(blk(recu[g][:, r, :, 0, :]), WU[:, :, :, cols])
                last = nc.scalar.copy(blk(recu[g][:, r, :, 1, :]), GF[:, :, :, cols])
            last.then_inc(packed[g], 1)

        take_in(0, 0, 0)
        with a.Fori(0, B // 2 - 1) as i:
            take_in(2 * i + 1, i, 1)
            pack(2 * i, i, 0)
            take_in(2 * i + 2, i + 1, 0)
            pack(2 * i + 1, i, 1)
        last = B // 2 - 1
        take_in(B - 1, last, 1)
        pack(B - 2, last, 0)
        pack(B - 1, last, 1)

        def fill(n, i, g):
            a.wait_ge(loaded[g], (i + 1) * (R + 1) * 16)
            k.plain(a)
            nc.scalar.copy(pa[g][:, :, :, HD], ustream[g][:, :, :]).then_inc(filled[g], 1)

        def rows(q):
            a.wait_ge(o_turned, q + 2)
            k.plain(a)
            src = k.psum[:, 2, :].rearrange("p (f r n) -> p n r f", f=V, r=R)
            dst = om.rearrange("p (b c) (h r f) -> p b c h r f", b=B, h=H, r=R)
            for b in range(B):
                last = nc.scalar.copy(dst[:, b, bass.ds(q, 1), :, :, :].rearrange("p c h r f -> p (c h) r f"), src[:, b * H:(b + 1) * H, :, :])
            last.then_inc(rows_in, 1)

        fill(0, 0, 0)
        fill(1, 0, 1)
        with a.Fori(1, NCH // 2) as i:
            fill(2 * i, i, 0)
            fill(2 * i + 1, i, 1)
            rows(i - 1)
        rows(NCH // 2 - 1)

    def gpsimd(p):
        c = Chain(p, pool_own)

        def halve(x, width, least):
            while width > least:
                width //= 2
                c.step(nc.gpsimd.tensor_tensor(x[:, :, 0:width], x[:, :, 0:width], x[:, :, width:2 * width], ALU.add))

        with p.Fori(0, B // 2) as i:
            for g in range(2):
                p.wait_ge(raw_in[g], i + 1)
                k.plain(p)
                kf = raw[g][:, 0, :, :, :].rearrange("p h j e -> p (h j) e")
                c.do(nc.gpsimd.tensor_tensor(raw[g][:, 2, :, :, :], raw[g][:, 2, :, :, :], sig[g][:, :, :, :], ALU.mult))
                c.step(nc.gpsimd.tensor_tensor(sq[:, :, :], kf, kf, ALU.mult))
                halve(sq, HD, 1)
                c.step(nc.gpsimd.tensor_scalar(norm, sq[:, :, 0], 1e-24, None, ALU.max))
                c.step(nc.gpsimd.tensor_tensor(norm, norm, k.mhalf[:, 0:H * C], ALU.pow))
                c.step(nc.gpsimd.tensor_tensor(kf, kf, norm.unsqueeze(2).to_broadcast([P, H * C, HD]), ALU.mult))
                c.restart()
                p.sem_inc(prepared[g], 1)

        with p.Fori(0, NCH // 2) as i:
            for g in range(2):
                p.wait_ge(scanned[g], i + 2)
                p.wait_ge(summed[g], i + 1)
                k.plain(p)
                for blk in range(CB):
                    G4 = stream[g][:, blk, 1, :].rearrange("p (t e) -> p t e", t=C).unsqueeze(2).to_broadcast([P, C, V, HD])
                    S4 = pb[g][:, blk, :, C].rearrange("p (v e) -> p v e", v=V).unsqueeze(1).to_broadcast([P, C, V, HD])
                    c.do(nc.gpsimd.tensor_tensor(qs[g][:, blk, :, :].rearrange("p (t v) e -> p t v e", t=C), G4, S4, ALU.mult))
                c.sync()
                p.sem_inc(states_read[g], 1)
                halve(qs[g].rearrange("p k w e -> p (k w) e"), HD, 4)
                c.restart()
                p.sem_inc(qs_in[g], 1)
        p.wait_ge(root_in, 1)
        nc.gpsimd.tensor_tensor(root[:, :], var[:, :], k.mhalf[:, 0:NT], ALU.pow).then_inc(root_out, 1)

    var = k.sb("dn_var", [P, NT], ctx=ctx)
    root = k.sb("dn_root2", [P, NT], ctx=ctx)
    stats = k.sb("dn_stats2", [P, NT, 6], ctx=ctx)
    mv = k.sb("dn_mv2", [P, NT, 2], ctx=ctx)

    def vector(v):
        c = Chain(v, own)

        def rows(which, mult, reduce):
            reduced, before = [c.n, c.n], None
            for q, i in enumerate(which):
                v.wait_ge(own, reduced[q % 2]) if reduced[q % 2] else None
                c.do(mult(i, prod[q % 2]))
                made = c.n
                if before:
                    v.wait_ge(own, before[2])
                    c.do(reduce(before[0], before[1]))
                    reduced[(q - 1) % 2] = c.n
                before = (i, prod[q % 2], made)
            c.sync()
            c.step(reduce(before[0], before[1]))

        def solve(i, g):
            v.wait_ge(prepared[g], i + 1)
            k.plain(v)
            K, Q = raw[g][:, 0, :, :, :], raw[g][:, 1, :, :, :]

            def gram(A, out):
                def mult(r, buf, n):
                    pr = buf[:, 0:H * n * HD].rearrange("p (h j e) -> p h j e", h=H, j=n)
                    return nc.vector.tensor_tensor(pr, K[:, :, 0:n, :], A[:, :, r, :].unsqueeze(2).to_broadcast([P, H, n, HD]), ALU.mult)

                def reduce(r, buf, n):
                    pr = buf[:, 0:H * n * HD].rearrange("p (h j e) -> p h j e", h=H, j=n)
                    return nc.vector.tensor_reduce(out[:, :, r, 0:n], pr, AXX, ALU.add)
                return mult, reduce

            mult, reduce = gram(K, L)
            rows(range(1, C), lambda r, buf: mult(r, buf, r), lambda r, buf: reduce(r, buf, r))
            mult_q, reduce_q = gram(Q, Pm)
            rows(range(C), lambda r, buf: mult_q(r, buf, r + 1), lambda r, buf: reduce_q(r, buf, r + 1))
            v.wait_ge(packed[1 - g], i + 1 + g)
            k.plain(v)
            bc = beta[g][:, :, :].unsqueeze(3)
            c.do(nc.vector.tensor_tensor(L, L, bc.to_broadcast([P, H, C, C]), ALU.mult))
            c.do(nc.vector.scalar_tensor_tensor(WU[:, :, :, 0:HD], K, -1.0, bc.to_broadcast([P, H, C, HD]), ALU.mult, ALU.mult))
            c.do(nc.vector.tensor_tensor(WU[:, :, :, HD:X2], raw[g][:, 2, :, :, :], bc.to_broadcast([P, H, C, HD]), ALU.mult))
            c.sync()

            def product(A, r, buf, n):
                pr = buf[:, 0:H * X2 * n].rearrange("p (h e j) -> p h e j", h=H, e=X2)
                return pr, nc.vector.tensor_tensor(pr, WU[:, :, 0:n, :].rearrange("p h j e -> p h e j"),
                                                   A[:, :, r, 0:n].unsqueeze(2).to_broadcast([P, H, X2, n]), ALU.mult)

            for r in range(1, C):
                pr, ins = product(L, r, prod[0], r)
                c.step(ins)
                c.step(nc.vector.tensor_reduce(red[:, :, :], pr, AXX, ALU.add))
                c.step(nc.vector.tensor_tensor(WU[:, :, r, :], WU[:, :, r, :], red[:, :, :], ALU.subtract))
            rows(range(C), lambda r, buf: product(Pm, r, buf, r + 1)[1],
                 lambda r, buf: nc.vector.tensor_reduce(GF[:, :, r, :], buf[:, 0:H * X2 * (r + 1)].rearrange(
                     "p (h e j) -> p h e j", h=H, e=X2), AXX, ALU.add))
            c.step(nc.vector.tensor_tensor(GF[:, :, :, 0:HD], GF[:, :, :, 0:HD], Q, ALU.add))
            c.restart()
            v.sem_inc(solved[g], 1)

        c.step(nc.vector.memset(L, 0.0))
        c.restart()
        with v.Fori(0, B // 2) as i:
            for g in range(2):
                solve(i, g)

        def outputs(i, g):
            v.wait_ge(qs_in[g], i + 1)
            v.wait_ge(f_loaded[g], i * 16 + 16)
            if g == 0:
                v.wait_ge(o_turned, i + 1)
            k.plain(v)
            c.step(nc.vector.tensor_reduce(osum[:, :], qs[g].rearrange("p k w e -> p (k w) e")[:, :, 0:4], AXX, ALU.add))
            half = o[:, g * CB * C:(g + 1) * CB * C, :].rearrange("p (k t) v -> p k (t v)", k=CB)
            c.step(nc.vector.tensor_tensor(half, osum[:, :].rearrange("p (k w) -> p k w", k=CB), fstream[g][:, :, :], ALU.add))
            v.sem_inc(summed[g], 1)
            if g == 1:
                v.sem_inc(o_ready, 1)

        def scan(i, g):
            v.wait_ge(filled[g], i + 1)
            k.plain(v)
            for blk in range(CB):
                st = pb[g][:, blk, :, C].rearrange("p (v e) -> p v e", v=V)
                wv = stream[g][:, blk, 0, :].rearrange("p (t e) -> p t e", t=C)
                kv = stream[g][:, blk, 2, :].rearrange("p (t e) -> p e t", t=C)
                c.step(nc.vector.tensor_tensor(pa[g][:, blk, :, 0:HD].rearrange("p (t v) e -> p t v e", t=C),
                                               wv.unsqueeze(2).to_broadcast([P, C, V, HD]), st.unsqueeze(1).to_broadcast([P, C, V, HD]), ALU.mult))
                ub = u[:, blk % 2, :]
                c.step(nc.vector.tensor_reduce(ub, pa[g][:, blk, :, :], AXX, ALU.add))
                c.step(nc.vector.tensor_tensor(pb[g][:, blk, :, 0:C].rearrange("p (v e) t -> p v e t", v=V),
                                               kv.unsqueeze(1).to_broadcast([P, V, HD, C]),
                                               ub.rearrange("p (t v) -> p v t", t=C).unsqueeze(2).to_broadcast([P, V, HD, C]), ALU.mult))
                if blk < CB - 1:
                    nxt = pb[g][:, blk + 1, :, C]
                else:
                    nxt = pb[1 - g][:, 0, :, C]
                    v.wait_ge(states_read[1 - g], i + 1 + g)
                    k.plain(v)
                c.step(nc.vector.tensor_reduce(nxt, pb[g][:, blk, :, :], AXX, ALU.add))
            c.restart()
            v.sem_inc(scanned[g], 1)

        for g in range(2):
            v.wait_ge(stored[g], B // 2 * (R + 1) * 16 + 1)
        c.step(nc.vector.memset(pb[0][:, 0, :, C], 0.0))
        c.restart()
        scan(0, 0)
        scan(0, 1)
        with v.Fori(1, NCH // 2) as i:
            for g in range(2):
                outputs(i - 1, g)
                c.restart()
                scan(i, g)
        for g in range(2):
            outputs(NCH // 2 - 1, g)
        c.restart()
        v.wait_ge(rows_in, NCH // 2 + 1)
        for n in range(NT):
            c.do(nc.vector.bn_stats(stats[:, n, :], om[:, n, :]))
        c.sync()
        for n in range(NT):
            c.do(nc.vector.bn_aggr(mv[:, n, :], stats[:, n, :]))
        c.sync()
        nc.vector.tensor_scalar(var[:, :], mv[:, :, 1], EPS, None, ALU.add).then_inc(root_in, 1)
        v.wait_ge(root_out, 1)
        for n in range(NT):
            c.do(nc.vector.tensor_scalar(om[:, n, :], om[:, n, :], mv[:, n, 0:1], root[:, n:n + 1], ALU.subtract, ALU.mult))
        c.sync()
        HALF = NT // 2
        for h in range(2):
            part, xs = om[:, h * HALF:(h + 1) * HALF, :], k.X[:, h * HALF:(h + 1) * HALF, :]
            c.step(nc.vector.tensor_tensor(part, part, lnw[:, :].unsqueeze(1).to_broadcast([P, HALF, D]), ALU.mult))
            c.step(nc.vector.tensor_tensor(part, part, lnb[:, :].unsqueeze(1).to_broadcast([P, HALF, D]), ALU.add))
            last = nc.vector.tensor_tensor(xs, xs, part, ALU.add)
            if h == 0:
                c.step(last)
        last.then_inc(k.layer_done, 1)

    k.add(sync=sync, vector=vector, scalar=scalar, tensor=tensor, gpsimd=gpsimd)


def channel_mix(k):
    nc, d, ctx = k.nc, k.dram, k.layer_ctx
    wr, wk, wv = (k.sb(f"cm_{n}", [P, D], ctx=ctx) for n in ("wr", "wk", "wv"))
    mu = k.sb("cm_mu", [P, 2], ctx=ctx)
    one_less = k.sb("cm_one_less", [P, 2], ctx=ctx)
    part = [k.sb(f"cm_part{q}", [P, GT], ctx=ctx) for q in range(2)]
    mixed = [[k.sb(f"cm_mix{g}{q}", [P, GT], ctx=ctx) for q in range(2)] for g in range(2)]
    relu = k.sb("cm_relu", [P, GT], ctx=ctx)
    kact = [k.sb(f"cm_kact{g}", [P, GT], ctx=ctx) for g in range(2)]
    gate = [k.sb(f"cm_gate{g}", [P, GT], ctx=ctx) for g in range(2)]
    gated = k.sb("cm_gated", [P, GT], ctx=ctx)
    w_in, own, a_own = (k.sem(f"cm_{n}") for n in ("w_in", "own", "a_own"))
    mix_in = [k.sem(f"cm_mix_in{g}") for g in range(2)]
    rk = [k.free_sem(f"cm_rk{g}") for g in range(2)]
    acted = [k.free_sem(f"cm_acted{g}") for g in range(2)]
    kv = [k.free_sem(f"cm_kv{g}") for g in range(2)]
    added = [k.free_sem(f"cm_added{g}") for g in range(2)]
    layer = k.layers
    xt = layer_norm(k, "cm")

    def sync(s):
        if layer:
            s.wait_ge(k.layer_done, layer)
        for dst, src in ((wr, "cm_wr"), (wk, "cm_wk"), (wv, "cm_wv"), (mu, "cm_mu")):
            s.dma_start(dst[:, :], d[src]).then_inc(w_in, 16)

    def vector(v):
        c = Chain(v, own)
        v.wait_ge(w_in, 64)
        for g in range(2):
            v.wait_ge(xt[g], NG // 2 + 1)
        c.step(nc.vector.tensor_scalar(one_less[:, :], mu[:, :], -1.0, 1.0, ALU.mult, ALU.add))
        c.restart()

        def mix(i, g):
            v.wait_ge(rk[g], i + 1)
            x = k.XT[:, bass.ds(i * S + g * GT, GT)]
            for q in range(2):
                c.do(nc.vector.tensor_scalar(part[q][:, :], x, mu[:, q:q + 1], None, ALU.mult))
            c.sync()
            lo = 1 - g
            for q in range(2):
                prev = k.XT[:, bass.ds(i * S + g * GT + lo - 1, GT - lo)]
                last = nc.vector.scalar_tensor_tensor(mixed[g][q][:, lo:GT], prev, one_less[:, q:q + 1], part[q][:, lo:GT],
                                                      ALU.mult, ALU.add)
                c.do(last)
                if lo:
                    c.do(nc.vector.tensor_copy(mixed[g][q][:, 0:1], part[q][:, 0:1]))
            c.sync()
            v.sem_inc(mix_in[g], 1)

        def add(i, g):
            v.wait_ge(kv[g], i + 2)
            v.wait_ge(acted[g], i + 2)
            c.step(nc.vector.tensor_tensor(gated[:, :], gate[g][:, :], k.psum[:, 6 + g, :], ALU.mult))
            xs = k.X[:, bass.ds(i * 2 * GROUP + g * GROUP, GROUP), :]
            c.step(nc.vector.tensor_tensor(xs, xs, gated[:, :].rearrange("p (n d) -> p n d", d=D), ALU.add))
            v.sem_inc(added[g], 1)

        with v.Fori(0, B) as i:
            for g in range(2):
                mix(i, g)
            for g in range(2):
                add(i, g)
            c.restart()
        nc.vector.tensor_copy(part[0][:, 0:1], part[0][:, 0:1]).then_inc(k.layer_done, 1)

    def tensor(t):
        t.wait_ge(w_in, 64)
        with t.Fori(0, B) as i:
            for g in range(2):
                t.wait_ge(mix_in[g], i + 1)
                t.wait_ge(acted[g], i + 1)
                for n in range(GROUP):
                    nc.tensor.matmul(k.psum[:, 2 + g, n * D:(n + 1) * D], mixed[g][0][:, n * P:(n + 1) * P], wr[:, :],
                                     start=True, stop=True)
                nc.tensor.matmul(k.psum[:, 4 + g, :], wk[:, :], mixed[g][1][:, :], start=True, stop=True).then_inc(rk[g], 1)
            for g in range(2):
                t.wait_ge(acted[g], i + 2)
                t.wait_ge(added[g], i + 1)
                for n in range(GROUP):
                    last = nc.tensor.matmul(k.psum[:, 6 + g, n * D:(n + 1) * D], kact[g][:, n * P:(n + 1) * P], wv[:, :],
                                            start=True, stop=True)
                last.then_inc(kv[g], 1)

    def scalar(a):
        c = Chain(a, a_own)
        with a.Fori(0, B) as i:
            for g in range(2):
                a.wait_ge(rk[g], i + 2)
                a.wait_ge(kv[g], i + 1)
                c.do(nc.scalar.activation(relu[:, :], k.psum[:, 4 + g, :], ACT.Relu))
                a.wait_ge(added[g], i + 1)
                c.do(nc.scalar.activation(gate[g][:, :], k.psum[:, 2 + g, :], ACT.Sigmoid))
                c.sync()
                c.step(nc.scalar.activation(kact[g][:, :], relu[:, :], ACT.Square))
                a.sem_inc(acted[g], 1)
            c.restart()

    k.add(sync=sync, vector=vector, scalar=scalar, tensor=tensor)


def dense_experts(k):
    nc, d, ctx = k.nc, k.dram, k.layer_ctx
    E = d["L1_ffn_gate_w"].shape[1]
    THRESHOLD = 0.1
    gw = k.sb("de_gw", [P, E], ctx=ctx)
    gb = k.sb("de_gb", [1, GROUP * E], ctx=ctx)
    ew = k.sb("de_ew", [P, E * D], ctx=ctx)
    eb = k.sb("de_eb", [E, D], ctx=ctx)
    stage = [k.sb(f"de_stage{g}", [P, GT], ctx=ctx) for g in range(2)]
    lg, pr, w = (k.sb(f"de_{n}", [P, NT, E], ctx=ctx) for n in ("lg", "pr", "w"))
    m, zs = (k.sb(f"de_{n}", [P, NT], ctx=ctx) for n in ("m", "zs"))
    wst = [k.sb(f"de_wst{g}", [P, GROUP, E], ctx=ctx) for g in range(2)]
    wT = [k.sb(f"de_wT{g}", [E, GT], ctx=ctx) for g in range(2)]
    w_in, own, centred, exped, weighed, a_own = (k.sem(f"de_{n}") for n in ("w_in", "own", "centred", "exped", "weighed", "a_own"))
    staged = [k.sem(f"de_staged{g}") for g in range(2)]
    gated = [k.free_sem(f"de_gated{g}") for g in range(2)]
    taken = [k.free_sem(f"de_taken{g}") for g in range(2)]
    staged2 = [k.sem(f"de_staged2{g}") for g in range(2)]
    turned = [k.sem(f"de_turned{g}") for g in range(2)]
    wT_in = [k.sem(f"de_wT_in{g}") for g in range(2)]
    biased = [k.free_sem(f"de_biased{g}") for g in range(2)]
    expert = [k.sem(f"de_expert{g}") for g in range(2)]
    summed = [k.free_sem(f"de_summed{g}") for g in range(2)]
    wst_free = [k.free_sem(f"de_wst_free{g}") for g in range(2)]
    HALVES = E * D // 512
    layer = k.layers
    xt = layer_norm(k, "de")

    def sync(s):
        if layer:
            s.wait_ge(k.layer_done, layer)
        for dst, src in ((gw, "L1_ffn_gate_w"), (gb, "de_gb"), (ew, "de_ew"), (eb, "L1_ffn_expert_b")):
            s.dma_start(dst[:, :], d[src]).then_inc(w_in, 16)

    def groups(eng, body):
        with eng.Fori(0, NG // 2 - 1) as i:
            body(2 * i, i, 0)
            body(2 * i + 1, i, 1)
        body(NG - 2, NG // 2 - 1, 0)
        body(NG - 1, NG // 2 - 1, 1, more=False)

    def gpsimd(p):
        p.wait_ge(weighed, 1)
        for g in range(2):
            p.wait_ge(gated[g], NG // 2 + 1)
        with p.Fori(0, NG // 2) as i:
            for g in range(2):
                p.wait_ge(wst_free[g], i + 1)
                k.plain(p)
                nc.gpsimd.tensor_copy(wst[g][:, :, :], w[:, bass.ds(i * 2 * GROUP + g * GROUP, GROUP), :])
                nc.gpsimd.tensor_copy(stage[g][:, :], k.XT[:, bass.ds(i * 2 * GT + g * GT, GT)]).then_inc(staged2[g], 1)

    def tensor(t):
        t.wait_ge(w_in, 64)
        with t.Fori(0, NG // 2) as i:
            for g in range(2):
                t.wait_ge(staged[g], i + 1)
                t.wait_ge(taken[g], i + 1)
                bank = k.psum[:, g, 0:GROUP * E]
                nc.tensor.matmul(bank, k.ones_row[:, :], gb[:, :], start=True, stop=True)
                for n in range(GROUP):
                    last = nc.tensor.matmul(bank[:, n * E:(n + 1) * E], stage[g][:, n * P:(n + 1) * P], gw[:, :],
                                            start=False, stop=True, skip_group_check=True)
                last.then_inc(gated[g], 1)
        for g in range(2):
            t.wait_ge(taken[g], NG // 2 + 1)

        def bias(n, i, g):
            t.wait_ge(staged2[g], i + 1)
            t.wait_ge(biased[g], i + 1)
            for m_ in range(GROUP):
                last = nc.tensor.transpose(k.psum[0:E, g, m_ * P:(m_ + 1) * P], wst[g][:, m_, :], k.ident[:, :])
            last.then_inc(turned[g], 1)
            t.wait_ge(wT_in[g], i + 1)
            for m_ in range(GROUP):
                last = nc.tensor.matmul(k.psum[:, g, m_ * D:(m_ + 1) * D], wT[g][:, m_ * P:(m_ + 1) * P], eb[:, :],
                                        start=True, stop=True)
            last.then_inc(turned[g], 1)

        def experts(n, g, pairs):
            for pair in pairs:
                for h in range(HALVES):
                    t.wait_ge(summed[h], n * (GROUP // 2) + pair + 1)
                    for u in range(2):
                        m_ = pair * 2 + u
                        last = nc.tensor.matmul(k.psum[:, 2 + 2 * h + u, :], stage[g][:, m_ * P:(m_ + 1) * P],
                                                ew[:, h * 512:(h + 1) * 512], start=True, stop=True)
                    last.then_inc(expert[h], 1)

        def body(n, i, g, more=True):
            experts(n, g, range(0, 1))
            if more:
                bias(n + 1, i + g, 1 - g)
            experts(n, g, range(1, GROUP // 2))

        bias(0, 0, 0)
        groups(t, body)

    def scalar(a):
        with a.Fori(0, NG // 2) as i:
            for g in range(2):
                a.wait_ge(xt[g], i + 2)
                a.wait_ge(gated[g], i + 1)
                k.plain(a)
                nc.scalar.copy(stage[g][:, :], k.XT[:, bass.ds(i * 2 * GT + g * GT, GT)]).then_inc(staged[g], 1)
        a.wait_ge(centred, 1)
        nc.scalar.activation(pr[:, :, :], lg[:, :, :], ACT.Exp).then_inc(exped, 1)
        with a.Fori(0, NG // 2) as i:
            for g in range(2):
                a.wait_ge(turned[g], 2 * i + 1)
                nc.scalar.copy(wT[g][:, :], k.psum[0:E, g, :]).then_inc(wT_in[g], 1)

    def vector(v):
        c = Chain(v, own)
        with v.Fori(0, NG // 2) as i:
            for g in range(2):
                v.wait_ge(gated[g], i + 2)
                nc.vector.tensor_copy(lg[:, bass.ds(i * 2 * GROUP + g * GROUP, GROUP), :],
                                      k.psum[:, g, 0:GROUP * E].rearrange("p (n e) -> p n e", e=E)).then_inc(taken[g], 1)
        for g in range(2):
            v.wait_ge(taken[g], NG // 2 + 1)
        wide = lambda x: x[:, :].unsqueeze(2).to_broadcast([P, NT, E])
        c.step(nc.vector.tensor_reduce(m[:, :], lg[:, :, :], AXX, ALU.max))
        nc.vector.tensor_tensor(lg[:, :, :], lg[:, :, :], wide(m), ALU.subtract).then_inc(centred, 1)
        v.wait_ge(exped, 1)
        c.step(nc.vector.tensor_reduce(zs[:, :], pr[:, :, :], AXX, ALU.add))
        c.step(nc.vector.reciprocal(m[:, :], zs[:, :]))
        c.step(nc.vector.tensor_tensor(pr[:, :, :], pr[:, :, :], wide(m), ALU.mult))
        c.step(nc.vector.scalar_tensor_tensor(w[:, :, :], pr[:, :, :], THRESHOLD, pr[:, :, :], ALU.is_ge, ALU.mult))
        c.step(nc.vector.tensor_reduce(zs[:, :], w[:, :, :], AXX, ALU.add))
        c.step(nc.vector.scalar_tensor_tensor(zs[:, :], zs[:, :], 0.0, zs[:, :], ALU.is_equal, ALU.add))
        c.step(nc.vector.reciprocal(m[:, :], zs[:, :]))
        c.step(nc.vector.tensor_tensor(w[:, :, :], w[:, :, :], wide(m), ALU.mult))
        v.sem_inc(weighed, 1)
        c.restart()

        def add_bias(n, i, g):
            v.wait_ge(turned[g], 2 * i + 2)
            xs = k.X[:, bass.ds(i * 2 * GROUP + g * GROUP, GROUP), :]
            c.step(nc.vector.tensor_tensor(xs, xs, k.psum[:, g, :].rearrange("p (n d) -> p n d", d=D), ALU.add))
            c.restart()
            v.sem_inc(biased[g], 1)

        def add_experts(n, i, g, more=True):
            for pair in range(GROUP // 2):
                for h in range(HALVES):
                    v.wait_ge(expert[h], n * (GROUP // 2) + pair + 1)
                    k.plain(v)
                    for e in range(E // HALVES):
                        for u in range(2):
                            x1 = k.X[:, bass.ds(n * GROUP + pair * 2 + u, 1), :].rearrange("p n d -> p (n d)")
                            before = c.n - 1
                            if before > 0:
                                v.wait_ge(own, before)
                            c.do(nc.vector.scalar_tensor_tensor(x1, k.psum[:, 2 + 2 * h + u, e * D:(e + 1) * D],
                                                                wst[g][:, pair * 2 + u, h * (E // HALVES) + e:h * (E // HALVES) + e + 1],
                                                                x1, ALU.mult, ALU.add))
                    c.restart()
                    v.sem_inc(summed[h], 1)
            v.sem_inc(wst_free[g], 1)
            if more:
                add_bias(n + 1, i + g, 1 - g)

        add_bias(0, 0, 0)
        groups(v, add_experts)
        nc.vector.tensor_copy(m[:, 0:1], m[:, 0:1]).then_inc(k.layer_done, 1)

    k.add(sync=sync, vector=vector, scalar=scalar, tensor=tensor, gpsimd=gpsimd)


def test_time_mlp(k):
    nc, d, ctx = k.nc, k.dram, k.layer_ctx
    LR = 0.001
    ETA = LR * 2 / (B * D)
    TOL2 = (1e-4) ** 2
    T = P // B
    NCH = S // T
    SWEEPS = 3
    R = 3 * P
    wkv = k.sb("tt_wkv", [P, 2 * D], ctx=ctx)
    wq = k.sb("tt_wq", [P, D], ctx=ctx)
    WN = 3 * D + 2
    W1N = D + 1
    w0 = k.sb("tt_w0", [P, WN], ctx=ctx)
    ws = k.sb("tt_ws", [P, WN], ctx=ctx)
    earlier = k.sb("tt_earlier", [P, P], ctx=ctx)
    ones = k.sb("tt_ones", [P, 1], ctx=ctx)
    stage = [k.sb(f"tt_stage{g}", [P, B, T], ctx=ctx) for g in range(2)]
    kv = [k.sb(f"tt_kv{g}", [P, R], ctx=ctx) for g in range(2)]
    gm = [k.sb(f"tt_gm{g}", [P, P], ctx=ctx) for g in range(2)]
    sg, aT, sp, tsp, usp, pm, dyT, qm, dhT = (k.sb(f"tt_{n}", [P, P], ctx=ctx) for n in
                                               ("sg", "aT", "sp", "tsp", "usp", "pm", "dyT", "qm", "dhT"))
    rowb = [k.sb(f"tt_rows{g}", [P, R], ctx=ctx) for g in range(2)]
    diff, dsum, vsum, sqr = (k.sb(f"tt_{n}", [P, R], ctx=ctx) for n in ("diff", "dsum", "vsum", "sqr"))
    verdict = k.sb("tt_verdict", [P, 6], ctx=ctx)
    vrow = k.sb("tt_vrow", [1, 8], ctx=ctx)
    flag = k.sb("tt_flag", [1, 1], I32, ctx=ctx)
    w1, w2, w2t = (ws[:, o:o + D] for o in (0, D + 2, 2 * D + 2))
    b1, b2 = ws[:, D:D + 1], ws[:, D + 1:D + 2]
    bank = lambda n: k.psum[:, n, :]
    PREP, HB, PB, YB, QB, DB, TB, WB = range(8)
    w_in = k.sem("tt_w_in")
    layer = k.layers
    xt = layer_norm(k, "tt")
    xt_v = k.XT[:, :].rearrange("p (b c t) -> p b c t", b=B, c=NCH)

    def sync(s):
        if layer:
            s.wait_ge(k.layer_done, layer)
        for dst, src in ((wkv, "L1_attn_W_KV"), (wq, "L1_attn_W_Q"), (w0, "tt_w0"), (earlier, "tt_earlier"), (ones, "tt_ones")):
            s.dma_start(dst[:, :], d[src]).then_inc(w_in, 16)

    class Run:

        def __init__(self, tag, sweeps, unrolled):
            names = ("staged", "kv_psum", "kv_in", "gram", "gm_in", "h", "sig", "a", "gate", "p", "pm", "y", "dy", "q", "qm",
                     "da", "dh", "turned", "rows", "grads1", "grads2", "weights1", "weights2", "own", "p_own", "judged")
            self.sweeps, self.unrolled = sweeps, unrolled
            self.prep_at, self.gram_at = (1, 2) if unrolled else (0, 0)
            (self.staged, self.kv_psum, self.kv_in, self.gram, self.gm_in, self.h, self.sig, self.a, self.gate, self.p,
             self.pm, self.y, self.dy, self.q, self.qm, self.da, self.dh, self.turned, self.rows, self.grads1, self.grads2, self.weights1, self.weights2,
             self.own, self.p_own, self.judged) = (k.sem(f"tt{tag}_{n}") for n in names)

        def chunks(self, eng, first, body):
            first()
            with eng.Fori(0, NCH // 2 - 1) as i:
                body(2 * i, 0, True)
                body(2 * i + 1, 1, True)
            body(NCH - 2, 0, True)
            body(NCH - 1, 1, False)

        def each(self, eng, c, sweep):
            N = self.sweeps
            if self.unrolled:
                for s in range(N):
                    sweep(c * N + s, c * (N - 1) + s - 1 if s else None, s)
            else:
                sweep(c * N, None, 0)
                with eng.Fori(0, N - 1) as s:
                    sweep(c * N + s + 1, c * (N - 1) + s, -1)

        def buf(self, s):
            return rowb[s % 2 if self.unrolled else 0]

        def before(self, s):
            return rowb[(s - 1) % 2 if self.unrolled else 0]

        def tensor(self, t):
            def prep_a(c, g):
                t.wait_ge(self.staged, c + 1)
                for lhsT, rhs, o in ((wkv[:, 0:D], stage[g][:, :, :], 0), (wkv[:, D:2 * D], stage[g][:, :, :], P)):
                    nc.tensor.matmul(bank(PREP)[:, o:o + P], lhsT, rhs, start=True, stop=True)
                nc.tensor.matmul(bank(PREP)[:, 2 * P:3 * P], stage[g][:, :, :], wkv[:, 0:D], start=True, stop=True).then_inc(self.kv_psum, 1)

            def prep_b(c, g):
                t.wait_ge(self.kv_in, c + 1)
                nc.tensor.matmul(bank(PREP)[:, 3 * P:4 * P], kv[g][:, 0:P], kv[g][:, 0:P], start=True, stop=True).then_inc(self.gram, 1)

            def first():
                prep_a(0, 0)
                prep_b(0, 0)

            def body(c, g, more):
                def sweep(n, m, s):
                    if s == 0:
                        t.wait_ge(self.gm_in, c + 1)
                        t.wait_ge(self.weights1, c + 1)
                        nc.tensor.matmul(bank(HB)[:, 0:P], w1, kv[g][:, 0:P], start=True, stop=True).then_inc(self.h, 1)
                    else:
                        nc.tensor.matmul(bank(HB)[:, 0:P], w1, kv[g][:, 0:P], start=True, stop=False)
                        t.wait_ge(self.rows, n)
                        nc.tensor.matmul(bank(HB)[:, 0:P], self.before(s)[:, 2 * P:3 * P], gm[g][:, :], start=False,
                                         stop=True).then_inc(self.h, 1)
                    if s == self.prep_at and more:
                        prep_a(c + 1, 1 - g)
                    if self.unrolled and s == self.gram_at and more:
                        prep_b(c + 1, 1 - g)
                    t.wait_ge(self.a, n + 1)
                    if s == 0:
                        t.wait_ge(self.weights2, c + 1)
                    if s:
                        nc.tensor.matmul(bank(PB)[:, 0:P], aT[:, :], aT[:, :], start=True, stop=True).then_inc(self.p, 1)
                        nc.tensor.matmul(bank(YB)[:, 0:P], w2, aT[:, :], start=True, stop=False)
                        t.wait_ge(self.pm, m + 1)
                        nc.tensor.matmul(bank(YB)[:, 0:P], self.before(s)[:, P:2 * P], pm[:, :], start=False,
                                         stop=True).then_inc(self.y, 1)
                    else:
                        nc.tensor.matmul(bank(YB)[:, 0:P], w2, aT[:, :], start=True, stop=True).then_inc(self.y, 1)
                        if not self.unrolled and more:
                            prep_b(c + 1, 1 - g)
                    nc.tensor.transpose(bank(PB)[:, P:2 * P], aT[:, :], k.ident[:, :]).then_inc(self.turned, 1)
                    t.wait_ge(self.dy, n + 1)
                    if s:
                        nc.tensor.matmul(bank(QB)[:, 0:P], dyT[:, :], dyT[:, :], start=True, stop=True).then_inc(self.q, 1)
                        nc.tensor.matmul(bank(DB)[:, 0:P], w2t, dyT[:, :], start=True, stop=False)
                        t.wait_ge(self.qm, m + 1)
                        nc.tensor.matmul(bank(DB)[:, 0:P], self.before(s)[:, 0:P], qm[:, :], start=False,
                                         stop=True).then_inc(self.da, 1)
                    else:
                        nc.tensor.matmul(bank(DB)[:, 0:P], w2t, dyT[:, :], start=True, stop=True).then_inc(self.da, 1)
                    nc.tensor.transpose(bank(QB)[:, P:2 * P], dyT[:, :], k.ident[:, :]).then_inc(self.turned, 1)
                    t.wait_ge(self.dh, n + 1)
                    nc.tensor.transpose(bank(TB)[:, 0:P], dhT[:, :], k.ident[:, :]).then_inc(self.turned, 1)

                self.each(t, c, sweep)
                r = self.buf(self.sweeps - 1)
                t.wait_ge(self.rows, (c + 1) * self.sweeps)
                dh, dy, act = r[:, 2 * P:3 * P], r[:, P:2 * P], r[:, 0:P]
                nc.tensor.matmul(bank(QB)[:, 0:D], kv[g][:, 2 * P:3 * P], dh, start=True, stop=True)
                nc.tensor.matmul(bank(QB)[:, D:W1N], dh, ones[:, :], start=True, stop=True).then_inc(self.grads1, 1)
                nc.tensor.matmul(bank(WB)[:, 0:1], dy, ones[:, :], start=True, stop=True)
                nc.tensor.matmul(bank(WB)[:, 1:1 + D], act, dy, start=True, stop=True)
                nc.tensor.matmul(bank(WB)[:, 1 + D:1 + 2 * D], dy, act, start=True, stop=True).then_inc(self.grads2, 1)

            self.chunks(t, first, body)

        def scalar(self, a):
            def take_kv(c, g):
                a.wait_ge(self.kv_psum, c + 1)
                nc.scalar.copy(kv[g][:, :], bank(PREP)[:, 0:R]).then_inc(self.kv_in, 1)

            def body(c, g, more):
                def sweep(n, m, s):
                    a.wait_ge(self.h, n + 1)
                    nc.scalar.activation(sg[:, :], bank(HB)[:, 0:P], ACT.Sigmoid, bias=b1).then_inc(self.sig, 1)
                    if s == self.prep_at and more:
                        take_kv(c + 1, 1 - g)
                    if self.unrolled and s == 0:
                        a.wait_ge(self.judged, c + 1)
                    r = self.buf(s)
                    a.wait_ge(self.turned, 3 * n + (1 if self.unrolled else 3))
                    nc.scalar.copy(r[:, 0:P], bank(PB)[:, P:2 * P])
                    a.wait_ge(self.turned, 3 * n + (2 if self.unrolled else 3))
                    nc.scalar.mul(r[:, P:2 * P], bank(QB)[:, P:2 * P], -ETA)
                    a.wait_ge(self.turned, 3 * n + 3)
                    nc.scalar.mul(r[:, 2 * P:R], bank(TB)[:, 0:P], -ETA).then_inc(self.rows, 1)

                self.each(a, c, sweep)

            self.chunks(a, lambda: take_kv(0, 0), body)

        def gpsimd(self, p):
            c_ = Chain(p, self.p_own)

            def put_stage(c, g):
                k.plain(p)
                nc.gpsimd.tensor_copy(stage[g][:, :, :], xt_v[:, :, bass.ds(c, 1), :]).then_inc(self.staged, 1)

            def body(c, g, more):
                def sweep(n, m, s):
                    if not self.unrolled and s == 0 and more:
                        p.wait_ge(self.gm_in, c + 1)
                        put_stage(c + 1, 1 - g)
                    p.wait_ge(self.a, n + 1)
                    c_.do(nc.gpsimd.tensor_tensor(tsp[:, :], aT[:, :], sg[:, :], ALU.mult))
                    c_.do(nc.gpsimd.tensor_tensor(usp[:, :], aT[:, :], sg[:, :], ALU.add))
                    c_.sync()
                    c_.step(nc.gpsimd.tensor_tensor(sp[:, :], usp[:, :], tsp[:, :], ALU.subtract))
                    c_.restart()
                    p.sem_inc(self.gate, 1)
                    if self.unrolled and s == 0 and more:
                        p.wait_ge(self.gm_in, c + 1)
                        put_stage(c + 1, 1 - g)

                self.each(p, c, sweep)
                if self.unrolled:
                    new, old = self.buf(self.sweeps - 1), self.before(self.sweeps - 1)
                    p.wait_ge(self.rows, (c + 1) * self.sweeps)
                    c_.do(nc.gpsimd.tensor_tensor(diff[:, :], new[:, :], old[:, :], ALU.subtract))
                    c_.do(nc.gpsimd.tensor_tensor(sqr[:, :], new[:, :], new[:, :], ALU.mult))
                    c_.sync()
                    p.sem_inc(self.judged, 1)
                    c_.do(nc.gpsimd.tensor_tensor(diff[:, :], diff[:, :], diff[:, :], ALU.mult))
                    c_.do(nc.gpsimd.tensor_tensor(vsum[:, :], vsum[:, :], sqr[:, :], ALU.add))
                    c_.sync()
                    c_.step(nc.gpsimd.tensor_tensor(dsum[:, :], dsum[:, :], diff[:, :], ALU.add))
                    c_.restart()

            self.chunks(p, lambda: put_stage(0, 0), body)
            p.sem_inc(self.judged, 1)

        def vector(self, v):
            c_ = Chain(v, self.own)

            def take_gram(c, g):
                v.wait_ge(self.gram, c + 1)
                nc.vector.scalar_tensor_tensor(gm[g][:, :], bank(PREP)[:, 3 * P:4 * P], 1.0, earlier[:, :], ALU.add,
                                               ALU.mult).then_inc(self.gm_in, 1)

            def body(c, g, more):
                def sweep(n, m, s):
                    v.wait_ge(self.sig, n + 1)
                    nc.vector.scalar_tensor_tensor(aT[:, :], bank(HB)[:, 0:P], b1, sg[:, :], ALU.add, ALU.mult).then_inc(self.a, 1)
                    if s:
                        v.wait_ge(self.p, m + 1)
                        nc.vector.scalar_tensor_tensor(pm[:, :], bank(PB)[:, 0:P], 1.0, earlier[:, :], ALU.add, ALU.mult).then_inc(self.pm, 1)
                    v.wait_ge(self.y, n + 1)
                    if s == 0:
                        v.wait_ge(self.weights2, c + 1)
                    nc.vector.scalar_tensor_tensor(dyT[:, :], bank(YB)[:, 0:P], b2, kv[g][:, P:2 * P], ALU.add, ALU.subtract).then_inc(self.dy, 1)
                    if s:
                        v.wait_ge(self.q, m + 1)
                        nc.vector.scalar_tensor_tensor(qm[:, :], bank(QB)[:, 0:P], -ETA, earlier[:, :], ALU.mult, ALU.mult).then_inc(self.qm, 1)
                    if s == self.gram_at and more:
                        take_gram(c + 1, 1 - g)
                    v.wait_ge(self.gate, n + 1)
                    v.wait_ge(self.da, n + 1)
                    nc.vector.tensor_tensor(dhT[:, :], bank(DB)[:, 0:P], sp[:, :], ALU.mult).then_inc(self.dh, 1)

                self.each(v, c, sweep)
                v.wait_ge(self.grads1, c + 1)
                nc.vector.tensor_tensor(ws[:, 0:W1N], ws[:, 0:W1N], bank(QB)[:, 0:W1N], ALU.add).then_inc(self.weights1, 1)
                v.wait_ge(self.grads2, c + 1)
                nc.vector.tensor_tensor(ws[:, W1N:WN], ws[:, W1N:WN], bank(WB)[:, 0:WN - W1N], ALU.add).then_inc(self.weights2, 1)

            def first():
                nc.vector.tensor_copy(ws[:, 0:W1N], w0[:, 0:W1N]).then_inc(self.weights1, 1)
                nc.vector.tensor_copy(ws[:, W1N:WN], w0[:, W1N:WN]).then_inc(self.weights2, 1)
                take_gram(0, 0)

            self.chunks(v, first, body)
            v.wait_ge(self.weights1, NCH + 1)
            v.wait_ge(self.weights2, NCH + 1)

    fast = Run("f", SWEEPS, True)
    exact = Run("e", T, False)
    (zeroed, fold, summed, flagged, q_in, bias_row, own2, done_e) = (
        k.sem(f"tt_{n}") for n in ("zeroed", "fold", "summed", "flagged", "q_in", "bias_row", "own2", "done_e"))
    settle = k.sem("tt_settle")

    def branch(eng, run):
        eng.wait_ge(flagged, 1)
        redo = eng.value_load(flag[0:1, 0:1], min_val=0, max_val=1)
        with eng.If(redo != 0):
            run(eng)

    def vector_judge(v):
        c = Chain(v, own2)
        v.wait_ge(w_in, 80)
        fast.vector(v)
        v.wait_ge(fast.judged, NCH + 2)
        c.do(nc.vector.tensor_reduce(verdict[:, 0:3], dsum[:, :].rearrange("p (q r) -> p q r", q=3), AXX, ALU.add))
        c.do(nc.vector.tensor_reduce(verdict[:, 3:6], vsum[:, :].rearrange("p (q r) -> p q r", q=3), AXX, ALU.add))
        c.sync()
        v.sem_inc(summed, 1)
        v.wait_ge(fold, 1)
        tot = k.psum[0:1, PREP, 0:6]
        c.step(nc.vector.tensor_copy(vrow[:, 0:6], tot))
        c.step(nc.vector.scalar_tensor_tensor(vrow[:, 0:3], vrow[:, 3:6], TOL2, vrow[:, 0:3], ALU.mult, ALU.is_ge))
        c.step(nc.vector.tensor_scalar(vrow[:, 3:6], vrow[:, 3:6], 1e30, None, ALU.is_lt))
        c.step(nc.vector.tensor_tensor(vrow[:, 0:3], vrow[:, 0:3], vrow[:, 3:6], ALU.mult))
        c.step(nc.vector.tensor_tensor(vrow[:, 6:7], vrow[:, 0:1], vrow[:, 1:2], ALU.mult))
        c.step(nc.vector.tensor_tensor(vrow[:, 7:8], vrow[:, 6:7], vrow[:, 2:3], ALU.mult))
        nc.vector.tensor_scalar(flag[:, :], vrow[:, 7:8], -1.0, 1.0, ALU.mult, ALU.add).then_inc(flagged, 1)
        branch(v, exact.vector)

    b2row = k.sb("tt_b2row", [1, GT], ctx=ctx)
    qT = [k.sb(f"tt_qT{g}", [P, GT], ctx=ctx) for g in range(2)]
    sgq = [k.sb(f"tt_sgq{g}", [P, GT], ctx=ctx) for g in range(2)]
    aq = [k.sb(f"tt_aq{g}", [P, GT], ctx=ctx) for g in range(2)]
    q_psum, hq, sq, a_q, yq = ([k.sem(f"tt_{n}{g}") for g in range(2)] for n in ("q_psum", "hq", "sq", "a_q", "yq"))
    qT_in = [k.sem(f"tt_qT_in{g}") for g in range(2)]
    added = [k.free_sem(f"tt_added{g}") for g in range(2)]

    def vector(v):
        vector_judge(v)
        v.sem_inc(settle, 1)
        v.wait_ge(bias_row, 1)
        for n in range(GROUP):
            last = nc.vector.tensor_copy(b2row[:, n * D:(n + 1) * D], k.psum[0:1, WB, 0:D])
        last.then_inc(bias_row, 1)
        with v.Fori(0, NG // 2) as i:
            for g in range(2):
                v.wait_ge(sq[g], i + 1)
                nc.vector.scalar_tensor_tensor(aq[g][:, :], bank(2 + g), b1, sgq[g][:, :], ALU.add, ALU.mult).then_inc(a_q[g], 1)
            for g in range(2):
                v.wait_ge(yq[g], i + 1)
                xs = k.X[:, bass.ds(i * 2 * GROUP + g * GROUP, GROUP), :]
                nc.vector.tensor_tensor(xs, xs, bank(4 + g).rearrange("p (n d) -> p n d", d=D), ALU.add).then_inc(added[g], 1)
        for g in range(2):
            v.wait_ge(added[g], NG // 2 + 1)
        nc.vector.tensor_copy(vrow[:, 0:1], vrow[:, 0:1]).then_inc(k.layer_done, 1)

    def tensor(t):
        t.wait_ge(w_in, 80)
        fast.tensor(t)
        t.wait_ge(summed, 1)
        nc.tensor.matmul(k.psum[0:1, PREP, 0:6], ones[:, :], verdict[:, :], start=True, stop=True).then_inc(fold, 1)
        branch(t, exact.tensor)
        t.wait_ge(settle, 1)
        nc.tensor.transpose(k.psum[0:1, WB, 0:D], b2, k.ident[:, :]).then_inc(bias_row, 1)
        t.wait_ge(bias_row, 2)
        with t.Fori(0, NG // 2) as i:
            for g in range(2):
                t.wait_ge(added[g], i + 1)
                nc.tensor.matmul(bank(g), wq[:, :], k.XT[:, bass.ds(i * 2 * GT + g * GT, GT)], start=True, stop=True).then_inc(q_psum[g], 1)
            for g in range(2):
                t.wait_ge(qT_in[g], i + 1)
                nc.tensor.matmul(bank(2 + g), w1, qT[g][:, :], start=True, stop=True).then_inc(hq[g], 1)
            for g in range(2):
                t.wait_ge(a_q[g], i + 1)
                nc.tensor.matmul(bank(4 + g), k.ones_row[:, :], b2row[:, :], start=True, stop=True)
                for n in range(GROUP):
                    last = nc.tensor.matmul(bank(4 + g)[:, n * D:(n + 1) * D], aq[g][:, n * P:(n + 1) * P], w2,
                                            start=False, stop=True, skip_group_check=True)
                last.then_inc(yq[g], 1)

    def scalar(a):
        fast.scalar(a)
        branch(a, exact.scalar)
        a.wait_ge(settle, 1)
        with a.Fori(0, NG // 2) as i:
            for g in range(2):
                a.wait_ge(q_psum[g], i + 1)
                nc.scalar.copy(qT[g][:, :], bank(g)).then_inc(qT_in[g], 1)
            for g in range(2):
                a.wait_ge(hq[g], i + 1)
                nc.scalar.activation(sgq[g][:, :], bank(2 + g), ACT.Sigmoid, bias=b1).then_inc(sq[g], 1)

    def gpsimd(p):
        for g in range(2):
            p.wait_ge(xt[g], NG // 2 + 1)
        nc.gpsimd.memset(dsum[:, :], 0.0).then_inc(zeroed, 1)
        nc.gpsimd.memset(vsum[:, :], 0.0).then_inc(zeroed, 1)
        p.wait_ge(zeroed, 2)
        p.sem_inc(fast.judged, 1)
        fast.gpsimd(p)
        branch(p, exact.gpsimd)

    k.add(sync=sync, vector=vector, scalar=scalar, tensor=tensor, gpsimd=gpsimd)


def attention(k, tag, H, HD, blocked):
    nc, d, ctx = k.nc, k.dram, k.layer_ctx
    BLOCK = 64
    N = B * H
    DV = HD
    KR = 6 * HD
    MR = 96
    ROWS = MR + 3
    V1 = DV + 1
    V3 = 3 * V1
    LAG = 3
    NPT = LAG + 1
    BY_POOL, BY_DVE, WHOLE = (0, 1, 3, 5, 6), (4, 7), (2,)
    ROW_HALVES = (2, 3, 4, 4, 3, 0, 0, 0)
    LIFT = 12 * log(2)
    SCALE = float(HD) ** -0.5
    NTB = S // P
    w = {n: k.sb(f"{tag}_w{n}", [P, D], ctx=ctx) for n in "qkv"}
    bias = k.sb(f"{tag}_bias", [P, 3], ctx=ctx) if not blocked else None
    gamma_beta = k.sb(f"{tag}_gamma_beta", [P, 2], ctx=ctx) if not blocked else None
    x = {n: [k.sb(f"{tag}_x{n}{g}", [P, GT], ctx=ctx) for g in range(2)] for n in "qkv"}
    parts = {n: [k.sb(f"{tag}_p{n}{g}", [P, 3, GT], BF16, ctx=ctx) for g in range(2)] for n in "qk"}
    rest = {n: k.sb(f"{tag}_r{n}", [P, GT], ctx=ctx) for n in "qk"}
    vrows = k.sb(f"{tag}_vrows", [P, B, H, NTB, V1], ctx=ctx)
    NST = 4
    qs = [k.sb(f"{tag}_qs{g}", [P, S], BF16, ctx=ctx) for g in range(NST)]
    kst = [k.sb(f"{tag}_ks{g}", [P, S], BF16, ctx=ctx) for g in range(NST)]
    vparts = k.sb(f"{tag}_vparts", [P, N * NTB, 3, V1], BF16, ctx=ctx)
    vrest = k.sb(f"{tag}_vrest", [P, N * NTB, V1], ctx=ctx)
    vh = [k.sb(f"{tag}_vh{g}", [P, NTB, V1], ctx=ctx) for g in range(2)]
    v3 = [k.sb(f"{tag}_v3{g}", [P, NTB, 3, V1], BF16, ctx=ctx) for g in range(2)]
    pt = [k.sb(f"{tag}_pt{g}", [P, S], ctx=ctx) for g in range(NPT)]
    upper = [t_[:, :].bitcast(BF16).rearrange("p (s two) -> p two s", two=2)[:, 1, :] for t_ in pt]
    prest = [k.sb(f"{tag}_prest{g}", [P, S], F16, ctx=ctx) for g in range(NPT)]
    oT = [k.sb(f"{tag}_oT{g}", [V3, S], ctx=ctx) for g in range(2)]
    osum = k.sb(f"{tag}_osum", [P, NTB, V1], ctx=ctx)
    NM = 3 if blocked else 2
    mx = [k.sb(f"{tag}_mx{g}", [P, NTB, NM], ctx=ctx) for g in range(2)]
    m1 = k.sb(f"{tag}_m1", [P, 4, NTB], ctx=ctx)
    mp = k.sb(f"{tag}_mp", [P, NTB, 3], BF16, ctx=ctx)
    corr = [k.sb(f"{tag}_corr{g}", [P, NTB], ctx=ctx) for g in range(2)]
    dcorr = [k.sb(f"{tag}_dcorr{g}", [P, NTB], ctx=ctx) for g in range(2)]
    den = k.sb(f"{tag}_den", [P, NTB], ctx=ctx)
    onorm = k.sb(f"{tag}_onorm", [P, NTB, DV], ctx=ctx)
    stk = {n: nc.dram_tensor(f"{tag}_{n}stk", (N, KR, S), BF16, kind="Internal").ap() for n in "qk"}
    bank = lambda n: k.psum[:, n, :]
    mk = lambda n: k.sem(f"{tag}_{n}")
    pair = lambda n, free=False: [(k.free_sem if free else k.sem)(f"{tag}_{n}{g}") for g in range(2)]
    (w_in, ready_w, own, p_own) = map(mk, ("w_in", "ready_w", "own", "p_own"))
    qkv_psum, x_in, v_turned = pair("qkv_psum"), pair("x_in", True), pair("v_turned", True)
    split, stored, v_done = pair("split"), pair("stored", True), pair("v_done", True)
    hi_in = pair("hi_in")
    vh_in = pair("vh_in")
    loaded = [k.sem(f"{tag}_loaded{g}") for g in range(NST)]
    s_psum, s_read = pair("s_psum"), pair("s_read", True)
    st_psum, pt_in = pair("st_psum"), pair("pt_in", True)
    pv = [k.free_sem(f"{tag}_pv{g}") for g in range(NPT)]
    pv_all = lambda n: (pv[NPT - 1], n * (NTB // NPT) + 1)
    rest_v, rest_p, v_split = mk("rest_v"), mk("rest_p"), mk("v_split")
    oT_in = k.free_sem(f"{tag}_oT_in")
    all_done = mk("all_done")
    corr_used = k.free_sem(f"{tag}_corr_used")
    neg_in, m_turned, m_in, o_turned, head_done, corr_in, corr_exp = map(
        mk, ("neg_in", "m_turned", "m_in", "o_turned", "head_done", "corr_in", "corr_exp"))
    layer = k.layers
    if blocked:
        xt = layer_norm(k, tag)
        n_w = 3
        O = k.XT
    else:
        aff_in = k.sem(f"{tag}_aff_in")
        xt = layer_norm(k, tag, twice=True, affine=(gamma_beta[:, 0:1], gamma_beta[:, 1:2]), affine_in=(aff_in, 16))
        n_w = 5
        wv_full = k.sb(f"{tag}_wv_full", [P, D, 8], ctx=ctx)
        bv_full = k.sb(f"{tag}_bv_full", [P, 8], ctx=ctx)

    def loop(eng, first, body):
        def at(n, i, m, **ends):
            body(n, lambda r, ahead=0: (i * (NST // r) + (m + ahead) // r, (m + ahead) % r), **ends)
        first()
        at(0, 0, 0, begins=True)
        at(1, 0, 1)
        with eng.Fori(0, N // NST - 1) as i:
            for m in range(2, 2 + NST):
                at(i * NST + m, i, m)
        at(N - 2, 0, N - 2)
        at(N - 1, 0, N - 1, more=False)

    def sync(s):
        if layer:
            s.wait_ge(k.layer_done, layer)
        if blocked:
            for n in "qkv":
                s.dma_start(w[n][:, :], d[f"{tag}_w{n}"]).then_inc(w_in, 16)
        else:
            s.dma_start(gamma_beta[:, :], d[f"{tag}_gamma_beta"]).then_inc(aff_in, 16)
            for n in "qk":
                s.dma_start(w[n][:, :], d[f"{tag}_w{n}"]).then_inc(w_in, 16)
            s.dma_start(bias[:, 0:2], d[f"{tag}_bias"]).then_inc(w_in, 16)
            s.dma_start(wv_full[:, :, :], d["L2_attn_Wv"].rearrange("p (c u) -> p c u", u=8)).then_inc(w_in, 16)
            s.dma_start(bv_full[:, :], d["L2_attn_bv"].rearrange("(c u) -> c u", u=8)).then_inc(w_in, 16)
        order = {"q": (0, 0, 0, 1, 1, 2), "k": (0, 1, 2, 0, 1, 0)}
        with s.Fori(0, B) as i:
            for g in range(2):
                s.wait_ge(split[g], i + 1)
                k.plain(s)
                for n in "qk":
                    for blk, part in enumerate(order[n]):
                        dst = stk[n][bass.ds(i * H, H), blk * HD:(blk + 1) * HD, g * GT:(g + 1) * GT]
                        s.dma_start(dst, parts[n][g][:, part, :]).then_inc(stored[g], 16)
        for g in range(2):
            s.wait_ge(stored[g], B * 12 * 16 + 1)
        s.wait_ge(ready_w, 2)

        def load(n, g):
            s.dma_start(qs[g][0:KR, :], stk["q"][bass.ds(n, 1), :, :].rearrange("n r s -> (n r) s")).then_inc(loaded[g], 16)
            s.dma_start(kst[g][0:KR, :], stk["k"][bass.ds(n, 1), :, :].rearrange("n r s -> (n r) s")).then_inc(loaded[g], 16)

        for g in range(NST):
            load(g, g)
        with s.Fori(1, N // NST) as i:
            for g in range(NST):
                s.wait_ge(st_psum[1], (i * NST + g - NST + 1) * (NTB // 2))
                k.plain(s)
                load(NST * i + g, g)

    def tensor(t):
        t.wait_ge(ready_w, 2)
        t.wait_ge(k.ident16_in, 1)
        for g in range(2):
            t.wait_ge(xt[g], NG // 2 + 1)
        with t.Fori(0, B) as i:
            for g in range(2):
                t.wait_ge(x_in[g], i + 1)
                for z, n in enumerate("qkv"):
                    last = nc.tensor.matmul(bank(3 * g + z), w[n][:, :], k.XT[:, bass.ds(i * S + g * GT, GT)],
                                            start=True, stop=True)
                last.then_inc(qkv_psum[g], 1)
            for g in range(2):
                t.wait_ge(x_in[g], i + 2)
                t.wait_ge(v_done[g], i + 1)
                for n in range(GROUP):
                    last = nc.tensor.transpose(bank(6 + g)[:, n * P:(n + 1) * P], x["v"][g][:, n * P:(n + 1) * P], k.ident[:, :])
                last.then_inc(v_turned[g], 1)
        for g in range(2):
            t.wait_ge(v_done[g], B + 1)

        t.wait_ge(v_split, 1)

        def rows_scores(n, b, half):
            st, h = half // 2, half % 2
            t.wait_ge(s_read[h], n * NTB + st + 1)
            nc.tensor.matmul(bank(h), qs[b][0:KR, st * P:(st + 1) * P], kst[b][0:KR, h * 512:(h + 1) * 512],
                             start=True, stop=True).then_inc(s_psum[h], 1)

        def max_rows(n):
            t.wait_ge(neg_in, n + 1)
            for st in range(NTB):
                last = nc.tensor.matmul(k.psum[MR:ROWS, st // 4, (st % 4) * P:(st % 4 + 1) * P], mp[:, st, :], k.ident16[:, :],
                                        start=True, stop=True)
            last.then_inc(m_turned, 1)

        def values(n, g, tt, between=None):
            c, u = tt % 2, n * (NTB // 2) + tt // 2
            buf = tt % NPT
            t.wait_ge(pt_in[c], u + 2)
            if tt in BY_DVE:
                t.wait_ge(rest_v, n * len(BY_DVE) + BY_DVE.index(tt) + 1)
            if tt in BY_POOL:
                t.wait_ge(rest_p, n * len(BY_POOL) + BY_POOL.index(tt) + 1)
            if tt == 0:
                t.wait_ge(oT_in, n + 1)
            for h in range(2):
                cols = slice(h * 512, (h + 1) * 512)
                if tt in WHOLE:
                    last = nc.tensor.matmul(k.psum[0:V1, 6 + h, :], vh[g][:, tt, :], pt[buf][:, cols], start=False, stop=False,
                                            skip_group_check=True)
                else:
                    lhsT = v3[g][:, tt, :, :].rearrange("p q e -> p (q e)")
                    nc.tensor.matmul(k.psum[0:V3, 6 + h, :], lhsT, upper[buf][:, cols], start=tt == 0, stop=False)
                    last = nc.tensor.matmul(k.psum[0:V3, 6 + h, :], lhsT, prest[buf][:, cols], start=False, stop=tt == NTB - 1)
                if h == 0 and between:
                    between()
            last.then_inc(pv[buf], 1)

        def turn_out(n, g, more=True):
            t.wait_ge(oT_in, n + 2)
            t.wait_ge(s_read[0], (n + 3) * NTB + 1 if more else N * NTB + 1)
            k.plain(t)
            for r in range(NTB):
                src = oT[g][:, :].rearrange("p (a r) -> p r a", r=NTB)[:, r, :] if not blocked else oT[g][:, r * P:(r + 1) * P]
                last = nc.tensor.transpose(bank(0)[:, r * V3:(r + 1) * V3], src, k.ident[0:V3, 0:V3])
            last.then_inc(o_turned, 1)

        def first():
            t.wait_ge(loaded[0], 32)
            for half in range(2 * NTB):
                rows_scores(0, 0, half)
            max_rows(0)

        def body(n, turn, begins=False, more=True):
            (i, g), (used, b), (used_next, b_next) = turn(2), turn(NST), turn(NST, 1)
            done = 0

            def ahead(x, count):
                nonlocal done
                for _ in range(min(count, sum(ROW_HALVES[:x + 1]) - done) if more else 0):
                    rows_scores(n + 1, b_next, done)
                    done += 1

            for x in range(NTB):
                c, u = x % 2, n * (NTB // 2) + x // 2
                if x == 0 and not begins:
                    values(n - 1, 1 - g, x - LAG + NTB)
                if x == 0:
                    t.wait_ge(m_in, n + 1)
                    if more:
                        t.wait_ge(loaded[b_next], used_next * 32 + 32)
                if x == LAG:
                    t.wait_ge(vh_in[g], i + 1)
                t.wait_ge(pt_in[c], u + 1)
                for h in range(2):
                    last = nc.tensor.matmul(bank(2 + 2 * c + h), kst[b][0:ROWS, x * P:(x + 1) * P],
                                            qs[b][0:ROWS, h * 512:(h + 1) * 512], start=True, stop=True)
                last.then_inc(st_psum[c], 1)
                ahead(x, 1)
                if x >= LAG:
                    values(n, g, x - LAG, lambda: ahead(x, 1))
                elif x and not begins:
                    values(n - 1, 1 - g, x - LAG + NTB, lambda: ahead(x, 1))
                ahead(x, 2 * NTB)
                if x == NTB - 3 and not begins:
                    turn_out(n - 1, 1 - g, more)
                if x == NTB - 2 and more:
                    if not begins:
                        t.wait_ge(head_done, n)
                    max_rows(n + 1)

        loop(t, first, body)
        for tt in range(NTB - LAG, NTB):
            values(N - 1, 1, tt)
        t.wait_ge(head_done, N - 1)
        turn_out(N - 1, 1, more=False)
        t.wait_ge(head_done, N)

    def scalar(a):
        with a.Fori(0, B) as i:
            for g in range(2):
                a.wait_ge(qkv_psum[g], i + 1)
                a.wait_ge(v_turned[g], i + 1)
                a.wait_ge(stored[g], i * 192 + 1)
                for z, n in enumerate("qkv"):
                    if blocked:
                        last = nc.scalar.copy(x[n][g][:, :], bank(3 * g + z))
                    else:
                        last = nc.scalar.activation(x[n][g][:, :], bank(3 * g + z), ACT.Identity, bias=bias[:, z:z + 1])
                    last.then_inc(own_a, 1)
                a.wait_ge(own_a, 3)
                a.sem_clear(own_a)
                a.sem_inc(x_in[g], 1)
            for g in range(2):
                a.wait_ge(v_turned[g], i + 2)
                src = bank(6 + g).rearrange("p (n h e) -> p h n e", n=GROUP, h=H)
                dst = vrows[:, bass.ds(i, 1), :, g * GROUP:(g + 1) * GROUP, 0:DV]
                k.plain(a)
                for n in range(GROUP):
                    last = nc.scalar.copy(dst[:, :, :, n, :].rearrange("p o h e -> p (o h) e"), src[:, :, n, :])
                last.then_inc(v_done[g], 1)

        def max_in(n, b):
            a.wait_ge(m_turned, n + 1)
            nc.scalar.copy(qs[b][MR:ROWS, :], k.psum[MR:ROWS, 0:2, :].rearrange("p b s -> p (b s)")).then_inc(m_in, 1)

        def correction(n, g, begins):
            a.wait_ge(corr_in, n + 1)
            if not begins:
                a.wait_ge(corr_used, n)
            nc.scalar.activation(corr[g][:, :], dcorr[g][:, :], ACT.Exp, scale=SCALE).then_inc(corr_exp, 1)

        def take_out(n, g):
            a.wait_ge(*pv_all(n + 1))
            nc.scalar.copy(oT[g][:, :], k.psum[0:V3, 6:8, :].rearrange("p b s -> p (b s)")).then_inc(oT_in, 1)

        def body(n, turn, begins=False, more=True):
            g = turn(2)[1]
            for x in range(NTB):
                c, u = x % 2, n * (NTB // 2) + x // 2
                a.wait_ge(st_psum[c], u + 1)
                a.wait_ge(pv[x % NPT], n * (NTB // NPT) + x // NPT + 1)
                nc.scalar.activation(pt[x % NPT][:, :], k.psum[:, 2 + 2 * c:4 + 2 * c, :].rearrange("p b s -> p (b s)"), ACT.Exp,
                                     scale=SCALE).then_inc(pt_in[c], 1)
                if x == LAG - 1 and not begins:
                    take_out(n - 1, 1 - g)
                if x == NTB - 2 and more:
                    max_in(n + 1, turn(NST, 1)[1])
                if x == NTB // 2 and blocked:
                    correction(n, g, begins)

        loop(a, lambda: max_in(0, 0), body)
        take_out(N - 1, 1)

    own_a = mk("own_a")

    def gpsimd(p):
        c_ = Chain(p, p_own)
        for g in range(NST):
            c_.do(nc.gpsimd.memset(qs[g][:, :], 0.0))
            c_.do(nc.gpsimd.memset(kst[g][:, :], 0.0))
        c_.do(nc.gpsimd.memset(vrows[:, :, :, :, :], 0.0 if blocked else 1.0))
        c_.sync()
        for g in range(NST):
            c_.step(nc.gpsimd.memset(kst[g][MR:ROWS, :], 1.0))
        if blocked:
            for b in range(B):
                c_.step(nc.gpsimd.memset(vrows[P - BLOCK:P, b, :, NTB - 1, DV:V1], 1.0))
        c_.sync()
        c_.restart()
        p.sem_inc(ready_w, 1)
        for g in range(2):
            p.wait_ge(v_done[g], B + 1)

        p.wait_ge(v_split, 1)

        def stage_v(n, g, first=False):
            if not first:
                p.wait_ge(*pv_all(n - 1))
                k.plain(p)
            nc.gpsimd.tensor_copy(vh[g][:, :, :], vrows[:, :, :, :, :].rearrange("p b h n e -> p (b h) n e")[:, bass.ds(n, 1), :, :])
            nc.gpsimd.tensor_copy(v3[g][:, :, :, :].rearrange("p n q e -> p (n q e)"),
                                  vparts[:, bass.ds(n * NTB, NTB), :, :].rearrange("p n q e -> p (n q e)")).then_inc(vh_in[g], 1)

        def body(n, turn, begins=False, more=True):
            for x in BY_POOL:
                p.wait_ge(pt_in[x % 2], n * (NTB // 2) + x // 2 + 2)
                nc.gpsimd.tensor_tensor(prest[x % NPT][:, :], pt[x % NPT][:, :], upper[x % NPT], ALU.subtract).then_inc(rest_p, 1)
            if more:
                stage_v(n + 1, turn(2, 1)[1])

        loop(p, lambda: stage_v(0, 0, first=True), body)

    def vector(v):
        c_ = Chain(v, own)
        v.wait_ge(w_in, 16 * n_w)
        if not blocked:
            c_.do(nc.vector.tensor_reduce(w["v"][:, :], wv_full[:, :, :], AXX, ALU.add))
            c_.do(nc.vector.tensor_reduce(bias[:, 2:3], bv_full[:, :], AXX, ALU.add))
            c_.restart()
        v.sem_inc(ready_w, 1)
        for g in range(2):
            v.wait_ge(xt[g], NG // 2 + 1)
        with v.Fori(0, B) as i:
            for g in range(2):
                v.wait_ge(x_in[g], i + 2)
                v.wait_ge(stored[g], i * 192 + 1)
                for n in "qk":
                    c_.do(nc.vector.tensor_copy(parts[n][g][:, 0, :], x[n][g][:, :]))
                c_.sync()
                for n in "qk":
                    c_.do(nc.vector.tensor_tensor(rest[n][:, :], x[n][g][:, :], parts[n][g][:, 0, :], ALU.subtract))
                c_.sync()
                for n in "qk":
                    c_.do(nc.vector.tensor_copy(parts[n][g][:, 1, :], rest[n][:, :]))
                c_.sync()
                for n in "qk":
                    c_.do(nc.vector.tensor_tensor(parts[n][g][:, 2, :], rest[n][:, :], parts[n][g][:, 1, :], ALU.subtract))
                c_.sync()
                v.sem_inc(split[g], 1)
            c_.restart()
        for g in range(2):
            v.wait_ge(v_done[g], B + 1)
        v.wait_ge(ready_w, 2)
        vv = vrows[:, :, :, :, :].rearrange("p b h n e -> p (b h n) e")
        c_.step(nc.vector.tensor_copy(vparts[:, :, 0, :], vv))
        c_.step(nc.vector.tensor_tensor(vrest[:, :, :], vv, vparts[:, :, 0, :], ALU.subtract))
        c_.step(nc.vector.tensor_copy(vparts[:, :, 1, :], vrest[:, :, :]))
        c_.step(nc.vector.tensor_tensor(vparts[:, :, 2, :], vrest[:, :, :], vparts[:, :, 1, :], ALU.subtract))
        v.sem_inc(v_split, 1)
        c_.restart()

        def row_max(n, g, half):
            st, h = half // 2, half % 2
            v.wait_ge(s_psum[h], n * NTB + st + 1)
            if blocked and h == 1:
                c_.do(nc.vector.tensor_reduce(mx[g][:, st, 1:2], bank(1)[:, 0:512 - BLOCK], AXX, ALU.max))
                ins = nc.vector.tensor_reduce(mx[g][:, st, 2:3], bank(1)[:, 512 - BLOCK:512], AXX, ALU.max)
            else:
                ins = nc.vector.tensor_reduce(mx[g][:, st, h:h + 1], bank(h), AXX, ALU.max)
            ins.then_inc(s_read[h], 1)

        def negate(n, g):
            for h in range(2):
                v.wait_ge(s_read[h], (n + 1) * NTB + 1)
            c_.sync()
            prev, mm, r1 = m1[:, 0, :], m1[:, 1, :], m1[:, 2, :]
            c_.step(nc.vector.tensor_tensor(prev, mx[g][:, :, 0], mx[g][:, :, 1], ALU.max))
            if blocked:
                c_.step(nc.vector.tensor_tensor(mm, prev, mx[g][:, :, 2], ALU.max))
                nc.vector.tensor_tensor(dcorr[g][:, :], prev, mm, ALU.subtract).then_inc(corr_in, 1)
            else:
                mm = prev
            neg = m1[:, 3, :]
            c_.step(nc.vector.tensor_scalar(neg, mm, -1.0, LIFT / SCALE, ALU.mult, ALU.add))
            c_.step(nc.vector.tensor_copy(mp[:, :, 0], neg))
            c_.step(nc.vector.tensor_tensor(r1, neg, mp[:, :, 0], ALU.subtract))
            c_.step(nc.vector.tensor_copy(mp[:, :, 1], r1))
            nc.vector.tensor_tensor(mp[:, :, 2], r1, mp[:, :, 1], ALU.subtract).then_inc(neg_in, 1)
            c_.restart()

        def first():
            for half in range(2 * NTB):
                row_max(0, 0, half)
            negate(0, 0)

        def finish(n, g):
            v.wait_ge(o_turned, n + 1)
            k.plain(v)
            c_.step(nc.vector.tensor_reduce(osum[:, :, :], bank(0)[:, 0:NTB * V3].rearrange("p (r q e) -> p r e q", q=3, e=V1), AXX, ALU.add))
            v.sem_inc(head_done, 1)
            if blocked:
                v.wait_ge(corr_exp, n + 1)
                c_.step(nc.vector.scalar_tensor_tensor(den[:, :], corr[g][:, :], 1.0, osum[:, :, DV], ALU.add, ALU.mult))
                v.sem_inc(corr_used, 1)
                c_.step(nc.vector.reciprocal(den[:, :], den[:, :]))
                c_.step(nc.vector.tensor_tensor(O[:, bass.ds(n * (NTB * DV), NTB * DV)].rearrange("p (r e) -> p r e", e=DV),
                                                osum[:, :, 0:DV], den[:, :].unsqueeze(2).to_broadcast([P, NTB, DV]), ALU.mult))
            else:
                c_.step(nc.vector.reciprocal(den[:, :], osum[:, :, DV]))
                c_.step(nc.vector.tensor_tensor(onorm[:, :, :], osum[:, :, 0:DV], den[:, :].unsqueeze(2).to_broadcast([P, NTB, DV]), ALU.mult))
                xs = k.X[:, bass.ds(n, 1), :].rearrange("p n d -> p (n d)")
                c_.step(nc.vector.tensor_tensor(xs, xs, onorm[:, :, :].rearrange("p r e -> p (r e)"), ALU.add))
            c_.restart()

        def take_rest(n, x):
            v.wait_ge(pt_in[x % 2], n * (NTB // 2) + x // 2 + 2)
            nc.vector.tensor_tensor(prest[x % NPT][:, :], pt[x % NPT][:, :], upper[x % NPT], ALU.subtract).then_inc(rest_v, 1)

        def body(n, turn, begins=False, more=True):
            done, g = 0, turn(2)[1]
            for x in range(NTB):
                if x == 0 and not begins and NTB - 1 in BY_DVE:
                    take_rest(n - 1, NTB - 1)
                if more:
                    for _ in range(ROW_HALVES[x]):
                        row_max(n + 1, 1 - g, done)
                        done += 1
                if x - 1 in BY_DVE:
                    take_rest(n, x - 1)
                if x == NTB - 3 and more:
                    v.wait_ge(m_turned, n + 1)
                    if blocked and not begins:
                        v.wait_ge(corr_exp, n)
                    negate(n + 1, 1 - g)
                if x == NTB - 3 and not begins:
                    finish(n - 1, 1 - g)

        loop(v, first, body)
        take_rest(N - 1, NTB - 1)
        finish(N - 1, 1)
        if blocked:
            v.sem_inc(all_done, 1)
        else:
            nc.vector.tensor_copy(den[:, 0:1], den[:, 0:1]).then_inc(k.layer_done, 1)

    k.add(sync=sync, vector=vector, scalar=scalar, tensor=tensor, gpsimd=gpsimd)
    if blocked:
        project_out(k, tag, O, H, HD, all_done, 1)


def project_out(k, tag, O, H, HD, head_done, N):
    nc, d, ctx = k.nc, k.dram, k.layer_ctx
    NTB = S // P
    ow = k.sb(f"{tag}_ow", [P, D], ctx=ctx)
    ob = k.sb(f"{tag}_ob", [1, GT], ctx=ctx)
    stage = [k.sb(f"{tag}_ostage{g}", [P, GROUP, D], ctx=ctx) for g in range(2)]
    oT = [k.sb(f"{tag}_ooT{g}", [P, GT], ctx=ctx) for g in range(2)]
    w_in = k.sem(f"{tag}_ow_in")
    staged, oT_in, outp = ([k.sem(f"{tag}_{n}{g}") for g in range(2)] for n in ("ostaged", "ooT_in", "ooutp"))
    turned, added = ([k.free_sem(f"{tag}_{n}{g}") for g in range(2)] for n in ("oturned", "oadded"))
    Ov = O[:, :].rearrange("p (b h n e) -> p b n h e", b=B, h=H, n=NTB)

    def sync(s):
        s.dma_start(ow[:, :], d[f"{tag}_ow"]).then_inc(w_in, 16)
        s.dma_start(ob[:, :], d[f"{tag}_ob"]).then_inc(w_in, 16)

    def gpsimd(p):
        p.wait_ge(head_done, N)
        with p.Fori(0, B) as i:
            for g in range(2):
                p.wait_ge(turned[g], i + 1)
                k.plain(p)
                for n in range(GROUP):
                    last = nc.gpsimd.tensor_copy(stage[g][:, n, :].rearrange("p (h e) -> p h e", h=H),
                                                 Ov[:, bass.ds(i, 1), g * GROUP + n, :, :].rearrange("p b h e -> p (b h) e"))
                last.then_inc(staged[g], 1)

    def tensor(t):
        t.wait_ge(w_in, 32)
        with t.Fori(0, B) as i:
            for g in range(2):
                t.wait_ge(staged[g], i + 1)
                for n in range(GROUP):
                    last = nc.tensor.transpose(k.psum[:, g, n * P:(n + 1) * P], stage[g][:, n, :], k.ident[:, :])
                last.then_inc(turned[g], 1)
                t.wait_ge(oT_in[g], i + 1)
                t.wait_ge(added[g], i + 1)
                nc.tensor.matmul(k.psum[:, 2 + g, :], k.ones_row[:, :], ob[:, :], start=True, stop=True)
                for n in range(GROUP):
                    last = nc.tensor.matmul(k.psum[:, 2 + g, n * D:(n + 1) * D], oT[g][:, n * P:(n + 1) * P], ow[:, :],
                                            start=False, stop=True, skip_group_check=True)
                last.then_inc(outp[g], 1)

    def scalar(a):
        with a.Fori(0, B) as i:
            for g in range(2):
                a.wait_ge(turned[g], i + 2)
                nc.scalar.copy(oT[g][:, :], k.psum[:, g, :]).then_inc(oT_in[g], 1)

    def vector(v):
        with v.Fori(0, B) as i:
            for g in range(2):
                v.wait_ge(outp[g], i + 1)
                xs = k.X[:, bass.ds(i * 2 * GROUP + g * GROUP, GROUP), :]
                nc.vector.tensor_tensor(xs, xs, k.psum[:, 2 + g, :].rearrange("p (n d) -> p n d", d=D), ALU.add).then_inc(added[g], 1)
        for g in range(2):
            v.wait_ge(added[g], B + 1)
        nc.vector.memset(oT[0][0:1, 0:1], 0.0).then_inc(k.layer_done, 1)

    k.add(sync=sync, vector=vector, scalar=scalar, tensor=tensor, gpsimd=gpsimd)


def routed_ffn(k):
    nc, d, ctx = k.nc, k.dram, k.layer_ctx
    E, _, HID = d["L3_ffn_w1"].shape
    G, KEEP, K = 4, 2, 2
    PAIR = NT * K
    sw1, sw2, sw3 = (k.sb(f"rf_sw{n}", [P, D], ctx=ctx) for n in (1, 2, 3))
    gw = k.sb("rf_gw", [P, E], ctx=ctx)
    eb = k.sb("rf_eb", [P, E], ctx=ctx)
    w13 = k.sb("rf_w13", [P, E, 2 * HID], ctx=ctx)
    w2 = k.sb("rf_w2", [HID, E, D], ctx=ctx)
    consts = k.sb("rf_consts", [P, G * G + E * E + PAIR + E * K * E + 2 + P], ctx=ctx)
    o0 = 0
    def const(n):
        nonlocal o0
        o0 += n
        return consts[:, o0 - n:o0]
    tri4, tri8, pos, delta, half, ones = const(G * G), const(E * E), const(PAIR), const(E * K * E), const(2), const(P)
    assert o0 == consts.shape[1], o0
    stage = [k.sb(f"rf_stage{g}", [P, GT], ctx=ctx) for g in range(2)]
    sg = [k.sb(f"rf_sg{g}", [P, GT], ctx=ctx) for g in range(2)]
    g1 = [k.sb(f"rf_g1{g}", [P, GT], ctx=ctx) for g in range(2)]
    uT = [k.sb(f"rf_uT{g}", [P, GT], ctx=ctx) for g in range(2)]
    lg, pr, sc = (k.sb(f"rf_{n}", [P, NT, E], ctx=ctx) for n in ("lg", "pr", "sc"))
    m = k.sb("rf_m", [P, NT], ctx=ctx)
    gs, gc, keep = (k.sb(f"rf_{n}", [P, NT, G], ctx=ctx) for n in ("gs", "gc", "keep"))
    gg, ge = (k.sb(f"rf_{n}", [P, NT, G, G], ctx=ctx) for n in ("gg", "ge"))
    ee, eq = (k.sb(f"rf_{n}", [P, NT, E, E], ctx=ctx) for n in ("ee", "eq"))
    cnt, keep8 = (k.sb(f"rf_{n}", [P, NT, E], ctx=ctx) for n in ("cnt", "keep8"))
    oh = k.sb("rf_oh", [P, NT, K, E], ctx=ctx)
    ohp = k.sb("rf_ohp", [P, NT, K, E], ctx=ctx)
    wts = k.sb("rf_wts", [P, NT, K], ctx=ctx)
    sel = k.sb("rf_sel", [P, NT, E], ctx=ctx)
    local = k.sb("rf_local", [P, E], ctx=ctx)
    offs = k.sb("rf_offs", [P, E], ctx=ctx)
    gx = k.sb("rf_gx", [P, PAIR, E + 1], ctx=ctx)
    ghot = k.sb("rf_ghot", [P, PAIR, E], ctx=ctx)
    spots = k.sb("rf_spots", [P, NT, K, E, E], ctx=ctx)
    xg = k.sb("rf_xg", [P, E, K * E, E], ctx=ctx)
    table = k.sb("rf_table", [P, K, 2 * HID], ctx=ctx)
    zero = k.sb("rf_zero", [P, P], ctx=ctx)
    ost = [k.sb(f"rf_ost{g}", [P, GROUP, P], ctx=ctx) for g in range(2)]
    oht = [k.sb(f"rf_oht{g}", [P, GT], ctx=ctx) for g in range(2)]
    wst = [k.sb(f"rf_wst{g}", [P, GROUP * K], ctx=ctx) for g in range(2)]
    wa = [k.sb(f"rf_wa{g}", [P, GROUP * K, 2 * HID], ctx=ctx) for g in range(2)]
    sh = [k.sb(f"rf_sh{g}", [P, GROUP * K, HID], ctx=ctx) for g in range(2)]
    th = [k.sb(f"rf_th{g}", [P, GROUP * K, HID], ctx=ctx) for g in range(2)]
    hh = [k.sb(f"rf_hh{g}", [P, GROUP * K, HID], ctx=ctx) for g in range(2)]
    hs = k.sb("rf_hs", [P, 2, HID], ctx=ctx)
    ht = k.sb("rf_ht", [HID, 2, E * E], ctx=ctx)
    pair = lambda n, free=False: [(k.free_sem if free else k.sem)(f"rf_{n}{g}") for g in range(2)]
    one = lambda n: k.sem(f"rf_{n}")
    w_in, own, p_own, centred, exped, counted, counts, xg_in, table_ps, table_in, routed, zeroed, folded, hs_in, ht_ps, ht_in, last_ps = map(
        one, ("w_in", "own", "p_own", "centred", "exped", "counted", "counts", "xg_in", "table_ps", "table_in", "routed",
              "zeroed", "folded", "hs_in", "ht_ps", "ht_in", "last_ps"))
    staged, hid, sig, u_in, outp = pair("staged"), pair("hid"), pair("sig"), pair("u_in", True), pair("outp", True)
    gated, taken, added = pair("gated", True), pair("taken", True), pair("added", True)
    spot_in, spot_t, oht_in, looked = pair("spot_in"), pair("spot_t"), pair("oht_in"), pair("looked")
    scaled, sig2, h_in, fold, th_in = pair("scaled", True), pair("sig2"), pair("h_in"), pair("fold", True), pair("th_in")
    layer = k.layers
    xt = layer_norm(k, "rf")
    bank = lambda n: k.psum[:, n, :]

    def sync(s):
        if layer:
            s.wait_ge(k.layer_done, layer)
        for dst, src in ((sw1, "rf_sw1"), (sw2, "rf_sw2"), (sw3, "rf_sw3"), (gw, "rf_gw"), (eb, "rf_eb"), (consts, "rf_consts")):
            s.dma_start(dst[:, :], d[src]).then_inc(w_in, 16)
        s.dma_start(w13[:, :, :], d["rf_w13"]).then_inc(w_in, 16)
        s.dma_start(w2[:, :, :], d["rf_w2"]).then_inc(w_in, 16)

    def gpsimd(p):
        c = Chain(p, p_own)
        for g in range(2):
            p.wait_ge(xt[g], NG // 2 + 1)
        with p.Fori(0, NG // 2) as i:
            for g in range(2):
                p.wait_ge(gated[g], i + 1)
                k.plain(p)
                nc.gpsimd.tensor_copy(stage[g][:, :], k.XT[:, bass.ds(i * 2 * GT + g * GT, GT)]).then_inc(staged[g], 1)
        nc.gpsimd.memset(zero[:, :], 0.0).then_inc(zeroed, 1)
        p.wait_ge(routed, 1)
        with p.Fori(0, NG // 2) as i:
            for g in range(2):
                p.wait_ge(fold[g], i + 1)
                p.wait_ge(scaled[g], i + 1)
                k.plain(p)
                at = bass.ds(i * 2 * GROUP + g * GROUP, GROUP)
                nc.gpsimd.tensor_copy(ost[g][:, :, :], spots[:, at, :, :, :].rearrange("p n q g e -> p n (q g e)"))
                nc.gpsimd.tensor_copy(wst[g][:, :], wts[:, at, :].rearrange("p n q -> p (n q)")).then_inc(spot_in[g], 1)
            for g in range(2):
                p.wait_ge(sig2[g], i + 1)
                c.step(nc.gpsimd.tensor_tensor(th[g][:, :, :], wa[g][:, :, 0:HID], sh[g][:, :, :], ALU.mult))
                nc.gpsimd.tensor_tensor(hh[g][:, :, :], th[g][:, :, :], wa[g][:, :, HID:2 * HID], ALU.mult).then_inc(h_in[g], 1)
            c.restart()

    def tensor(t):
        t.wait_ge(w_in, 128)
        for g in range(2):
            t.wait_ge(xt[g], NG // 2 + 1)
        with t.Fori(0, NG // 2) as i:
            for g in range(2):
                t.wait_ge(u_in[g], i + 1)
                x = k.XT[:, bass.ds(i * 2 * GT + g * GT, GT)]
                nc.tensor.matmul(bank(2 * g), sw1[:, :], x, start=True, stop=True)
                nc.tensor.matmul(bank(2 * g + 1), sw3[:, :], x, start=True, stop=True).then_inc(hid[g], 1)
            for g in range(2):
                t.wait_ge(staged[g], i + 1)
                t.wait_ge(taken[g], i + 1)
                for n in range(GROUP):
                    last = nc.tensor.matmul(bank(4 + g)[:, n * E:(n + 1) * E], stage[g][:, n * P:(n + 1) * P], gw[:, :],
                                            start=True, stop=True)
                last.then_inc(gated[g], 1)
            for g in range(2):
                t.wait_ge(u_in[g], i + 2)
                t.wait_ge(added[g], i + 1)
                for n in range(GROUP):
                    last = nc.tensor.matmul(bank(6 + g)[:, n * D:(n + 1) * D], uT[g][:, n * P:(n + 1) * P], sw2[:, :],
                                            start=True, stop=True)
                last.then_inc(outp[g], 1)
        t.wait_ge(xg_in, 1)
        for g in range(2):
            t.wait_ge(u_in[g], NG // 2 + 1)
            t.wait_ge(taken[g], NG // 2 + 1)
            t.wait_ge(added[g], NG // 2 + 1)
        for e in range(E):
            last = nc.tensor.matmul(bank(0)[:, 0:2 * HID], xg[:, e, :, :].rearrange("p q e -> p (q e)"), w13[:, e, :],
                                    start=e == 0, stop=e == E - 1)
        last.then_inc(table_ps, 1)
        t.wait_ge(counted, 1)
        nc.tensor.matmul(bank(1)[:, 0:E], ones, local[:, :], start=True, stop=True).then_inc(counts, 1)
        t.wait_ge(zeroed, 1)
        nc.tensor.matmul(bank(7)[:, 0:P], zero[:, :], zero[:, :], start=True, stop=True)
        t.wait_ge(table_in, 1)
        t.wait_ge(routed, 1)
        with t.Fori(0, NG // 2) as i:
            for g in range(2):
                t.wait_ge(spot_in[g], i + 1)
                for n in range(GROUP):
                    last = nc.tensor.transpose(bank(5 + g)[:, n * P:(n + 1) * P], ost[g][:, n, :], k.ident[:, :])
                last.then_inc(spot_t[g], 1)
            for g in range(2):
                t.wait_ge(oht_in[g], i + 1)
                t.wait_ge(scaled[g], i + 1)
                for n in range(GROUP):
                    last = nc.tensor.matmul(k.psum[:, 2 * g + n // 2, (n % 2) * 2 * P:(n % 2 + 1) * 2 * P],
                                            oht[g][:, n * P:(n + 1) * P], table[:, :, :].rearrange("p q h -> p (q h)"),
                                            start=True, stop=True)
                last.then_inc(looked[g], 1)
            for g in range(2):
                t.wait_ge(h_in[g], i + 1)
                for n in range(GROUP):
                    last = nc.tensor.matmul(bank(7)[:, 0:P], ost[g][:, n, :], hh[g][:, n * K:(n + 1) * K, :].rearrange("p q h -> p (q h)"),
                                            start=False, stop=True, skip_group_check=True)
                last.then_inc(fold[g], 1)
        t.wait_ge(fold[0], NG // 2 + 1)
        t.wait_ge(fold[1], NG // 2 + 1)
        t.sem_inc(folded, 1)
        t.wait_ge(hs_in, 1)
        nc.tensor.transpose(k.psum[0:HID, 0, 0:P], hs[:, 0, :], k.ident[:, :]).then_inc(ht_ps, 1)
        t.wait_ge(ht_in, 1)
        for e in range(E):
            last = nc.tensor.matmul(k.psum[0:E, 1, 0:D], ht[:, 0, e * E:(e + 1) * E], w2[:, e, :], start=e == 0, stop=e == E - 1)
        last.then_inc(last_ps, 1)

    def scalar(a):
        with a.Fori(0, NG // 2) as i:
            for g in range(2):
                a.wait_ge(hid[g], i + 1)
                nc.scalar.activation(sg[g][:, :], bank(2 * g), ACT.Sigmoid).then_inc(sig[g], 1)
        a.wait_ge(centred, 1)
        nc.scalar.activation(pr[:, :, :], lg[:, :, :], ACT.Exp).then_inc(exped, 1)
        with a.Fori(0, NG // 2) as i:
            for g in range(2):
                a.wait_ge(spot_t[g], i + 1)
                nc.scalar.copy(oht[g][:, :], bank(5 + g)).then_inc(oht_in[g], 1)
            for g in range(2):
                a.wait_ge(scaled[g], i + 2)
                nc.scalar.activation(sh[g][:, :, :], wa[g][:, :, 0:HID], ACT.Sigmoid).then_inc(sig2[g], 1)

    def vector(v):
        c = Chain(v, own)
        V = nc.vector
        with v.Fori(0, NG // 2) as i:
            for g in range(2):
                v.wait_ge(sig[g], i + 1)
                c.step(V.tensor_tensor(g1[g][:, :], bank(2 * g), sg[g][:, :], ALU.mult))
                c.step(V.tensor_tensor(uT[g][:, :], bank(2 * g + 1), g1[g][:, :], ALU.mult))
                v.sem_inc(u_in[g], 1)
            for g in range(2):
                v.wait_ge(gated[g], i + 2)
                V.tensor_copy(lg[:, bass.ds(i * 2 * GROUP + g * GROUP, GROUP), :],
                              bank(4 + g)[:, 0:GROUP * E].rearrange("p (n e) -> p n e", e=E)).then_inc(taken[g], 1)
            for g in range(2):
                v.wait_ge(outp[g], i + 2)
                xs = k.X[:, bass.ds(i * 2 * GROUP + g * GROUP, GROUP), :]
                V.tensor_tensor(xs, xs, bank(6 + g).rearrange("p (n d) -> p n d", d=D), ALU.add).then_inc(added[g], 1)
            c.restart()
        for g in range(2):
            v.wait_ge(taken[g], NG // 2 + 1)
            v.wait_ge(added[g], NG // 2 + 1)
        v.wait_ge(w_in, 128)
        V.tensor_tensor(xg[:, :, :, :].rearrange("p g q e -> p (g q) e"), k.XT[:, 0:E].unsqueeze(1).to_broadcast([P, E * K * E, E]),
                        delta.unsqueeze(2).to_broadcast([P, E * K * E, E]), ALU.mult).then_inc(xg_in, 1)
        wide = lambda x: x.unsqueeze(2).to_broadcast([P, NT, E])
        c.step(V.tensor_reduce(m[:, :], lg[:, :, :], AXX, ALU.max))
        V.tensor_tensor(lg[:, :, :], lg[:, :, :], wide(m[:, :]), ALU.subtract).then_inc(centred, 1)
        v.wait_ge(exped, 1)
        c.step(V.tensor_reduce(m[:, :], pr[:, :, :], AXX, ALU.add))
        c.step(V.reciprocal(m[:, :], m[:, :]))
        c.step(V.tensor_tensor(pr[:, :, :], pr[:, :, :], wide(m[:, :]), ALU.mult))
        c.step(V.tensor_tensor(sc[:, :, :], pr[:, :, :], eb[:, :].unsqueeze(1).to_broadcast([P, NT, E]), ALU.add))
        s2 = sc[:, :, :].rearrange("p n (g e) -> p n g e", g=G)
        c.step(V.tensor_tensor(gs[:, :, :], s2[:, :, :, 0], s2[:, :, :, 1], ALU.add))
        other = gs[:, :, :].unsqueeze(2).to_broadcast([P, NT, G, G])
        this = gs[:, :, :].unsqueeze(3).to_broadcast([P, NT, G, G])
        c.do(V.tensor_tensor(gg[:, :, :, :], other, this, ALU.is_gt))
        c.do(V.tensor_tensor(ge[:, :, :, :], other, this, ALU.is_equal))
        c.sync()
        flat = lambda x: x[:, :, :, :].rearrange("p n a b -> p n (a b)")
        c.step(V.tensor_tensor(flat(ge), flat(ge), tri4.unsqueeze(1).to_broadcast([P, NT, G * G]), ALU.mult))
        c.step(V.tensor_tensor(flat(gg), flat(gg), flat(ge), ALU.add))
        c.step(V.tensor_reduce(gc[:, :, :], gg[:, :, :, :], AXX, ALU.add))
        c.step(V.tensor_scalar(keep[:, :, :], gc[:, :, :], float(KEEP), None, ALU.is_lt))
        c.step(V.tensor_copy(keep8[:, :, :].rearrange("p n (g e) -> p n g e", g=G), keep[:, :, :].unsqueeze(3).to_broadcast([P, NT, G, E // G])))
        other = sc[:, :, :].unsqueeze(2).to_broadcast([P, NT, E, E])
        this = sc[:, :, :].unsqueeze(3).to_broadcast([P, NT, E, E])
        c.do(V.tensor_tensor(ee[:, :, :, :], other, this, ALU.is_gt))
        c.do(V.tensor_tensor(eq[:, :, :, :], other, this, ALU.is_equal))
        c.sync()
        c.step(V.tensor_tensor(flat(eq), flat(eq), tri8.unsqueeze(1).to_broadcast([P, NT, E * E]), ALU.mult))
        c.step(V.tensor_tensor(flat(ee), flat(ee), flat(eq), ALU.add))
        c.step(V.tensor_tensor(ee[:, :, :, :], ee[:, :, :, :], keep8[:, :, :].unsqueeze(2).to_broadcast([P, NT, E, E]), ALU.mult))
        c.step(V.tensor_reduce(cnt[:, :, :], ee[:, :, :, :], AXX, ALU.add))
        for q in range(K):
            c.do(V.scalar_tensor_tensor(oh[:, :, q, :], cnt[:, :, :], float(q), keep8[:, :, :], ALU.is_equal, ALU.mult))
        c.sync()
        for q in range(K):
            c.do(V.tensor_tensor(ohp[:, :, q, :], oh[:, :, q, :], pr[:, :, :], ALU.mult))
        c.step(V.tensor_tensor(sel[:, :, :], oh[:, :, 0, :], oh[:, :, 1, :], ALU.add))
        c.step(V.tensor_reduce(wts[:, :, :], ohp[:, :, :, :], AXX, ALU.add))
        V.tensor_reduce(local[:, :], sel[:, :, :].rearrange("p n e -> p e n"), AXX, ALU.add).then_inc(counted, 1)
        v.wait_ge(table_ps, 1)
        for q in range(K):
            last = V.tensor_scalar(table[:, q, :], bank(0)[:, 0:2 * HID], half[:, q:q + 1], None, ALU.mult)
            last.then_inc(own, 1)
            c.n += 1
        c.sync()
        v.sem_inc(table_in, 1)
        v.wait_ge(counts, 1)
        c.step(V.tensor_copy(offs[:, :], bank(1)[:, 0:E]))
        for e in range(1, E):
            c.step(V.tensor_tensor(offs[:, e:e + 1], offs[:, e - 1:e], offs[:, e:e + 1], ALU.add))
        c.do(V.memset(gx[:, :, 0:1], 1.0))
        c.do(V.tensor_tensor(gx[:, :, 1:E + 1], pos.unsqueeze(2).to_broadcast([P, PAIR, E]),
                             offs[:, :].unsqueeze(1).to_broadcast([P, PAIR, E]), ALU.is_ge))
        c.sync()
        c.step(V.tensor_tensor(ghot[:, :, :], gx[:, :, 0:E], gx[:, :, 1:E + 1], ALU.subtract))
        c.step(V.tensor_tensor(spots[:, :, :, :, :].rearrange("p n q g e -> p (n q) g e"), ghot[:, :, :].unsqueeze(3).to_broadcast([P, PAIR, E, E]),
                               oh[:, :, :, :].rearrange("p n q e -> p (n q) e").unsqueeze(2).to_broadcast([P, PAIR, E, E]), ALU.mult))
        v.sem_inc(routed, 1)
        c.restart()
        with v.Fori(0, NG // 2) as i:
            for g in range(2):
                v.wait_ge(looked[g], i + 1)
                V.tensor_tensor(wa[g][:, :, :], k.psum[:, 2 * g:2 * g + 2, :].rearrange("p b (q h) -> p (b q) h", h=2 * HID),
                                wst[g][:, :].unsqueeze(2).to_broadcast([P, GROUP * K, 2 * HID]), ALU.mult).then_inc(scaled[g], 1)
        v.wait_ge(folded, 1)
        c.step(V.tensor_scalar(hs[:, 1, :], bank(7)[:, 0:HID], half[:, 0:1], None, ALU.mult))
        V.scalar_tensor_tensor(hs[:, 0, :], bank(7)[:, HID:2 * HID], half[:, 1:2], hs[:, 1, :], ALU.mult, ALU.add).then_inc(hs_in, 1)
        v.wait_ge(ht_ps, 1)
        c.step(V.tensor_copy(ht[:, 1, :], k.psum[0:HID, 0, 0:E * E]))
        V.tensor_tensor(ht[:, 0, :], k.psum[0:HID, 0, E * E:K * E * E], ht[:, 1, :], ALU.add).then_inc(ht_in, 1)
        v.wait_ge(last_ps, 1)
        c.step(V.tensor_tensor(k.X[0:E, 0, :], k.X[0:E, 0, :], k.psum[0:E, 1, 0:D], ALU.add))
        V.memset(m[:, 0:1], 0.0).then_inc(k.layer_done, 1)

    k.add(sync=sync, vector=vector, scalar=scalar, tensor=tensor, gpsimd=gpsimd)


BUILDERS = {7: routed_ffn, 4: lambda k: attention(k, "sa", 8, 16, False), 6: lambda k: attention(k, "ba", 16, 8, True),
            2: test_time_mlp, 3: dense_experts, 5: channel_mix, 0: delta_net, 1: sine_ffn}


def build(nc, dram, out):
    with ExitStack() as ctx:
        k = Core(nc, ctx, dram)
        stored = k.sem("stored")

        def halves(g):
            g.wait_ge(k.consts_in, 64)
            nc.gpsimd.tensor_copy(k.ident16[:, :], k.ident[:, :]).then_inc(k.ident16_in, 1)

        k.add(gpsimd=halves)

        def load(s):
            s.dma_start(k.mhalf[:, :], dram["mhalf"]).then_inc(k.consts_in, 16)
            s.dma_start(k.X[:, :, :], dram["L0_attn_x"].rearrange("b (t p) d -> p (b t) d", p=P)).then_inc(k.consts_in, 16)
            s.dma_start(k.ident[:, :], dram["ident"]).then_inc(k.consts_in, 16)
            s.dma_start(k.ones_row[:, :], dram["ones_row"]).then_inc(k.consts_in, 16)

        k.add(sync=load)
        arrived, opened = {e: k.sem(f"arrived_{e}") for e in k.programs}, k.sem("opened")
        kept = []
        contexts = {}

        def turn_over(s, n):
            if n:
                for e in k.programs:
                    s.wait_ge(arrived[e], n)
                s.wait_ge(k.layer_done, n)
                for x in kept[n - 1][0]:
                    s.sem_clear(x)
            for m in (n + 1,) if n else (0, 1):
                if m < len(kept):
                    for f in kept[m][1]:
                        s.sem_inc(f, 1)
                    s.sem_inc(opened, 1)

        for n, which in enumerate(LAYERS):
            if n >= 2:
                contexts[n - 2].close()
            k.sem_ctx = contexts[n] = ExitStack()
            k.layer_sems, k.free = [], []
            for e in k.programs:
                if e == "sync":
                    k.programs[e].append(lambda s, n=n: turn_over(s, n))
                k.programs[e].append(lambda eng, n=n: eng.wait_ge(opened, n + 1))
            with ExitStack() as layer_ctx:
                k.layer_ctx = layer_ctx
                BUILDERS[which](k)
                k.layers += 1
            kept.append((k.layer_sems, k.free))
            for e in k.programs:
                k.programs[e].append(lambda eng, e=e: eng.sem_inc(arrived[e], 1))
        n_layers = k.layers

        def store(s):
            s.wait_ge(k.layer_done, n_layers)
            s.dma_start(out.rearrange("b (t p) d -> p (b t) d", p=P), k.X[:, :, :]).then_inc(stored, 16)
            s.wait_ge(stored, 16)

        k.add(sync=store)
        block = ctx.enter_context(nc.Block())

        @block.sync
        def _(s):
            for f in k.programs["sync"]:
                f(s)

        @block.tensor
        def _(t):
            for f in k.programs["tensor"]:
                f(t)

        @block.scalar
        def _(a):
            for f in k.programs["scalar"]:
                f(a)

        @block.vector
        def _(v):
            for f in k.programs["vector"]:
                f(v)

        @block.gpsimd
        def _(g):
            for f in k.programs["gpsimd"]:
                f(g)


def lay_out(inputs):
    f = np.float32
    a = {n: np.ascontiguousarray(v) for n, v in inputs.items()}
    a["mhalf"] = np.full((P, P), -0.5, f)
    a["ident"] = np.eye(P, dtype=f)
    a["ones_row"] = np.ones((1, P), f)
    col = lambda n: a[n].reshape(-1, P).T
    a["sf_cols"] = np.ascontiguousarray(np.stack([col("L0_ffn_b1"), col("L0_ffn_quantum_phases"),
                                                  col("L0_ffn_quantum_weights_real"), col("L0_ffn_quantum_weights_imag")], 1))
    a["sf_b2"] = np.tile(a["L0_ffn_b2"], GROUP)[None]
    a["dn_wqkv"] = np.concatenate([a[f"L0_attn_W{n}"] for n in "kqvb"], 1)
    a["dn_lnw"] = np.tile(a["L0_attn_ln_w"], (P, 1))
    a["dn_lnb"] = np.tile(a["L0_attn_ln_b"], (P, 1))
    for n in ("r", "k", "v"):
        a[f"cm_w{n}"] = np.ascontiguousarray(a[f"L2_ffn_W_{n}"].T)
    a["cm_mu"] = np.ascontiguousarray(np.stack([a["L2_ffn_mu_r"], a["L2_ffn_mu_k"]], 1))
    a["de_gb"] = np.tile(a["L1_ffn_gate_b"], GROUP)[None]
    a["de_ew"] = np.ascontiguousarray(a["L1_ffn_expert_w"].transpose(1, 0, 2).reshape(D, -1))
    b = lambda n: a[n][:, None]
    a["tt_w0"] = np.concatenate([a["L1_attn_W1"], b("L1_attn_b1"), b("L1_attn_b2"), a["L1_attn_W2"], a["L1_attn_W2"].T], 1)
    step = np.arange(P) % (P // B)
    a["tt_earlier"] = (step[:, None] < step[None, :]).astype(f)
    a["tt_ones"] = np.ones((P, 1), f)
    a["sa_wq"], a["sa_wk"] = a["L2_attn_Wq"], a["L2_attn_Wk"]
    a["sa_bias"] = np.ascontiguousarray(np.stack([a["L2_attn_bq"], a["L2_attn_bk"]], 1))
    a["sa_gamma_beta"] = np.ascontiguousarray(np.stack([a["L2_attn_gamma"], a["L2_attn_beta"]], 1))
    for n in "qkv":
        a[f"ba_w{n}"] = np.ascontiguousarray(a[f"L3_attn_{n}_w"].T)
    a["ba_ow"] = np.ascontiguousarray(a["L3_attn_out_w"].T)
    a["ba_ob"] = np.tile(a["L3_attn_out_b"], GROUP)[None]
    E, G, K = 8, 4, 2
    for n in (1, 2, 3):
        a[f"rf_sw{n}"] = np.ascontiguousarray(a[f"L3_ffn_sw{n}"].T)
    a["rf_gw"] = np.ascontiguousarray(a["L3_ffn_w_gate"].T)
    a["rf_eb"] = np.tile(a["L3_ffn_expert_bias"], (P, 1))
    a["rf_w13"] = np.ascontiguousarray(np.concatenate([a["L3_ffn_w1"], a["L3_ffn_w3"]], 2).transpose(1, 0, 2))
    a["rf_w2"] = np.ascontiguousarray(a["L3_ffn_w2"].transpose(1, 0, 2))
    before = lambda n: np.tile((np.arange(n)[None, :] < np.arange(n)[:, None]).astype(f).reshape(-1), (P, 1))
    pos = K * (np.arange(NT)[None, :, None] * P + np.arange(P)[:, None, None]) + np.arange(K)[None, None, :]
    delta = np.zeros((E, K, E), f)
    delta[np.arange(E), :, np.arange(E)] = 1
    half = np.stack([np.arange(P) < P // 2, np.arange(P) >= P // 2], 1)
    a["rf_consts"] = np.concatenate([before(G), before(E), pos.reshape(P, -1).astype(f), np.tile(delta.reshape(-1), (P, 1)),
                                     half.astype(f), np.ones((P, P), f)], 1)
    return a


def kernel(**inputs):
    import concourse.bacc as bacc
    from concourse.bass_utils import run_bass_kernel_spmd as run

    nc = bacc.Bacc("TRN2", target_bir_lowering=False, num_devices=1)
    arrays = lay_out(inputs)
    dram = {n: nc.dram_tensor(f"in_{n}", v.shape, mybir.dt.from_np(v.dtype), kind="ExternalInput").ap()
            for n, v in arrays.items()}
    out = nc.dram_tensor("out_x", (B, S, D), F32, kind="ExternalOutput").ap()
    build(nc, dram, out)
    r = run(nc, [{f"in_{n}": v for n, v in arrays.items()}], core_ids=[0])
    return r.results[0]["out_x"]
```
